# Optimizing a Trainium2 kernel written in Bass

```python
import numpy as np
import jax
import jax.numpy as jnp

def _softmax(x, axis=-1):
    return jax.nn.softmax(x, axis=axis)

def _gelu(x):
    return jax.nn.gelu(x, approximate=True)

def _silu(x):
    return jax.nn.silu(x)

def _sigmoid(x):
    return jax.nn.sigmoid(x)

def _layernorm(x, axis=-1, eps=1e-05):
    m = jnp.mean(x, axis=axis, keepdims=True)
    v = jnp.var(x, axis=axis, keepdims=True)
    return (x - m) / jnp.sqrt(v + eps)

def _scatter_add(tgt, idx, src, axis=0):
    return tgt.at[idx].add(src)

def _segment_sum(src, seg, n):
    return jax.ops.segment_sum(src, seg, n)
kernel_name = 'mk_xattn_ffn_d4_seqx_r4_bf904c'

def setup_inputs(seed: int=0):
    np.random.seed(seed)
    _w = jnp.asarray

    def _rec_inputs():
        import jax
        import jax.numpy as jnp
        _rk = jax.random.key(seed)
        x = -0.0002928 + 1 * jax.random.normal(jax.random.fold_in(_rk, 1), (16, 128, 256), jnp.float32)
        _lenS = 128 - jax.random.randint(jax.random.fold_in(_rk, 7), (16,), 0, max(1, 128 // 4) + 1, jnp.int32)
        _lenS2 = 128 - jax.random.randint(jax.random.fold_in(_rk, 8), (16,), 0, max(1, 128 // 4) + 1, jnp.int32)
        _ctx_512P = jax.random.normal(jax.random.fold_in(_rk, 11), (16, 16, 128), jnp.float32)
        _ctx_512c = jax.random.dirichlet(jax.random.fold_in(_rk, 511), 0.3 * jnp.ones((16,), jnp.float32), (16, 128))
        _ctx_512t = jnp.einsum('bsk,bkd->bsd', _ctx_512c, _ctx_512P)
        _ctx_512t = _ctx_512t * jax.lax.rsqrt(jnp.mean(jnp.square(_ctx_512t)) + 1e-12) * 0.953939
        ctx_512 = -1.52775e-05 + 0.999936 * (_ctx_512t + 0.3 * jax.random.normal(jax.random.fold_in(_rk, 611), (16, 128, 128), jnp.float32))
        itok_BxS2xS_0_7 = jax.random.randint(jax.random.fold_in(_rk, 12), (16, 128, 128), 0, 8, jnp.int32)
        return (x, ctx_512, itok_BxS2xS_0_7)
    x, ctx_512, itok_BxS2xS_0_7 = _rec_inputs()

    def _L0_xattn_setup():
        import jax, jax.numpy as jnp
        import numpy as np
        NUM_HEADS = 16
        HEAD_DIM = 64
        Q_DIM = 256
        KV_DIM = 128
        INNER = NUM_HEADS * HEAD_DIM
        key = jax.random.key(seed)
        ks = jax.random.split(key, 7)
        B, N, M = (32, 128, 512)
        q = jax.random.normal(ks[0], (B, N, Q_DIM), dtype=jnp.float32)
        kv = jax.random.normal(ks[1], (B, M, KV_DIM), dtype=jnp.float32)
        Wq = jax.random.normal(ks[2], (Q_DIM, INNER), dtype=jnp.float32) / np.sqrt(Q_DIM)
        Wk = jax.random.normal(ks[3], (KV_DIM, INNER), dtype=jnp.float32) / np.sqrt(KV_DIM)
        Wv = jax.random.normal(ks[4], (KV_DIM, INNER), dtype=jnp.float32) / np.sqrt(KV_DIM)
        Wo = jax.random.normal(ks[5], (INNER, Q_DIM), dtype=jnp.float32) / np.sqrt(INNER)
        bo = jax.random.normal(ks[6], (Q_DIM,), dtype=jnp.float32) * 0.01
        return {'q': q, 'kv': kv, 'Wq': Wq, 'Wk': Wk, 'Wv': Wv, 'Wo': Wo, 'bo': bo}
    _L0_xattn_all = _L0_xattn_setup()
    _L0_xattn_in = {k: v for k, v in _L0_xattn_all.items() if k in ('Wq', 'Wk', 'Wv', 'Wo', 'bo')}
    del _L0_xattn_all

    def _L0_ffn_setup():
        import jax, jax.numpy as jnp
        import numpy as np
        B, S, D = (2, 256, 256)
        E, K, F, FS = (8, 2, 128, 256)
        key = jax.random.key(seed)
        ks = jax.random.split(key, 9)
        s = lambda k, shape, fan: jax.random.normal(k, shape, jnp.float32) * fan ** (-0.5)
        return {'x': jax.random.normal(ks[0], (B, S, D), jnp.float32), 'Wr': s(ks[1], (D, E), D), 'Wg': s(ks[2], (E, D, F), D), 'Wu': s(ks[3], (E, D, F), D), 'Wd': s(ks[4], (E, F, D), F), 'Sg': s(ks[5], (D, FS), D), 'Su': s(ks[6], (D, FS), D), 'Sd': s(ks[7], (FS, D), FS), 'expert_bias': jnp.zeros((E,), jnp.float32)}
    _L0_ffn_all = _L0_ffn_setup()
    _L0_ffn_in = {k: v for k, v in _L0_ffn_all.items() if k in ('Wr', 'Wg', 'Wu', 'Wd', 'Sg', 'Su', 'Sd', 'expert_bias')}
    del _L0_ffn_all

    def _L1_xattn_setup():
        import jax, jax.numpy as jnp
        import numpy as np
        B, LQ, LK = (8, 512, 512)
        QD, KD, VD = (256, 128, 128)
        key = jax.random.key(seed)
        ks = jax.random.split(key, 9)
        s = 0.02
        return {'query': jax.random.normal(ks[0], (B, LQ, QD), jnp.float32), 'key': jax.random.normal(ks[1], (B, LK, KD), jnp.float32), 'value': jax.random.normal(ks[2], (B, LK, VD), jnp.float32), 'Wq': jax.random.normal(ks[3], (QD, QD), jnp.float32) * s, 'bq': jnp.zeros((QD,), jnp.float32), 'Wk': jax.random.normal(ks[4], (KD, QD), jnp.float32) * s, 'bk': jnp.zeros((QD,), jnp.float32), 'Wv': jax.random.normal(ks[5], (VD, QD), jnp.float32) * s, 'bv': jnp.zeros((QD,), jnp.float32)}
    _L1_xattn_all = _L1_xattn_setup()
    _L1_xattn_in = {k: v for k, v in _L1_xattn_all.items() if k in ('Wq', 'bq', 'Wk', 'bk', 'Wv', 'bv')}
    del _L1_xattn_all

    def _L1_ffn_setup():
        import jax, jax.numpy as jnp
        import numpy as np
        E = 32
        H = 256
        I = 128
        G = 8
        TKG = 4
        TOPK = 8
        NSH = 2
        SCALE = 2.5
        key = jax.random.key(seed)
        ks = jax.random.split(key, 10)
        s = 0.02
        return {'hidden_states': jax.random.normal(ks[0], (2, 256, H), jnp.float32), 'gate_w': jax.random.normal(ks[1], (E, H), jnp.float32) * s, 'gate_bias': jax.random.normal(ks[2], (E,), jnp.float32) * s, 'w_gate': jax.random.normal(ks[3], (E, I, H), jnp.float32) * s, 'w_up': jax.random.normal(ks[4], (E, I, H), jnp.float32) * s, 'w_down': jax.random.normal(ks[5], (E, H, I), jnp.float32) * s, 'sh_gate': jax.random.normal(ks[6], (I * NSH, H), jnp.float32) * s, 'sh_up': jax.random.normal(ks[7], (I * NSH, H), jnp.float32) * s, 'sh_down': jax.random.normal(ks[8], (H, I * NSH), jnp.float32) * s}
    _L1_ffn_all = _L1_ffn_setup()
    _L1_ffn_in = {k: v for k, v in _L1_ffn_all.items() if k in ('gate_w', 'gate_bias', 'w_gate', 'w_up', 'w_down', 'sh_gate', 'sh_up', 'sh_down')}
    del _L1_ffn_all

    def _L2_xattn_setup():
        import jax, jax.numpy as jnp
        import numpy as np
        key = jax.random.key(seed)
        k1, k2, k3, k4, k5 = jax.random.split(key, 5)
        B, K, S, E, I, D = (4, 2, 128, 8, 256, 512)
        x = jax.random.normal(k1, (B, S, I), dtype=jnp.float32)
        weights = jax.random.uniform(k2, (B, K, S), dtype=jnp.float32)
        ensembles = jax.random.randint(k3, (B, K, S), 0, E, dtype=jnp.int64)
        lim1 = float(np.sqrt(6.0 / (D + I)))
        proj_in = jax.random.uniform(k4, (E, D, I), dtype=jnp.float32, minval=-lim1, maxval=lim1)
        proj_out = jax.random.uniform(k5, (E, I, D), dtype=jnp.float32, minval=-lim1, maxval=lim1)
        return {'x': x, 'weights': weights, 'ensembles': ensembles, 'proj_in': proj_in, 'proj_out': proj_out}
    _L2_xattn_all = _L2_xattn_setup()
    _L2_xattn_in = {k: v for k, v in _L2_xattn_all.items() if k in ('proj_in', 'proj_out')}
    del _L2_xattn_all

    def _L2_ffn_setup():
        import jax, jax.numpy as jnp
        import numpy as np
        HIDDEN = 256
        INTER = 1024
        N_EXPERTS = 8

        def geglu(x, w1, w2, w3):
            return jax.nn.gelu(x @ w1, approximate=False) * (x @ w2) @ w3
        key = jax.random.key(seed)
        ks = jax.random.split(key, 8)
        s = 0.02
        x = jax.random.normal(ks[0], (2, 512, HIDDEN), dtype=jnp.float32)
        w1s = jax.random.normal(ks[1], (HIDDEN, INTER), dtype=jnp.float32) * s
        w2s = jax.random.normal(ks[2], (HIDDEN, INTER), dtype=jnp.float32) * s
        w3s = jax.random.normal(ks[3], (INTER, HIDDEN), dtype=jnp.float32) * s
        W1 = jax.random.normal(ks[4], (N_EXPERTS, HIDDEN, INTER), dtype=jnp.float32) * s
        W2 = jax.random.normal(ks[5], (N_EXPERTS, HIDDEN, INTER), dtype=jnp.float32) * s
        W3 = jax.random.normal(ks[6], (N_EXPERTS, INTER, HIDDEN), dtype=jnp.float32) * s
        Wg = jax.random.normal(ks[7], (HIDDEN, N_EXPERTS), dtype=jnp.float32) * s
        return {'x': x, 'w1s': w1s, 'w2s': w2s, 'w3s': w3s, 'W1': W1, 'W2': W2, 'W3': W3, 'Wg': Wg}
    _L2_ffn_all = _L2_ffn_setup()
    _L2_ffn_in = {k: v for k, v in _L2_ffn_all.items() if k in ('w1s', 'w2s', 'w3s', 'W1', 'W2', 'W3', 'Wg')}
    del _L2_ffn_all

    def _L3_xattn_setup():
        import jax, jax.numpy as jnp
        import numpy as np
        HEADS = 16
        D_MODEL = 256
        IMG_MODEL = 128
        D_K = D_MODEL // HEADS
        key = jax.random.key(seed)
        ks = jax.random.split(key, 12)
        B, LQ, LKV = (8, 512, 256)
        s_dm = 1.0 / np.sqrt(D_MODEL)
        s_im = 1.0 / np.sqrt(IMG_MODEL)
        return {'q': jax.random.normal(ks[0], (B, LQ, D_MODEL), jnp.float32), 'k': jax.random.normal(ks[1], (B, LKV, IMG_MODEL), jnp.float32), 'v': jax.random.normal(ks[2], (B, LKV, IMG_MODEL), jnp.float32), 'Wq': jax.random.normal(ks[3], (D_MODEL, D_MODEL), jnp.float32) * s_dm, 'bq': jnp.zeros((D_MODEL,), jnp.float32), 'Wk': jax.random.normal(ks[4], (IMG_MODEL, D_MODEL), jnp.float32) * s_im, 'bk': jnp.zeros((D_MODEL,), jnp.float32), 'Wv': jax.random.normal(ks[5], (IMG_MODEL, D_MODEL), jnp.float32) * s_im, 'bv': jnp.zeros((D_MODEL,), jnp.float32), 'Wo': jax.random.normal(ks[6], (D_MODEL, D_MODEL), jnp.float32) * s_dm, 'bo': jnp.zeros((D_MODEL,), jnp.float32)}
    _L3_xattn_all = _L3_xattn_setup()
    _L3_xattn_in = {k: v for k, v in _L3_xattn_all.items() if k in ('Wq', 'bq', 'Wk', 'bk', 'Wv', 'bv', 'Wo', 'bo')}
    del _L3_xattn_all

    def _L3_ffn_setup():
        import math
        import jax, jax.numpy as jnp
        import numpy as np
        CAPACITY_FACTOR = 1.25
        key = jax.random.key(seed)
        ks = jax.random.split(key, 5)
        B, S, H, F, E = (4, 1024, 256, 256, 32)
        scale_in = 1.0 / math.sqrt(H)
        scale_mid = 1.0 / math.sqrt(F)
        return {'x': jax.random.normal(ks[0], (B, S, H), dtype=jnp.float32), 'w_router': jax.random.normal(ks[1], (H, E), dtype=jnp.float32) * scale_in, 'w_gate': jax.random.normal(ks[2], (E, H, F), dtype=jnp.float32) * scale_in, 'w_up': jax.random.normal(ks[3], (E, H, F), dtype=jnp.float32) * scale_in, 'w_down': jax.random.normal(ks[4], (E, F, H), dtype=jnp.float32) * scale_mid}
    _L3_ffn_all = _L3_ffn_setup()
    _L3_ffn_in = {k: v for k, v in _L3_ffn_all.items() if k in ('w_router', 'w_gate', 'w_up', 'w_down')}
    del _L3_ffn_all
    return {'x': x, 'ctx_512': ctx_512, 'itok_BxS2xS_0_7': itok_BxS2xS_0_7, 'L0_xattn_Wq': _L0_xattn_in['Wq'], 'L0_xattn_Wk': _L0_xattn_in['Wk'], 'L0_xattn_Wv': _L0_xattn_in['Wv'], 'L0_xattn_Wo': _L0_xattn_in['Wo'], 'L0_xattn_bo': _L0_xattn_in['bo'], 'L0_ffn_Wr': _L0_ffn_in['Wr'], 'L0_ffn_Wg': _L0_ffn_in['Wg'], 'L0_ffn_Wu': _L0_ffn_in['Wu'], 'L0_ffn_Wd': _L0_ffn_in['Wd'], 'L0_ffn_Sg': _L0_ffn_in['Sg'], 'L0_ffn_Su': _L0_ffn_in['Su'], 'L0_ffn_Sd': _L0_ffn_in['Sd'], 'L0_ffn_expert_bias': _L0_ffn_in['expert_bias'], 'L1_xattn_Wq': _L1_xattn_in['Wq'], 'L1_xattn_bq': _L1_xattn_in['bq'], 'L1_xattn_Wk': _L1_xattn_in['Wk'], 'L1_xattn_bk': _L1_xattn_in['bk'], 'L1_xattn_Wv': _L1_xattn_in['Wv'], 'L1_xattn_bv': _L1_xattn_in['bv'], 'L1_ffn_gate_w': _L1_ffn_in['gate_w'], 'L1_ffn_gate_bias': _L1_ffn_in['gate_bias'], 'L1_ffn_w_gate': _L1_ffn_in['w_gate'], 'L1_ffn_w_up': _L1_ffn_in['w_up'], 'L1_ffn_w_down': _L1_ffn_in['w_down'], 'L1_ffn_sh_gate': _L1_ffn_in['sh_gate'], 'L1_ffn_sh_up': _L1_ffn_in['sh_up'], 'L1_ffn_sh_down': _L1_ffn_in['sh_down'], 'L2_xattn_proj_in': _L2_xattn_in['proj_in'], 'L2_xattn_proj_out': _L2_xattn_in['proj_out'], 'L2_ffn_w1s': _L2_ffn_in['w1s'], 'L2_ffn_w2s': _L2_ffn_in['w2s'], 'L2_ffn_w3s': _L2_ffn_in['w3s'], 'L2_ffn_W1': _L2_ffn_in['W1'], 'L2_ffn_W2': _L2_ffn_in['W2'], 'L2_ffn_W3': _L2_ffn_in['W3'], 'L2_ffn_Wg': _L2_ffn_in['Wg'], 'L3_xattn_Wq': _L3_xattn_in['Wq'], 'L3_xattn_bq': _L3_xattn_in['bq'], 'L3_xattn_Wk': _L3_xattn_in['Wk'], 'L3_xattn_bk': _L3_xattn_in['bk'], 'L3_xattn_Wv': _L3_xattn_in['Wv'], 'L3_xattn_bv': _L3_xattn_in['bv'], 'L3_xattn_Wo': _L3_xattn_in['Wo'], 'L3_xattn_bo': _L3_xattn_in['bo'], 'L3_ffn_w_router': _L3_ffn_in['w_router'], 'L3_ffn_w_gate': _L3_ffn_in['w_gate'], 'L3_ffn_w_up': _L3_ffn_in['w_up'], 'L3_ffn_w_down': _L3_ffn_in['w_down']}

def reference(x, ctx_512, itok_BxS2xS_0_7, L0_xattn_Wq, L0_xattn_Wk, L0_xattn_Wv, L0_xattn_Wo, L0_xattn_bo, L0_ffn_Wr, L0_ffn_Wg, L0_ffn_Wu, L0_ffn_Wd, L0_ffn_Sg, L0_ffn_Su, L0_ffn_Sd, L0_ffn_expert_bias, L1_xattn_Wq, L1_xattn_bq, L1_xattn_Wk, L1_xattn_bk, L1_xattn_Wv, L1_xattn_bv, L1_ffn_gate_w, L1_ffn_gate_bias, L1_ffn_w_gate, L1_ffn_w_up, L1_ffn_w_down, L1_ffn_sh_gate, L1_ffn_sh_up, L1_ffn_sh_down, L2_xattn_proj_in, L2_xattn_proj_out, L2_ffn_w1s, L2_ffn_w2s, L2_ffn_w3s, L2_ffn_W1, L2_ffn_W2, L2_ffn_W3, L2_ffn_Wg, L3_xattn_Wq, L3_xattn_bq, L3_xattn_Wk, L3_xattn_bk, L3_xattn_Wv, L3_xattn_bv, L3_xattn_Wo, L3_xattn_bo, L3_ffn_w_router, L3_ffn_w_gate, L3_ffn_w_up, L3_ffn_w_down):
    import jax
    import jax.numpy as jnp

    def _L0_xattn_ref(q, kv, Wq, Wk, Wv, Wo, bo):
        import jax, jax.numpy as jnp
        import numpy as np
        NUM_HEADS = 16
        HEAD_DIM = 64
        Q_DIM = 256
        KV_DIM = 128
        INNER = NUM_HEADS * HEAD_DIM
        B, N, _ = q.shape
        M = kv.shape[1]
        scale = HEAD_DIM ** (-0.5)
        qh = (q @ Wq).reshape(B, N, NUM_HEADS, HEAD_DIM).transpose(0, 2, 1, 3)
        kh = (kv @ Wk).reshape(B, M, NUM_HEADS, HEAD_DIM).transpose(0, 2, 1, 3)
        vh = (kv @ Wv).reshape(B, M, NUM_HEADS, HEAD_DIM).transpose(0, 2, 1, 3)
        scores = jnp.einsum('bhnd,bhmd->bhnm', qh, kh) * scale
        attn = jax.nn.softmax(scores, axis=-1)
        out = jnp.einsum('bhnm,bhmd->bhnd', attn, vh)
        out = out.transpose(0, 2, 1, 3).reshape(B, N, INNER)
        return out @ Wo + bo

    def _L0_ffn_ref(x, Wr, Wg, Wu, Wd, Sg, Su, Sd, expert_bias):
        import jax, jax.numpy as jnp
        import numpy as np
        B, S, D = (2, 256, 256)
        E, K, F, FS = (8, 2, 128, 256)
        b, s, d = x.shape
        xf = x.reshape(-1, d)
        T = xf.shape[0]
        logits = xf @ Wr + expert_bias
        top_v, top_i = jax.lax.top_k(logits, K)
        probs = jax.nn.softmax(top_v, axis=-1)
        rw = jnp.zeros_like(logits).at[jnp.arange(T)[:, None], top_i].set(probs)
        gate = jnp.einsum('td,edf->tef', xf, Wg)
        up = jnp.einsum('td,edf->tef', xf, Wu)
        h = jax.nn.silu(gate) * up
        eo = jnp.einsum('tef,efd->ted', h, Wd)
        out = jnp.einsum('te,ted->td', rw, eo)
        out = out + jax.nn.silu(xf @ Sg) * (xf @ Su) @ Sd
        return out.reshape(b, s, d)

    def _L1_xattn_ref(query, key, value, Wq, bq, Wk, bk, Wv, bv):
        import jax, jax.numpy as jnp
        import numpy as np
        B, LQ, LK = (8, 512, 512)
        QD, KD, VD = (256, 128, 128)
        q = jnp.einsum('bld,de->ble', query, Wq) + bq
        k = jnp.einsum('bld,de->ble', key, Wk) + bk
        v = jnp.einsum('bld,de->ble', value, Wv) + bv
        scores = jnp.einsum('bqe,bke->bqk', q, k)
        attn = jax.nn.softmax(scores, axis=-1)
        out = jnp.einsum('bqk,bke->bqe', attn, v)
        return out

    def _L1_ffn_ref(hidden_states, gate_w, gate_bias, w_gate, w_up, w_down, sh_gate, sh_up, sh_down):
        import jax, jax.numpy as jnp
        import numpy as np
        E = 32
        H = 256
        I = 128
        G = 8
        TKG = 4
        TOPK = 8
        NSH = 2
        SCALE = 2.5
        B, S, Hd = hidden_states.shape
        h = hidden_states.reshape(-1, Hd)
        logits = h.astype(jnp.float32) @ gate_w.T
        scores = jax.nn.sigmoid(logits)
        sc = scores + gate_bias
        grp = sc.reshape(-1, G, E // G)
        group_scores = jax.lax.top_k(grp, 2)[0].sum(-1)
        gidx = jax.lax.top_k(group_scores, TKG)[1]
        gmask = jnp.sum(jax.nn.one_hot(gidx, G, dtype=sc.dtype), axis=1)
        smask = jnp.repeat(gmask, E // G, axis=1)
        masked = jnp.where(smask > 0, sc, jnp.zeros_like(sc))
        tki = jax.lax.top_k(masked, TOPK)[1]
        tkw = jnp.take_along_axis(scores, tki, axis=1)
        tkw = tkw / (tkw.sum(-1, keepdims=True) + 1e-20)
        tkw = tkw * SCALE
        combine = (jax.nn.one_hot(tki, E, dtype=tkw.dtype) * tkw[..., None]).sum(1)
        g = jax.nn.silu(jnp.einsum('th,eih->tei', h, w_gate))
        u = jnp.einsum('th,eih->tei', h, w_up)
        routed = jnp.einsum('tei,ehi->th', g * u * combine[:, :, None], w_down)
        sg = jax.nn.silu(h @ sh_gate.T)
        shared = sg * (h @ sh_up.T) @ sh_down.T
        return (routed + shared).reshape(B, S, Hd)

    def _L2_xattn_ref(x, weights, ensembles, proj_in, proj_out):
        import jax, jax.numpy as jnp
        import numpy as np
        E = proj_in.shape[0]
        h = jax.nn.relu(jnp.einsum('edi,bsi->bsed', proj_in, x))
        o = jnp.einsum('eid,bsed->bsei', proj_out, h)
        onehot = jax.nn.one_hot(ensembles, E, dtype=x.dtype)
        gate = jnp.einsum('bks,bkse->bse', weights, onehot)
        return jnp.einsum('bsei,bse->bsi', o, gate)

    def _L2_ffn_ref(x, w1s, w2s, w3s, W1, W2, W3, Wg):
        import jax, jax.numpy as jnp
        import numpy as np
        HIDDEN = 256
        INTER = 1024
        N_EXPERTS = 8

        def geglu(x, w1, w2, w3):
            return jax.nn.gelu(x @ w1, approximate=False) * (x @ w2) @ w3
        B, T, C = x.shape
        xf = x.reshape(-1, C)
        shared = geglu(xf, w1s, w2s, w3s)
        logits = xf @ Wg
        idx = jnp.argmax(logits, axis=-1)
        final = jnp.zeros_like(xf)
        for e in range(N_EXPERTS):
            y = geglu(xf, W1[e], W2[e], W3[e])
            final = final + jnp.where((idx == e)[:, None], y, 0.0)
        return (shared + final).reshape(B, T, C)

    def _L3_xattn_ref(q, k, v, Wq, bq, Wk, bk, Wv, bv, Wo, bo):
        import jax, jax.numpy as jnp
        import numpy as np
        HEADS = 16
        D_MODEL = 256
        IMG_MODEL = 128
        D_K = D_MODEL // HEADS
        B, LQ, _ = q.shape
        LKV = k.shape[1]
        qh = (q @ Wq + bq).reshape(B, LQ, HEADS, D_K).transpose(0, 2, 1, 3)
        kh = (k @ Wk + bk).reshape(B, LKV, HEADS, D_K).transpose(0, 2, 1, 3)
        vh = (v @ Wv + bv).reshape(B, LKV, HEADS, D_K).transpose(0, 2, 1, 3)
        scale = 1.0 / np.sqrt(D_K)
        scores = jnp.einsum('bhqd,bhkd->bhqk', qh, kh) * scale
        attn = jax.nn.softmax(scores, axis=-1)
        out = jnp.einsum('bhqk,bhkd->bhqd', attn, vh)
        concat = out.transpose(0, 2, 1, 3).reshape(B, LQ, D_MODEL)
        return concat @ Wo + bo

    def _L3_ffn_ref(x, w_router, w_gate, w_up, w_down):
        import math
        import jax, jax.numpy as jnp
        import numpy as np
        CAPACITY_FACTOR = 1.25
        B, S, H = x.shape
        E = w_gate.shape[0]
        T = B * S
        C = int(math.ceil(CAPACITY_FACTOR * T / E))
        xt = x.reshape(T, H)
        logits = xt @ w_router
        probs = jax.nn.softmax(logits, axis=-1)
        top1 = jnp.argmax(probs, axis=-1)
        gate = jnp.take_along_axis(probs, top1[:, None], axis=1)[:, 0]
        onehot = jax.nn.one_hot(top1, E, dtype=jnp.int32)
        pos = jnp.cumsum(onehot, axis=0)[jnp.arange(T), top1] - 1
        accepted = pos < C
        slot = jnp.where(accepted, top1 * C + pos, E * C)
        buf = jnp.zeros((E * C + 1, H), dtype=x.dtype).at[slot].set(xt)
        buf = buf[:E * C].reshape(E, C, H)
        g = jnp.einsum('ech,ehf->ecf', buf, w_gate)
        u = jnp.einsum('ech,ehf->ecf', buf, w_up)
        y = jnp.einsum('ecf,efh->ech', jax.nn.silu(g) * u, w_down)
        out_tok = y.reshape(E * C, H)[jnp.clip(slot, 0, E * C - 1)]
        out_tok = jnp.where(accepted[:, None], out_tok * gate[:, None], 0.0)
        return (xt + out_tok).reshape(B, S, H)
    x = x + _L0_xattn_ref(_layernorm(x, axis=-1), ctx_512, L0_xattn_Wq, L0_xattn_Wk, L0_xattn_Wv, L0_xattn_Wo, L0_xattn_bo)
    x = x + _L0_ffn_ref(_layernorm(x, axis=-1), L0_ffn_Wr, L0_ffn_Wg, L0_ffn_Wu, L0_ffn_Wd, L0_ffn_Sg, L0_ffn_Su, L0_ffn_Sd, L0_ffn_expert_bias)
    x = x + _L1_xattn_ref(_layernorm(x, axis=-1), ctx_512, ctx_512, L1_xattn_Wq, L1_xattn_bq, L1_xattn_Wk, L1_xattn_bk, L1_xattn_Wv, L1_xattn_bv)
    x = x + _L1_ffn_ref(_layernorm(x, axis=-1), L1_ffn_gate_w, L1_ffn_gate_bias, L1_ffn_w_gate, L1_ffn_w_up, L1_ffn_w_down, L1_ffn_sh_gate, L1_ffn_sh_up, L1_ffn_sh_down)
    x = x + _L2_xattn_ref(_layernorm(x, axis=-1), ctx_512, itok_BxS2xS_0_7, L2_xattn_proj_in, L2_xattn_proj_out)
    x = x + _L2_ffn_ref(_layernorm(x, axis=-1), L2_ffn_w1s, L2_ffn_w2s, L2_ffn_w3s, L2_ffn_W1, L2_ffn_W2, L2_ffn_W3, L2_ffn_Wg)
    x = x + _L3_xattn_ref(_layernorm(x, axis=-1), ctx_512, ctx_512, L3_xattn_Wq, L3_xattn_bq, L3_xattn_Wk, L3_xattn_bk, L3_xattn_Wv, L3_xattn_bv, L3_xattn_Wo, L3_xattn_bo)
    x = x + _L3_ffn_ref(_layernorm(x, axis=-1), L3_ffn_w_router, L3_ffn_w_gate, L3_ffn_w_up, L3_ffn_w_down)
    return x

_drawn_inputs = setup_inputs


def setup_inputs(seed=0):
    import zlib

    import numpy as np

    out = dict(_drawn_inputs(seed))
    spreads = {'L0_ffn_expert_bias': (0.0, 0.1),
     'L1_xattn_bq': (0.0, 0.59),
     'L1_xattn_bk': (0.0, 0.8),
     'L1_xattn_bv': (0.0, 0.1),
     'L3_xattn_bq': (0.0, 0.8),
     'L3_xattn_bk': (0.0, 0.8),
     'L3_xattn_bv': (0.0, 0.8),
     'L3_xattn_bo': (0.0, 0.8)}
    factors = {'L1_ffn_gate_w': 8.0,
     'L1_ffn_gate_bias': 8.0,
     'L1_ffn_w_gate': 7.31,
     'L1_ffn_w_up': 7.217,
     'L1_ffn_w_down': 7.223,
     'L1_ffn_sh_gate': 4.231,
     'L1_ffn_sh_up': 4.404,
     'L1_ffn_sh_down': 4.216,
     'L2_ffn_w1s': 8.0,
     'L2_ffn_w2s': 8.0,
     'L2_ffn_w3s': 8.0,
     'L2_ffn_W1': 8.0,
     'L2_ffn_W2': 8.0,
     'L2_ffn_W3': 8.0,
     'L2_ffn_Wg': 8.0,
     'L3_xattn_Wq': 4.273,
     'L3_xattn_Wk': 4.192,
     'L3_ffn_w_router': 8.0,
     'L3_ffn_w_gate': 8.0,
     'L3_ffn_w_up': 8.0,
     'L3_ffn_w_down': 8.0}
    for name, (base, spread) in spreads.items():
        noise = np.random.default_rng([zlib.crc32(name.encode()), seed]).standard_normal(out[name].shape)
        drawn = base * np.exp(spread * noise) if base else spread * noise
        out[name] = jnp.asarray(drawn.astype(out[name].dtype))
    for name, factor in factors.items():
        out[name] = (out[name] * factor).astype(out[name].dtype)
    return out
```

```python
from contextlib import ExitStack

import numpy as np
import concourse.bass as bass
from concourse import mybir

F32 = mybir.dt.float32
I32 = mybir.dt.int32
ACT = mybir.ActivationFunctionType
ALU = mybir.AluOpType
AX = mybir.AxisListType

P = 128
B = 16
D = 256
KC = D // P
T = B * P
GT = 4
GW = GT * P
NG = B // GT
EPS = 1e-5
BIG = 3.0e38
CAPACITY = -(-5 * T // (4 * 32))


LIVE = []


def signal(nc, name):
    LIVE.append(nc.alloc_semaphore(name))
    return LIVE[-1]


def recycle_signals(nc):
    nc.clear_and_free_semaphores(LIVE)
    LIVE.clear()
    nc.all_engine_barrier()


def layer_norm(nc, tag, x, xn, xnT, ident):
    with ExitStack() as ctx:
        stats = ctx.enter_context(nc.sbuf_tensor(f"{tag}_stats", [P, B, 6], F32))
        mean_var = ctx.enter_context(nc.sbuf_tensor(f"{tag}_mean_var", [P, B, 2], F32))
        spread = ctx.enter_context(nc.sbuf_tensor(f"{tag}_spread", [P, B, 3], F32))
        turned = ctx.enter_context(nc.psum_tensor(f"{tag}_turned", [P, 2, GW], F32))
        stats_done = signal(nc, f"{tag}_stats_done")
        var_ready = signal(nc, f"{tag}_var_ready")
        std_ready = signal(nc, f"{tag}_std_ready")
        rstd_ready = signal(nc, f"{tag}_rstd_ready")
        xn_ready = signal(nc, f"{tag}_xn_ready")
        turned_ready = signal(nc, f"{tag}_turned_ready")
        xnT_written = signal(nc, f"{tag}_xnT_written")
        with nc.Block() as block:
            @block.vector
            def _(dve):
                for t in range(B):
                    nc.vector.bn_stats(stats[:, t, :], x[:, t, :]).then_inc(stats_done, 1)
                dve.wait_ge(stats_done, B)
                for t in range(B):
                    nc.vector.bn_aggr(mean_var[:, t, :], stats[:, t, :]).then_inc(var_ready, 1)
                dve.wait_ge(var_ready, B)
                nc.vector.tensor_scalar(spread[:, :, 0], mean_var[:, :, 1], EPS, None, ALU.add).then_inc(var_ready, 1)
                dve.wait_ge(std_ready, 1)
                nc.vector.reciprocal(spread[:, :, 2], spread[:, :, 1]).then_inc(rstd_ready, 1)
                dve.wait_ge(rstd_ready, 1)
                for t in range(B):
                    nc.vector.tensor_scalar(xn[:, t, :], x[:, t, :], mean_var[:, t, 0:1], spread[:, t, 2:3],
                                            ALU.subtract, ALU.mult).then_inc(xn_ready, 1)

            @block.tensor
            def _(pe):
                for g in range(NG):
                    for k in range(KC):
                        n = g * KC + k
                        if n >= 2:
                            pe.wait_ge(xnT_written, n - 1)
                        for j in range(GT):
                            t = g * GT + j
                            pe.wait_ge(xn_ready, t + 1)
                            last = nc.tensor.transpose(turned[:, n % 2, j * P:(j + 1) * P],
                                                       xn[:, t, k * P:(k + 1) * P], ident[:, :])
                        last.then_inc(turned_ready, 1)

            @block.scalar
            def _(act):
                act.wait_ge(var_ready, B + 1)
                nc.scalar.activation(spread[:, :, 1], spread[:, :, 0], ACT.Sqrt).then_inc(std_ready, 1)
                for g in range(NG):
                    for k in range(KC):
                        n = g * KC + k
                        act.wait_ge(turned_ready, n + 1)
                        nc.scalar.activation(xnT[:, k, g * GW:(g + 1) * GW], turned[:, n % 2, :],
                                             ACT.Copy).then_inc(xnT_written, 1)


def routing(nc, tag, xnT, rw, wr_dram, n_experts, finish, bias_dram=None):
    with ExitStack() as ctx:
        E = n_experts
        wr = ctx.enter_context(nc.sbuf_tensor(f"{tag}_wr", [P, KC, E], F32))
        bias = ctx.enter_context(nc.sbuf_tensor(f"{tag}_bias", [P, E], F32))
        logits = ctx.enter_context(nc.psum_tensor(f"{tag}_logits", [P, B, E], F32))
        wr_loaded = signal(nc, f"{tag}_wr_loaded")
        bias_loaded = signal(nc, f"{tag}_bias_loaded")
        logits_ready = signal(nc, f"{tag}_logits_ready")
        programs = finish(nc, ctx, tag, logits, bias, rw, logits_ready, bias_loaded)
        with nc.Block() as block:
            @block.sync
            def _(sp):
                sp.dma_start(wr[:, :, :], wr_dram.rearrange("(k p) e -> p k e", p=P)).then_inc(wr_loaded, 16)
                if bias_dram is not None:
                    sp.dma_start(bias[:, :], bias_dram[None, :].to_broadcast([P, E])).then_inc(bias_loaded, 16)

            @block.tensor
            def _(pe):
                pe.wait_ge(wr_loaded, 16)
                for t in range(B):
                    for k in range(KC):
                        last = nc.tensor.matmul(logits[:, t, :], xnT[:, k, t * P:(t + 1) * P], wr[:, k, :],
                                                start=(k == 0), stop=(k == KC - 1))
                last.then_inc(logits_ready, 1)
                if "tensor" in programs:
                    programs["tensor"](pe)

            @block.scalar
            def _(act):
                programs["scalar"](act)

            @block.vector
            def _(dve):
                programs["vector"](dve)


def choose_top(nc, step, count, values, width, top, left, mask):
    full = width + 8 - count
    for t in range(B):
        last = nc.vector.max(top[:, t, :], values[:, t, 0:full])
    step(last, B)
    for t in range(B):
        last = nc.vector.match_replace(left[:, t, 0:full], top[:, t, :], values[:, t, 0:full], -BIG)
    step(last, B)
    step(nc.vector.tensor_tensor(mask, left[:, :, 0:width], values[:, :, 0:width], ALU.is_lt))


def small_tensors(nc, ctx, tag, **shapes):
    return [ctx.enter_context(nc.sbuf_tensor(f"{tag}_{name}", shape, F32)) for name, shape in shapes.items()]


def stepper(dve, sem):
    done = [0]

    def step(ins, _=None):
        done[0] += 1
        ins.then_inc(sem, 1)
        dve.wait_ge(sem, done[0])
    return step


def finish_top2_softmax(nc, ctx, tag, logits, bias, rw, logits_ready, bias_loaded):
    E = logits.shape[2]
    values, top, left, mask, ex, total = small_tensors(
        nc, ctx, tag, values=[P, B, E + 6], top=[P, B, 8], left=[P, B, E + 6], mask=[P, B, E],
        ex=[P, B, E], total=[P, B, 2])
    chain = signal(nc, f"{tag}_chain")
    shifted = signal(nc, f"{tag}_shifted")
    exp_ready = signal(nc, f"{tag}_exp_ready")

    def vector(dve):
        step = stepper(dve, chain)
        step(nc.vector.memset(values[:, :, E:E + 6], BIG))
        step(nc.vector.memset(rw[:, :, E:], 1.0))
        dve.wait_ge(bias_loaded, 16)
        dve.wait_ge(logits_ready, 1)
        step(nc.vector.tensor_tensor(values[:, :, 0:E], logits[:, :, :],
                                     bias[:, None, :].to_broadcast([P, B, E]), ALU.add))
        choose_top(nc, step, 2, values, E, top, left, mask[:, :, :])
        nc.vector.tensor_tensor(ex[:, :, :], values[:, :, 0:E], top[:, :, 6:7].to_broadcast([P, B, E]),
                                ALU.subtract).then_inc(shifted, 1)
        dve.wait_ge(exp_ready, 1)
        step(nc.vector.tensor_tensor(mask[:, :, :], mask[:, :, :], values[:, :, 0:E], ALU.mult))
        step(nc.vector.reduce_sum(total[:, :, 0], mask[:, :, :], AX.X))
        step(nc.vector.reciprocal(total[:, :, 1], total[:, :, 0]))
        step(nc.vector.tensor_tensor(rw[:, :, 0:E], mask[:, :, :], total[:, :, 1:2].to_broadcast([P, B, E]),
                                     ALU.mult))

    def scalar(act):
        act.wait_ge(shifted, 1)
        nc.scalar.activation(values[:, :, 0:E], ex[:, :, :], ACT.Exp).then_inc(exp_ready, 1)

    return {"vector": vector, "scalar": scalar}


def finish_grouped_top8(nc, ctx, tag, logits, bias, rw, logits_ready, bias_loaded):
    E, GROUPS, KEPT, SCALE = logits.shape[2], 8, 4, 2.5
    M = E // GROUPS
    scores, biased, best, pair, chosen, top, left, mask, total = small_tensors(
        nc, ctx, tag, scores=[P, B, E], biased=[P, B, E], best=[P, B, GROUPS + 8 - KEPT],
        pair=[P, B, GROUPS], chosen=[P, B, GROUPS], top=[P, B, 8], left=[P, B, E], mask=[P, B, E], total=[P, B, 2])
    chain = signal(nc, f"{tag}_chain")
    scores_ready = signal(nc, f"{tag}_scores_ready")

    def vector(dve):
        step = stepper(dve, chain)
        step(nc.vector.memset(best[:, :, GROUPS:], BIG))
        step(nc.vector.memset(rw[:, :, E:], 1.0))
        dve.wait_ge(bias_loaded, 16)
        dve.wait_ge(scores_ready, 1)
        step(nc.vector.tensor_tensor(biased[:, :, :], scores[:, :, :],
                                     bias[:, None, :].to_broadcast([P, B, E]), ALU.add))
        member = biased[:, :, :].rearrange("p b (g m) -> p b g m", m=M)
        pairs = [(i, j) for i in range(M) for j in range(i + 1, M)]
        for n, (i, j) in enumerate(pairs):
            out = best[:, :, 0:GROUPS] if n == 0 else pair[:, :, :]
            step(nc.vector.tensor_tensor(out, member[:, :, :, i], member[:, :, :, j], ALU.add))
            if n:
                step(nc.vector.tensor_tensor(best[:, :, 0:GROUPS], best[:, :, 0:GROUPS], pair[:, :, :], ALU.max))
        choose_top(nc, step, KEPT, best, GROUPS, top, left, chosen[:, :, :])
        for m in range(M):
            last = nc.vector.tensor_tensor(member[:, :, :, m], member[:, :, :, m], chosen[:, :, :], ALU.mult)
        step(last)
        choose_top(nc, step, 8, biased, E, top, left, mask[:, :, :])
        step(nc.vector.tensor_tensor(mask[:, :, :], mask[:, :, :], scores[:, :, :], ALU.mult))
        step(nc.vector.reduce_sum(total[:, :, 0], mask[:, :, :], AX.X))
        step(nc.vector.tensor_scalar(total[:, :, 0], total[:, :, 0], 1e-20, None, ALU.add))
        step(nc.vector.reciprocal(total[:, :, 1], total[:, :, 0]))
        step(nc.vector.tensor_tensor(mask[:, :, :], mask[:, :, :], total[:, :, 1:2].to_broadcast([P, B, E]), ALU.mult))
        step(nc.vector.tensor_scalar(rw[:, :, 0:E], mask[:, :, :], SCALE, None, ALU.mult))

    def scalar(act):
        act.wait_ge(logits_ready, 1)
        nc.scalar.activation(scores[:, :, :], logits[:, :, :], ACT.Sigmoid).then_inc(scores_ready, 1)

    return {"vector": vector, "scalar": scalar}


def finish_top1(repeat):
    def finish(nc, ctx, tag, logits, bias, rw, logits_ready, bias_loaded):
        E = logits.shape[2]
        values, top, left, mask = small_tensors(
            nc, ctx, tag, values=[P, B, E + 7], top=[P, B, 8], left=[P, B, E + 7], mask=[P, B, E])
        chain = signal(nc, f"{tag}_chain")
        values_ready = signal(nc, f"{tag}_values_ready")

        def vector(dve):
            step = stepper(dve, chain)
            step(nc.vector.memset(values[:, :, E:], BIG))
            step(nc.vector.memset(rw[:, :, E * repeat:], 1.0))
            dve.wait_ge(values_ready, 1)
            choose_top(nc, step, 1, values, E, top, left, mask[:, :, :])
            for r in range(repeat):
                last = nc.vector.tensor_copy(rw[:, :, r:E * repeat:repeat], mask[:, :, :])
            step(last)

        def scalar(act):
            act.wait_ge(logits_ready, 1)
            nc.scalar.activation(values[:, :, 0:E], logits[:, :, :], ACT.Copy).then_inc(values_ready, 1)

        return {"vector": vector, "scalar": scalar}
    return finish


def finish_top1_capacity(until, ones, capacity):
    def finish(nc, ctx, tag, logits, bias, rw, logits_ready, bias_loaded):
        E = logits.shape[2]
        values, ex, top, left, mask, total, before, peak = small_tensors(
            nc, ctx, tag, values=[P, B, E + 7], ex=[P, B, E], top=[P, B, 8], left=[P, B, E + 7],
            mask=[P, B, E], total=[P, B, 2], before=[P, B, E], peak=[P, B, 1])
        running = ctx.enter_context(nc.psum_tensor(f"{tag}_running", [P, B, E], F32))
        count = ctx.enter_context(nc.psum_tensor(f"{tag}_count", [P, B, E], F32))
        chain = signal(nc, f"{tag}_chain")
        shifted = signal(nc, f"{tag}_shifted")
        exp_ready = signal(nc, f"{tag}_exp_ready")
        mask_ready = signal(nc, f"{tag}_mask_ready")
        counted = signal(nc, f"{tag}_counted")

        def vector(dve):
            step = stepper(dve, chain)
            step(nc.vector.memset(values[:, :, E:], BIG))
            step(nc.vector.memset(before[:, 0, :], 0.0))
            dve.wait_ge(logits_ready, 1)
            step(nc.vector.reduce_max(peak[:, :, 0], logits[:, :, :], AX.X))
            nc.vector.tensor_tensor(ex[:, :, :], logits[:, :, :], peak[:, :, :].to_broadcast([P, B, E]),
                                    ALU.subtract).then_inc(shifted, 1)
            dve.wait_ge(exp_ready, 1)
            step(nc.vector.reduce_sum(total[:, :, 0], values[:, :, 0:E], AX.X))
            step(nc.vector.reciprocal(total[:, :, 1], total[:, :, 0]))
            step(nc.vector.tensor_tensor(values[:, :, 0:E], values[:, :, 0:E],
                                         total[:, :, 1:2].to_broadcast([P, B, E]), ALU.mult))
            choose_top(nc, step, 1, values, E, top, left, mask[:, :, :])
            step(nc.vector.tensor_tensor(ex[:, :, :], values[:, :, 0:E], mask[:, :, :], ALU.mult))
            nc.vector.tensor_copy(top[:, 0, 0:1], top[:, 0, 0:1]).then_inc(mask_ready, 1)
            dve.wait_ge(counted, 1)
            for t in range(1, B):
                step(nc.vector.tensor_tensor(before[:, t, :], before[:, t - 1, :], count[:, t - 1, :], ALU.add))
            step(nc.vector.tensor_tensor(before[:, :, :], before[:, :, :], running[:, :, :], ALU.add))
            step(nc.vector.tensor_scalar(before[:, :, :], before[:, :, :], float(capacity), None, ALU.is_le))
            step(nc.vector.tensor_tensor(rw[:, :, :], ex[:, :, :], before[:, :, :], ALU.mult))

        def scalar(act):
            act.wait_ge(shifted, 1)
            nc.scalar.activation(values[:, :, 0:E], ex[:, :, :], ACT.Exp).then_inc(exp_ready, 1)

        def tensor(pe):
            pe.wait_ge(mask_ready, 1)
            flat = mask[:, :, :].rearrange("p b e -> p (b e)")
            nc.tensor.matmul(running[:, :, :].rearrange("p b e -> p (b e)"), until[:, :], flat, start=True, stop=True)
            nc.tensor.matmul(count[:, :, :].rearrange("p b e -> p (b e)"), ones[:, :], flat,
                             start=True, stop=True).then_inc(counted, 1)

        return {"vector": vector, "scalar": scalar, "tensor": tensor}
    return finish


def ensemble_gate(nc, tag, rw, ctx_dram, itok_dram, ones, n_experts, repeat):
    E = n_experts
    with ExitStack() as ctx:
        weight = ctx.enter_context(nc.sbuf_tensor(f"{tag}_weight", [P, B, P], F32))
        index = ctx.enter_context(nc.sbuf_tensor(f"{tag}_index", [P, B, P], I32))
        index_f = ctx.enter_context(nc.sbuf_tensor(f"{tag}_index_f", [P, B, P], F32))
        picked = ctx.enter_context(nc.sbuf_tensor(f"{tag}_picked", [P, 2, B, P], F32))
        gate = ctx.enter_context(nc.psum_tensor(f"{tag}_gate", [P, E, B], F32))
        weight_loaded = signal(nc, f"{tag}_weight_loaded")
        index_loaded = signal(nc, f"{tag}_index_loaded")
        index_ready = signal(nc, f"{tag}_index_ready")
        picked_ready = signal(nc, f"{tag}_picked_ready")
        gate_ready = signal(nc, f"{tag}_gate_ready")
        with nc.Block() as block:
            @block.sync
            def _(sp):
                sp.dma_start(index[:, :, :], itok_dram.rearrange("b k s -> k b s")).then_inc(index_loaded, 16)
                sp.dma_start(weight[:, :, :], ctx_dram.rearrange("b k s -> k b s")).then_inc(weight_loaded, 16)

            @block.vector
            def _(dve):
                dve.wait_ge(index_loaded, 16)
                nc.vector.tensor_copy(index_f[:, :, :], index[:, :, :]).then_inc(index_ready, 1)
                dve.wait_ge(index_ready, 1)
                dve.wait_ge(weight_loaded, 16)
                for e in range(E):
                    if e >= 2:
                        dve.wait_ge(gate_ready, e - 1)
                    nc.vector.scalar_tensor_tensor(
                        picked[:, e % 2, :, :].rearrange("p b s -> p (b s)"),
                        index_f[:, :, :].rearrange("p b s -> p (b s)"), float(e),
                        weight[:, :, :].rearrange("p b s -> p (b s)"),
                        ALU.is_equal, ALU.mult).then_inc(picked_ready, 1)
                dve.wait_ge(gate_ready, E)
                for r in range(repeat):
                    nc.vector.tensor_copy(rw[:, :, r:E * repeat:repeat],
                                          gate[:, :, :].rearrange("p e b -> p b e"))

            @block.tensor
            def _(pe):
                for e in range(E):
                    pe.wait_ge(picked_ready, e + 1)
                    for b in range(B):
                        last = nc.tensor.matmul(gate[:, e, b:b + 1], picked[:, e % 2, b, :], ones[:, 0:1],
                                                start=True, stop=True)
                    last.then_inc(gate_ready, 1)


def experts(nc, tag, x, xnT, rw, w_dram, func, gated):
    E, _, C, WIDTH = w_dram.shape
    AB = (2 if gated else 1) * D
    STEPS = 2 * NG * C
    PAIRS = E // 2
    assert E % 2 == 0 and WIDTH == AB + D
    with ExitStack() as ctx:
        w = ctx.enter_context(nc.sbuf_tensor(f"{tag}_w", [P, 2, C, WIDTH], F32))
        acted = ctx.enter_context(nc.sbuf_tensor(f"{tag}_acted", [P, 2, GW], F32))
        hidden = ctx.enter_context(nc.sbuf_tensor(f"{tag}_hidden", [P, 2, GW], F32))
        gate = ctx.enter_context(nc.psum_tensor(f"{tag}_gate", [P, 2, GW], F32))
        up = ctx.enter_context(nc.psum_tensor(f"{tag}_up", [P, 2, GW], F32))
        out = ctx.enter_context(nc.psum_tensor(f"{tag}_out", [P, 2, GT, D], F32))
        w_loaded = [signal(nc, f"{tag}_w_loaded{s}") for s in range(2)]
        gate_ready = signal(nc, f"{tag}_gate_ready")
        up_ready = signal(nc, f"{tag}_up_ready")
        acted_ready = signal(nc, f"{tag}_acted_ready")
        hidden_ready = signal(nc, f"{tag}_hidden_ready")
        down_done = signal(nc, f"{tag}_down_done")
        combined = signal(nc, f"{tag}_combined")

        def step_of(s):
            return s // (NG * C), s // C % NG, s % C

        def pairs(engine, program):
            if PAIRS > 1:
                with engine.Fori(0, PAIRS - 1) as pair:
                    program(pair, False)
            program(PAIRS - 1, True)

        with nc.Block() as block:
            @block.sync
            def _(sp):
                for s in range(2):
                    sp.dma_start(w[:, s, :, :], w_dram[s, :, :, :]).then_inc(w_loaded[s], 16)
                with sp.Fori(1, PAIRS) as pair:
                    for s in range(2):
                        sp.wait_ge(down_done, STEPS * pair - (1 - s) * NG * C)
                        sp.dma_start(w[:, s, :, :],
                                     w_dram[bass.ds(2 * pair + s, 1), :, :, :].rearrange("a p c n -> p (a c) n")
                                     ).then_inc(w_loaded[s], 16)

            @block.tensor
            def _(pe):
                def gate_up(pair, s):
                    e, g, c = step_of(s % STEPS)
                    nth = STEPS * pair + s
                    if g == 0 and c == 0:
                        pe.wait_ge(w_loaded[e], 16 * (pair + s // STEPS) + 16)
                    if s > 0:
                        pe.wait_ge(hidden_ready, 2 + nth - 1)
                    for part, (bank, ready) in enumerate(((gate, gate_ready), (up, up_ready))[:AB // D]):
                        for k in range(KC):
                            at = part * D + k * P
                            last = nc.tensor.matmul(bank[:, s % 2, :], w[:, e, c, at:at + P],
                                                    xnT[:, k, g * GW:(g + 1) * GW], start=(k == 0), stop=(k == KC - 1))
                        last.then_inc(ready, 1)

                def down(pair, s):
                    e, g, c = step_of(s)
                    nth = STEPS * pair + s
                    turn = 2 * NG * pair + s // C
                    pe.wait_ge(hidden_ready, 2 + nth + 1)
                    if c == 0:
                        pe.wait_ge(combined, NG + turn - 1)
                    for j in range(GT):
                        last = nc.tensor.matmul(out[:, g % 2, j, :], hidden[:, s % 2, j * P:(j + 1) * P],
                                                w[:, e, c, AB:AB + D], start=(c == 0 and j % 2 == 0),
                                                stop=(c == C - 1), skip_group_check=True)
                    last.then_inc(down_done, 1)

                def program(pair, last):
                    for s in range(STEPS):
                        if not (last and s == STEPS - 1):
                            gate_up(pair, s + 1)
                        down(pair, s)

                gate_up(0, 0)
                pairs(pe, program)

            @block.scalar
            def _(act):
                def program(pair, last):
                    for s in range(STEPS):
                        nth = STEPS * pair + s
                        act.wait_ge(gate_ready, nth + 1)
                        if gated:
                            nc.scalar.activation(acted[:, s % 2, :], gate[:, s % 2, :], func).then_inc(acted_ready, 1)
                        else:
                            nc.scalar.activation(hidden[:, s % 2, :], gate[:, s % 2, :], func).then_inc(hidden_ready, 1)
                pairs(act, program)

            @block.vector
            def _(dve):
                def multiply(pair, s):
                    if not gated:
                        return
                    nth = STEPS * pair + s
                    dve.wait_ge(acted_ready, nth + 1)
                    dve.wait_ge(up_ready, nth + 1)
                    nc.vector.tensor_tensor(hidden[:, s % 2, :], acted[:, s % 2, :], up[:, s % 2, :],
                                            ALU.mult).then_inc(hidden_ready, 1)

                def combine(pair, s):
                    e, g, _ = step_of(s)
                    turn = 2 * NG * pair + s // C
                    dve.wait_ge(down_done, STEPS * pair + s + 1)
                    dve.wait_ge(combined, turn + 1)
                    for j in range(GT):
                        t = g * GT + j
                        expert = 2 * pair + e
                        weight = rw[:, t, expert:expert + 1] if isinstance(pair, int) else \
                            rw[:, t, bass.ds(expert, 1)]
                        last = nc.vector.scalar_tensor_tensor(x[:, t, :], out[:, g % 2, j, :], weight, x[:, t, :],
                                                              ALU.mult, ALU.add)
                    last.then_inc(combined, 1)

                def program(pair, last):
                    for s in range(STEPS):
                        if not (last and s == STEPS - 1):
                            multiply(pair, s + 1)
                        if s % C == C - 1:
                            combine(pair, s)

                dve.sem_inc(combined, NG)
                dve.sem_inc(hidden_ready, 2)
                multiply(0, 0)
                pairs(dve, program)


def attention(nc, tag, x, xnT, ctxT_dram, ident, wq_dram, wk_dram, wv_dram, heads, padded, head_dim, scale,
              wo_dram=None, bq_dram=None, bk_dram=None, bv_dram=None, bo_dram=None):
    CQ = wq_dram.shape[1] // P
    V = wv_dram.shape[1]
    ROWS = min(padded, P)
    RT = P // ROWS
    HC = padded // ROWS
    GH = min(heads, RT * 4)
    GROUPS = heads // GH
    QUAD = min(4, heads)
    QUADS = heads // QUAD
    QC = min(CQ, 4)
    VW = min(V, 512)
    CO = V // P
    OC = min(CO, 4)
    PROJ = [("q", i) for i in range(CQ // QC)] + [("k", i) for i in range(CQ // QC)] + [("v", i) for i in range(V // VW)]
    TURN = [("p", i) for i in range(QUADS)]
    LAST = ([("o", i) for i in range(CO // OC)] + [("y", 0)]) if wo_dram is not None else []
    USES = len(PROJ) + len(TURN) + len(LAST)

    def use_of(pair, b, kind, i, final=False):
        if (kind, i) in PROJ:
            if isinstance(pair, int) and pair == 0 and b == 0:
                at, pair = PROJ.index((kind, i)), 0
            else:
                at = len(PROJ) + USES * (b - 1) + PROJ.index((kind, i))
        else:
            at = (0 if final else len(PROJ)) + len(PROJ) + USES * b + (TURN + LAST).index((kind, i))
        return at % 2, USES * pair + at // 2, 2 * USES * pair + at

    def place(h):
        r = h % RT
        return h // GH, r, (h % GH) // RT, r * ROWS, h // RT * HC

    with ExitStack() as ctx:
        def sb(name, shape):
            return ctx.enter_context(nc.sbuf_tensor(f"{tag}_{name}", shape, F32))

        def sem(name):
            return signal(nc, f"{tag}_{name}")
        wq, wk, wv = sb("wq", [P, KC, CQ * P]), sb("wk", [P, CQ * P]), sb("wv", [P, V])
        wo = sb("wo", [P, CO, D]) if wo_dram is not None else None
        bq = sb("bq", [P, CQ]) if bq_dram is not None else None
        bk = sb("bk", [P, CQ]) if bk_dram is not None else None
        bv = sb("bv", [P, V]) if bv_dram is not None else None
        bo = sb("bo", [P, D]) if bo_dram is not None else None
        keys = sb("keys", [P, 2, P])
        q, k, v = sb("q", [P, 2, CQ, P]), sb("k", [P, 2, CQ, P]), sb("v", [P, 2, V])
        probs = sb("probs", [P, heads, P])
        probsT = sb("probsT", [P, 2, QUAD, P])
        peak, bias = sb("peak", [P, GROUPS, RT, GH // RT]), sb("bias", [P, GROUPS, RT, GH // RT])
        total, inverse = sb("total", [P, heads]), sb("inverse", [P, heads])
        o, oT = sb("o", [P, V]), sb("oT", [P, CO, P])
        work = ctx.enter_context(nc.psum_tensor(f"{tag}_work", [P, 2, 512], F32))
        scores = ctx.enter_context(nc.psum_tensor(f"{tag}_scores", [P, 4, 512], F32))
        o_sum = ctx.enter_context(nc.psum_tensor(f"{tag}_o_sum", [P, 2, 512], F32))
        weights_loaded, keys_loaded = sem("weights_loaded"), [sem("keys_loaded0"), sem("keys_loaded1")]
        work_ready, work_free = sem("work_ready"), [sem("work_free0"), sem("work_free1")]
        qkv_ready, scores_ready, bias_ready, exp_done = sem("qkv_ready"), sem("scores_ready"), sem("bias_ready"), sem("exp_done")
        o_summed, o_ready, chain, x_ready = sem("o_summed"), sem("o_ready"), sem("chain"), sem("x_ready")
        n_weights = 3 + sum(m is not None for m in (wo, bq, bk, bv, bo))

        def batches(engine, program):
            with engine.Fori(0, B // 2 - 1) as pair:
                for b in range(2):
                    program(pair, b, False)
            for b in range(2):
                program(B // 2 - 1, b, b == 1)

        def next_of(pair, b):
            return (pair, 1) if b == 0 else (pair + 1, 0)

        with nc.Block() as block:
            @block.sync
            def _(sp):
                def load(dst, src):
                    sp.dma_start(dst, src).then_inc(weights_loaded, 16)
                load(wq[:, :, :], wq_dram.rearrange("(k p) n -> p k n", p=P))
                load(wk[:, :], wk_dram)
                load(wv[:, :], wv_dram)
                for b in range(2):
                    sp.dma_start(keys[:, b, :], ctxT_dram[b, :, :]).then_inc(keys_loaded[b], 16)
                if wo is not None:
                    load(wo[:, :, :], wo_dram.rearrange("(c p) n -> p c n", p=P))
                if bq is not None:
                    load(bq[:, :], bq_dram)
                    load(bk[:, :], bk_dram)
                    load(bv[:, :], bv_dram[None, :].to_broadcast([P, V]))
                if bo is not None:
                    load(bo[:, :], bo_dram[None, :].to_broadcast([P, D]))
                with sp.Fori(1, B // 2) as pair:
                    for b in range(2):
                        sp.wait_ge(qkv_ready, 2 * pair - 1 + b)
                        sp.dma_start(keys[:, b, :], ctxT_dram[bass.ds(2 * pair + b, 1), :, :].rearrange("a d m -> d (a m)")
                                     ).then_inc(keys_loaded[b], 16)

            @block.tensor
            def _(pe):
                def take(pair, b, kind, i, final=False):
                    slot, before, _ = use_of(pair, b, kind, i, final)
                    if not isinstance(before, int) or before > 0:
                        pe.wait_ge(work_free[slot], before)
                    return slot

                def read_out(pair, b, kind, i, final=False):
                    slot, before, _ = use_of(pair, b, kind, i, final)
                    pe.wait_ge(work_free[slot], before + 1)

                def project(pair, b):
                    for kind, i in PROJ:
                        slot = take(pair, b, kind, i)
                        if (kind, i) == ("k", 0):
                            pe.wait_ge(keys_loaded[b], 16 * pair + 16)
                        if kind == "q":
                            for j in range(QC):
                                at = (i * QC + j) * P
                                for c in range(KC):
                                    last = nc.tensor.matmul(work[:, slot, j * P:(j + 1) * P], wq[:, c, at:at + P],
                                                            xnT[:, c, bass.ts(2 * pair + b, P)],
                                                            start=(c == 0), stop=(c == KC - 1))
                        elif kind == "k":
                            for j in range(QC):
                                at = (i * QC + j) * P
                                last = nc.tensor.matmul(work[:, slot, j * P:(j + 1) * P], wk[:, at:at + P],
                                                        keys[:, b, :], start=True, stop=True)
                        else:
                            last = nc.tensor.matmul(work[:, slot, 0:VW], keys[:, b, :], wv[:, i * VW:(i + 1) * VW],
                                                    start=True, stop=True)
                        last.then_inc(work_ready, 1)

                def score(pair, b, g):
                    if g == 0:
                        pe.wait_ge(qkv_ready, 2 * pair + b + 1)
                    n = GROUPS * (2 * pair + b) + g
                    for h in range(g * GH, (g + 1) * GH):
                        _, r, col, row, chunk = place(h)
                        bank = (g * RT + r) % 4
                        for c in range(HC):
                            last = nc.tensor.matmul(scores[:, bank, col * P:(col + 1) * P],
                                                    q[row:row + ROWS, b, chunk + c, :], k[row:row + ROWS, b, chunk + c, :],
                                                    start=(c == 0), stop=(c == HC - 1))
                    last.then_inc(scores_ready, 1)

                def turn(pair, b, i, final):
                    slot = take(pair, b, "p", i, final)
                    pe.wait_ge(exp_done, heads * (2 * pair + b) + QUAD * (i + 1))
                    for j in range(QUAD):
                        last = nc.tensor.transpose(work[:, slot, j * P:(j + 1) * P], probs[:, i * QUAD + j, :],
                                                   ident[:, :])
                    last.then_inc(work_ready, 1)

                def weigh(pair, b, i, final):
                    read_out(pair, b, "p", i, final)
                    if i == 0:
                        pe.wait_ge(o_ready, 2 * pair + b + 1)
                    for j in range(QUAD):
                        h = i * QUAD + j
                        at = h * (V // heads)
                        last = nc.tensor.matmul(o_sum[:, at // 512, at % 512:at % 512 + V // heads], probsT[:, i % 2, j, :],
                                                v[:, b, at:at + V // heads], start=True, stop=True)
                    if i == QUADS - 1:
                        last.then_inc(o_summed, 1)

                def project_out(pair, b, final):
                    pe.wait_ge(o_ready, 2 * pair + b + 2)
                    for kind, i in LAST[:-1]:
                        slot = take(pair, b, kind, i, final)
                        for j in range(OC):
                            c = i * OC + j
                            last = nc.tensor.transpose(work[:, slot, j * P:(j + 1) * P], o[:, c * P:(c + 1) * P],
                                                       ident[:, :])
                        last.then_inc(work_ready, 1)
                    slot = take(pair, b, "y", 0, final)
                    for kind, i in LAST[:-1]:
                        read_out(pair, b, kind, i, final)
                    for c in range(CO):
                        last = nc.tensor.matmul(work[:, slot, 0:D], oT[:, c, :], wo[:, c, :],
                                                start=(c == 0), stop=(c == CO - 1))
                    last.then_inc(work_ready, 1)

                def program(pair, b, final):
                    for g in range(GROUPS):
                        score(pair, b, g)
                    if not final:
                        project(*next_of(pair, b))
                    for i in range(QUADS):
                        turn(pair, b, i, final)
                        if i > 0:
                            weigh(pair, b, i - 1, final)
                    weigh(pair, b, QUADS - 1, final)
                    if wo is not None:
                        project_out(pair, b, final)

                pe.wait_ge(weights_loaded, 16 * n_weights)
                project(0, 0)
                batches(pe, program)

            @block.scalar
            def _(act):
                def copy_out(pair, b, kind, i, dst, width, final=False):
                    slot, _, before = use_of(pair, b, kind, i, final)
                    act.wait_ge(work_ready, before + 1)
                    nc.scalar.activation(dst, work[:, slot, 0:width], ACT.Copy).then_inc(work_free[slot], 1)

                def exps(pair, b, i):
                    for h in range(i * QUAD, (i + 1) * QUAD):
                        g, r, col, _, _ = place(h)
                        if h % GH == 0:
                            act.wait_ge(bias_ready, GROUPS * (2 * pair + b) + g + 1)
                        nc.scalar.activation(probs[:, h, :], scores[:, (g * RT + r) % 4, col * P:(col + 1) * P], ACT.Exp,
                                             bias=bias[:, g, r, col:col + 1], scale=scale,
                                             accum_out=total[:, h:h + 1]).then_inc(exp_done, 1)

                def program(pair, b, final):
                    for i in range(QUADS + 1):
                        if i < QUADS:
                            exps(pair, b, i)
                        if i > 0:
                            copy_out(pair, b, "p", i - 1, probsT[:, (i - 1) % 2, :, :].rearrange("p a n -> p (a n)"),
                                     QUAD * P, final)
                    for kind, i in LAST[:-1]:
                        copy_out(pair, b, kind, i, oT[:, i * OC:(i + 1) * OC, :].rearrange("p a n -> p (a n)"),
                                 OC * P, final)

                batches(act, program)

            @block.vector
            def _(dve):
                def largest(pair, b, g):
                    dve.wait_ge(scores_ready, GROUPS * (2 * pair + b) + g + 1)
                    bank = g * RT % 4
                    nc.vector.reduce_max(
                        peak[:, g, :, :],
                        scores[:, bank:bank + RT, 0:GH // RT * P].rearrange("p r (c n) -> p r c n", n=P),
                        AX.X).then_inc(chain, 1)
                    dve.wait_ge(chain, (GROUPS + 1) * (2 * pair + b) + g + 1)
                    nc.vector.tensor_scalar(bias[:, g, :, :], peak[:, g, :, :], -scale, None,
                                            ALU.mult).then_inc(bias_ready, 1)

                def projected(pair, b):
                    for kind, i in PROJ:
                        slot, _, before = use_of(pair, b, kind, i)
                        dve.wait_ge(work_ready, before + 1)
                        if kind == "v":
                            dst, src = v[:, b, i * VW:(i + 1) * VW], work[:, slot, 0:VW]
                            add = bv[:, i * VW:(i + 1) * VW] if bv is not None else None
                        else:
                            dst = (q if kind == "q" else k)[:, b, i * QC:(i + 1) * QC, :]
                            src = work[:, slot, 0:QC * P].rearrange("p (a n) -> p a n", n=P)
                            rows = bq if kind == "q" else bk
                            add = rows[:, i * QC:(i + 1) * QC, None].to_broadcast([P, QC, P]) if bq is not None else None
                        if add is not None:
                            last = nc.vector.tensor_tensor(dst, src, add, ALU.add)
                        else:
                            last = nc.vector.tensor_copy(dst, src)
                        last.then_inc(work_free[slot], 1)
                    nc.vector.tensor_copy(peak[:, 0, 0, 0:1], peak[:, 0, 0, 0:1]).then_inc(qkv_ready, 1)

                def program(pair, b, final):
                    for g in range(GROUPS):
                        largest(pair, b, g)
                    if not final:
                        projected(*next_of(pair, b))
                    dve.wait_ge(exp_done, heads * (2 * pair + b + 1))
                    nc.vector.reciprocal(inverse[:, :], total[:, :]).then_inc(chain, 1)
                    dve.wait_ge(chain, (GROUPS + 1) * (2 * pair + b + 1))
                    dve.wait_ge(o_summed, 2 * pair + b + 1)
                    tile = x[:, bass.ds(2 * pair + b, 1), :].rearrange("p a d -> p (a d)") \
                        if not isinstance(pair, int) else x[:, 2 * pair + b, :]
                    if wo is None:
                        nc.vector.scalar_tensor_tensor(tile, o_sum[:, 0, 0:V], inverse[:, 0:1], tile,
                                                       ALU.mult, ALU.add).then_inc(o_ready, 1)
                        return
                    banks = max(1, V // 512)
                    sums = o_sum[:, 0:banks, 0:V // banks].rearrange("p a (h n) -> p (a h) n", n=V // heads) \
                        if banks == 1 else o_sum[:, :, :].rearrange("p a (h n) -> p (a h) n", n=V // heads)
                    nc.vector.tensor_tensor(o[:, :].rearrange("p (h n) -> p h n", n=V // heads), sums,
                                            inverse[:, :, None].to_broadcast([P, heads, V // heads]),
                                            ALU.mult).then_inc(o_ready, 1)
                    slot, _, before = use_of(pair, b, "y", 0, final)
                    dve.wait_ge(work_ready, before + 1)
                    nc.vector.tensor_tensor(tile, tile, work[:, slot, 0:D], ALU.add).then_inc(work_free[slot], 1)

                dve.sem_inc(o_ready, 1)
                dve.wait_ge(weights_loaded, 16 * n_weights)
                if bo is not None:
                    nc.vector.tensor_tensor(x[:, :, :], x[:, :, :], bo[:, None, :].to_broadcast([P, B, D]),
                                            ALU.add).then_inc(x_ready, 1)
                    dve.wait_ge(x_ready, 1)
                nc.vector.memset(peak[:, :, :, :], 0.0)
                projected(0, 0)
                batches(dve, program)


def build(nc, t, out, stages=range(8)):
    with ExitStack() as ctx:
        x = ctx.enter_context(nc.sbuf_tensor("x", [P, B, D], F32))
        xn = ctx.enter_context(nc.sbuf_tensor("xn", [P, B, D], F32))
        xnT = ctx.enter_context(nc.sbuf_tensor("xnT", [P, KC, T], F32))
        ident = ctx.enter_context(nc.sbuf_tensor("ident", [P, P], F32))
        ones = ctx.enter_context(nc.sbuf_tensor("ones", [P, P], F32))
        until = ctx.enter_context(nc.sbuf_tensor("until", [P, P], F32))
        LIVE.clear()
        loaded = nc.alloc_semaphore("loaded")
        stored = nc.alloc_semaphore("stored")

        def load(sp):
            sp.dma_start(x[:, :, :], t["x"].rearrange("b p d -> p b d")).then_inc(loaded, 16)
            sp.dma_start(ident[:, :], t["identity"]).then_inc(loaded, 16)
            sp.dma_start(until[:, :], t["until"]).then_inc(loaded, 16)
            sp.wait_ge(loaded, 48)

        with nc.Block() as block:
            @block.sync
            def _(sp):
                load(sp)

            @block.gpsimd
            def _(pool):
                nc.gpsimd.memset(ones[:, :], 1.0)

        def routed(tag, columns, route, *arguments):
            with nc.sbuf_tensor(f"{tag}_rw", [P, B, columns], F32) as rw:
                route(rw)
                experts(nc, tag, x, xnT, rw, *arguments)

        if 0 in stages:
            layer_norm(nc, "n0", x, xn, xnT, ident)
            attention(nc, "a0", x, xnT, t["ctxT"], ident, t["L0_xattn_Wq"], t["L0_xattn_Wk"], t["L0_xattn_Wv"],
                      16, 64, 64, 64 ** -0.5, wo_dram=t["L0_xattn_Wo"], bo_dram=t["L0_xattn_bo"])
        recycle_signals(nc)
        if 1 in stages:
            layer_norm(nc, "n1", x, xn, xnT, ident)
            routed("f0", 10, lambda rw: routing(nc, "r0", xnT, rw, t["L0_wr"], 8, finish_top2_softmax,
                                                t["L0_ffn_expert_bias"]), t["L0_experts"], ACT.Silu, True)
        recycle_signals(nc)
        if 2 in stages:
            layer_norm(nc, "n2", x, xn, xnT, ident)
            attention(nc, "a1", x, xnT, t["ctxT"], ident, t["L1_xattn_Wq"], t["L1_xattn_Wk"], t["L1_xattn_Wv"],
                      1, 256, 256, 1.0, bq_dram=t["L1_xattn_bq"], bk_dram=t["L1_xattn_bk"], bv_dram=t["L1_xattn_bv"])
        recycle_signals(nc)
        if 3 in stages:
            layer_norm(nc, "n3", x, xn, xnT, ident)
            routed("f1", 34, lambda rw: routing(nc, "r1", xnT, rw, t["L1_wr"], 32, finish_grouped_top8,
                                                t["L1_ffn_gate_bias"]), t["L1_experts"], ACT.Silu, True)
        recycle_signals(nc)
        if 4 in stages:
            layer_norm(nc, "n4", x, xn, xnT, ident)
            routed("e2", 16, lambda rw: ensemble_gate(nc, "g2", rw, t["ctx"], t["itok"], ones, 8, 2),
                   t["L2_ensemble"], ACT.Relu, False)
        recycle_signals(nc)
        if 5 in stages:
            layer_norm(nc, "n5", x, xn, xnT, ident)
            routed("f2", 36, lambda rw: routing(nc, "r2", xnT, rw, t["L2_wr"], 8, finish_top1(4)),
                   t["L2_experts"], ACT.Gelu, True)
        recycle_signals(nc)
        if 6 in stages:
            layer_norm(nc, "n6", x, xn, xnT, ident)
            attention(nc, "a3", x, xnT, t["ctxT"], ident, t["L3_xattn_Wq"], t["L3_xattn_Wk"], t["L3_xattn_Wv"],
                      16, 32, 16, 0.25, wo_dram=t["L3_xattn_Wo"], bq_dram=t["L3_xattn_bq"], bk_dram=t["L3_xattn_bk"],
                      bv_dram=t["L3_xattn_bv"], bo_dram=t["L3_xattn_bo"])
        recycle_signals(nc)
        if 7 in stages:
            layer_norm(nc, "n7", x, xn, xnT, ident)
            x_summed = signal(nc, "x_summed")

            def route(rw):
                routing(nc, "r3", xnT, rw, t["L3_wr"], 32, finish_top1_capacity(until, ones, CAPACITY))
                with nc.Block() as block:
                    @block.gpsimd
                    def _(pool):
                        nc.gpsimd.tensor_tensor(x[:, :, :], x[:, :, :], xn[:, :, :], ALU.add).then_inc(x_summed, 1)
                        pool.wait_ge(x_summed, 1)
            routed("f3", 32, route, t["L3_experts"], ACT.Silu, True)
        with nc.Block() as block:
            @block.sync
            def _(sp):
                sp.dma_start(out.rearrange("b p d -> p b d"), x[:, :, :]).then_inc(stored, 16)
                sp.wait_ge(stored, 16)


def pack(a, b, c, chunks):
    def rows(m):
        e, _, f = m.shape
        return m.reshape(e, KC, P, f // P, P).transpose(0, 3, 2, 1, 4).reshape(e * (f // P), P, D)
    parts = [rows(a)] + ([rows(b)] if b is not None else []) + [c.reshape(-1, P, D)]
    packed = np.concatenate(parts, axis=2)
    return np.ascontiguousarray(packed.reshape(-1, chunks, P, packed.shape[2]).transpose(0, 2, 1, 3))


def kernel(**inputs):
    import concourse.bacc as bacc
    from concourse.bass_utils import run_bass_kernel_spmd

    a = {name: np.asarray(value) for name, value in inputs.items()}
    f = lambda name: a[name].astype(a[name].dtype)
    sw = lambda m: m.transpose(0, 2, 1)
    arrays = {
        "x": a["x"], "ctx": a["ctx_512"], "itok": a["itok_BxS2xS_0_7"],
        "ctxT": np.ascontiguousarray(sw(a["ctx_512"])),
        "identity": np.eye(P, dtype=np.float32),
        "until": np.triu(np.ones((P, P), np.float32)),
        "L0_experts": np.concatenate([pack(a["L0_ffn_Wg"], a["L0_ffn_Wu"], a["L0_ffn_Wd"], 1),
                                      pack(a["L0_ffn_Sg"][None], a["L0_ffn_Su"][None], a["L0_ffn_Sd"][None], 1)]),
        "L0_wr": a["L0_ffn_Wr"], "L0_ffn_expert_bias": a["L0_ffn_expert_bias"],
        "L1_experts": np.concatenate([pack(sw(a["L1_ffn_w_gate"]), sw(a["L1_ffn_w_up"]), sw(a["L1_ffn_w_down"]), 1),
                                      pack(a["L1_ffn_sh_gate"].T[None], a["L1_ffn_sh_up"].T[None],
                                           a["L1_ffn_sh_down"].T[None], 1)]),
        "L1_wr": np.ascontiguousarray(a["L1_ffn_gate_w"].T), "L1_ffn_gate_bias": a["L1_ffn_gate_bias"],
        "L2_ensemble": pack(sw(a["L2_xattn_proj_in"]), None, sw(a["L2_xattn_proj_out"]), 2),
        "L2_experts": np.concatenate([pack(a["L2_ffn_W1"], a["L2_ffn_W2"], a["L2_ffn_W3"], 2),
                                      pack(a["L2_ffn_w1s"][None], a["L2_ffn_w2s"][None], a["L2_ffn_w3s"][None], 2)]),
        "L2_wr": a["L2_ffn_Wg"],
        "L3_experts": pack(a["L3_ffn_w_gate"], a["L3_ffn_w_up"], a["L3_ffn_w_down"], 2),
        "L3_wr": a["L3_ffn_w_router"],
    }
    for name in a:
        if "_xattn_" in name and "proj" not in name:
            m = a[name]
            if name in ("L3_xattn_Wq", "L3_xattn_Wk"):
                m = np.concatenate([m.reshape(-1, 16, 16), np.zeros((m.shape[0], 16, 16), m.dtype)], 2).reshape(-1, 512)
            if name in ("L3_xattn_bq", "L3_xattn_bk"):
                m = np.concatenate([m.reshape(16, 16), np.zeros((16, 16), m.dtype)], 1).reshape(512)
            if name in ("L1_xattn_bq", "L1_xattn_bk", "L3_xattn_bq", "L3_xattn_bk"):
                m = m.reshape(-1, P).T
            arrays[name] = m
    arrays = {name: np.ascontiguousarray(value) for name, value in arrays.items()}
    nc = bacc.Bacc("TRN2", target_bir_lowering=False, num_devices=1)
    tensors = {name: nc.dram_tensor(name + "_dram", value.shape, mybir.dt.from_np(value.dtype),
                                    kind="ExternalInput").ap() for name, value in arrays.items()}
    out = nc.dram_tensor("out_dram", (B, P, D), F32, kind="ExternalOutput").ap()
    build(nc, tensors, out)
    result = run_bass_kernel_spmd(nc, [{name + "_dram": value for name, value in arrays.items()}], core_ids=[0])
    return result.results[0]["out_dram"]
```

```python
from contextlib import ExitStack

import numpy as np
import concourse.bass as bass
from concourse import mybir

F32 = mybir.dt.float32
I32 = mybir.dt.int32
ACT = mybir.ActivationFunctionType
ALU = mybir.AluOpType
AX = mybir.AxisListType

P = 128
B = 16
D = 256
KC = D // P
T = B * P
GT = 4
GW = GT * P
NG = B // GT
EPS = 1e-5
BIG = 3.0e38
CAPACITY = -(-5 * T // (4 * 32))
SORTED_TILES = 24


LIVE = []


def signal(nc, name):
    LIVE.append(nc.alloc_semaphore(name))
    return LIVE[-1]


def recycle_signals(nc):
    nc.clear_and_free_semaphores(LIVE)
    LIVE.clear()
    nc.all_engine_barrier()


def layer_norm(nc, tag, x, xn, xnT, ident):
    with ExitStack() as ctx:
        stats = ctx.enter_context(nc.sbuf_tensor(f"{tag}_stats", [P, B, 6], F32))
        mean_var = ctx.enter_context(nc.sbuf_tensor(f"{tag}_mean_var", [P, B, 2], F32))
        spread = ctx.enter_context(nc.sbuf_tensor(f"{tag}_spread", [P, B, 3], F32))
        turned = ctx.enter_context(nc.psum_tensor(f"{tag}_turned", [P, 2, GW], F32))
        stats_done = signal(nc, f"{tag}_stats_done")
        var_ready = signal(nc, f"{tag}_var_ready")
        std_ready = signal(nc, f"{tag}_std_ready")
        rstd_ready = signal(nc, f"{tag}_rstd_ready")
        xn_ready = signal(nc, f"{tag}_xn_ready")
        turned_ready = signal(nc, f"{tag}_turned_ready")
        xnT_written = signal(nc, f"{tag}_xnT_written")
        with nc.Block() as block:
            @block.vector
            def _(dve):
                for t in range(B):
                    nc.vector.bn_stats(stats[:, t, :], x[:, t, :]).then_inc(stats_done, 1)
                dve.wait_ge(stats_done, B)
                for t in range(B):
                    nc.vector.bn_aggr(mean_var[:, t, :], stats[:, t, :]).then_inc(var_ready, 1)
                dve.wait_ge(var_ready, B)
                nc.vector.tensor_scalar(spread[:, :, 0], mean_var[:, :, 1], EPS, None, ALU.add).then_inc(var_ready, 1)
                dve.wait_ge(std_ready, 1)
                nc.vector.reciprocal(spread[:, :, 2], spread[:, :, 1]).then_inc(rstd_ready, 1)
                dve.wait_ge(rstd_ready, 1)
                for t in range(B):
                    nc.vector.tensor_scalar(xn[:, t, :], x[:, t, :], mean_var[:, t, 0:1], spread[:, t, 2:3],
                                            ALU.subtract, ALU.mult).then_inc(xn_ready, 1)

            @block.tensor
            def _(pe):
                for g in range(NG):
                    for k in range(KC):
                        n = g * KC + k
                        if n >= 2:
                            pe.wait_ge(xnT_written, n - 1)
                        for j in range(GT):
                            t = g * GT + j
                            pe.wait_ge(xn_ready, t + 1)
                            last = nc.tensor.transpose(turned[:, n % 2, j * P:(j + 1) * P],
                                                       xn[:, t, k * P:(k + 1) * P], ident[:, :])
                        last.then_inc(turned_ready, 1)

            @block.scalar
            def _(act):
                act.wait_ge(var_ready, B + 1)
                nc.scalar.activation(spread[:, :, 1], spread[:, :, 0], ACT.Sqrt).then_inc(std_ready, 1)
                for g in range(NG):
                    for k in range(KC):
                        n = g * KC + k
                        act.wait_ge(turned_ready, n + 1)
                        nc.scalar.activation(xnT[:, k, g * GW:(g + 1) * GW], turned[:, n % 2, :],
                                             ACT.Copy).then_inc(xnT_written, 1)


def routing(nc, tag, xnT, rw, wr_dram, n_experts, finish, bias_dram=None):
    with ExitStack() as ctx:
        E = n_experts
        wr = ctx.enter_context(nc.sbuf_tensor(f"{tag}_wr", [P, KC, E], F32))
        bias = ctx.enter_context(nc.sbuf_tensor(f"{tag}_bias", [P, E], F32))
        logits = ctx.enter_context(nc.psum_tensor(f"{tag}_logits", [P, B, E], F32))
        wr_loaded = signal(nc, f"{tag}_wr_loaded")
        bias_loaded = signal(nc, f"{tag}_bias_loaded")
        logits_ready = signal(nc, f"{tag}_logits_ready")
        programs = finish(nc, ctx, tag, logits, bias, rw, logits_ready, bias_loaded)
        with nc.Block() as block:
            @block.sync
            def _(sp):
                sp.dma_start(wr[:, :, :], wr_dram.rearrange("(k p) e -> p k e", p=P)).then_inc(wr_loaded, 16)
                if bias_dram is not None:
                    sp.dma_start(bias[:, :], bias_dram[None, :].to_broadcast([P, E])).then_inc(bias_loaded, 16)

            @block.tensor
            def _(pe):
                pe.wait_ge(wr_loaded, 16)
                for t in range(B):
                    for k in range(KC):
                        last = nc.tensor.matmul(logits[:, t, :], xnT[:, k, t * P:(t + 1) * P], wr[:, k, :],
                                                start=(k == 0), stop=(k == KC - 1))
                last.then_inc(logits_ready, 1)
                if "tensor" in programs:
                    programs["tensor"](pe)

            @block.scalar
            def _(act):
                programs["scalar"](act)

            @block.vector
            def _(dve):
                programs["vector"](dve)


def choose_top(nc, step, count, values, width, top, left, mask):
    full = width + 8 - count
    for t in range(B):
        last = nc.vector.max(top[:, t, :], values[:, t, 0:full])
    step(last, B)
    for t in range(B):
        last = nc.vector.match_replace(left[:, t, 0:full], top[:, t, :], values[:, t, 0:full], -BIG)
    step(last, B)
    step(nc.vector.tensor_tensor(mask, left[:, :, 0:width], values[:, :, 0:width], ALU.is_lt))


def small_tensors(nc, ctx, tag, **shapes):
    return [ctx.enter_context(nc.sbuf_tensor(f"{tag}_{name}", shape, F32)) for name, shape in shapes.items()]


def stepper(dve, sem):
    done = [0]

    def step(ins, _=None):
        done[0] += 1
        ins.then_inc(sem, 1)
        dve.wait_ge(sem, done[0])
    return step


def finish_top2_softmax(nc, ctx, tag, logits, bias, rw, logits_ready, bias_loaded):
    E = logits.shape[2]
    values, top, left, mask, ex, total = small_tensors(
        nc, ctx, tag, values=[P, B, E + 6], top=[P, B, 8], left=[P, B, E + 6], mask=[P, B, E],
        ex=[P, B, E], total=[P, B, 2])
    chain = signal(nc, f"{tag}_chain")
    shifted = signal(nc, f"{tag}_shifted")
    exp_ready = signal(nc, f"{tag}_exp_ready")

    def vector(dve):
        step = stepper(dve, chain)
        step(nc.vector.memset(values[:, :, E:E + 6], BIG))
        step(nc.vector.memset(rw[:, :, E:], 1.0))
        dve.wait_ge(bias_loaded, 16)
        dve.wait_ge(logits_ready, 1)
        step(nc.vector.tensor_tensor(values[:, :, 0:E], logits[:, :, :],
                                     bias[:, None, :].to_broadcast([P, B, E]), ALU.add))
        choose_top(nc, step, 2, values, E, top, left, mask[:, :, :])
        nc.vector.tensor_tensor(ex[:, :, :], values[:, :, 0:E], top[:, :, 6:7].to_broadcast([P, B, E]),
                                ALU.subtract).then_inc(shifted, 1)
        dve.wait_ge(exp_ready, 1)
        step(nc.vector.tensor_tensor(mask[:, :, :], mask[:, :, :], values[:, :, 0:E], ALU.mult))
        step(nc.vector.reduce_sum(total[:, :, 0], mask[:, :, :], AX.X))
        step(nc.vector.reciprocal(total[:, :, 1], total[:, :, 0]))
        step(nc.vector.tensor_tensor(rw[:, :, 0:E], mask[:, :, :], total[:, :, 1:2].to_broadcast([P, B, E]),
                                     ALU.mult))

    def scalar(act):
        act.wait_ge(shifted, 1)
        nc.scalar.activation(values[:, :, 0:E], ex[:, :, :], ACT.Exp).then_inc(exp_ready, 1)

    return {"vector": vector, "scalar": scalar}


def finish_grouped_top8(nc, ctx, tag, logits, bias, rw, logits_ready, bias_loaded):
    E, GROUPS, KEPT, SCALE = logits.shape[2], 8, 4, 2.5
    M = E // GROUPS
    scores, biased, best, pair, chosen, top, left, mask, total = small_tensors(
        nc, ctx, tag, scores=[P, B, E], biased=[P, B, E], best=[P, B, GROUPS + 8 - KEPT],
        pair=[P, B, GROUPS], chosen=[P, B, GROUPS], top=[P, B, 8], left=[P, B, E], mask=[P, B, E], total=[P, B, 2])
    chain = signal(nc, f"{tag}_chain")
    scores_ready = signal(nc, f"{tag}_scores_ready")

    def vector(dve):
        step = stepper(dve, chain)
        step(nc.vector.memset(best[:, :, GROUPS:], BIG))
        step(nc.vector.memset(rw[:, :, E:], 1.0))
        dve.wait_ge(bias_loaded, 16)
        dve.wait_ge(scores_ready, 1)
        step(nc.vector.tensor_tensor(biased[:, :, :], scores[:, :, :],
                                     bias[:, None, :].to_broadcast([P, B, E]), ALU.add))
        member = biased[:, :, :].rearrange("p b (g m) -> p b g m", m=M)
        pairs = [(i, j) for i in range(M) for j in range(i + 1, M)]
        for n, (i, j) in enumerate(pairs):
            out = best[:, :, 0:GROUPS] if n == 0 else pair[:, :, :]
            step(nc.vector.tensor_tensor(out, member[:, :, :, i], member[:, :, :, j], ALU.add))
            if n:
                step(nc.vector.tensor_tensor(best[:, :, 0:GROUPS], best[:, :, 0:GROUPS], pair[:, :, :], ALU.max))
        choose_top(nc, step, KEPT, best, GROUPS, top, left, chosen[:, :, :])
        for m in range(M):
            last = nc.vector.tensor_tensor(member[:, :, :, m], member[:, :, :, m], chosen[:, :, :], ALU.mult)
        step(last)
        choose_top(nc, step, 8, biased, E, top, left, mask[:, :, :])
        step(nc.vector.tensor_tensor(mask[:, :, :], mask[:, :, :], scores[:, :, :], ALU.mult))
        step(nc.vector.reduce_sum(total[:, :, 0], mask[:, :, :], AX.X))
        step(nc.vector.tensor_scalar(total[:, :, 0], total[:, :, 0], 1e-20, None, ALU.add))
        step(nc.vector.reciprocal(total[:, :, 1], total[:, :, 0]))
        step(nc.vector.tensor_tensor(mask[:, :, :], mask[:, :, :], total[:, :, 1:2].to_broadcast([P, B, E]), ALU.mult))
        step(nc.vector.tensor_scalar(rw[:, :, 0:E], mask[:, :, :], SCALE, None, ALU.mult))

    def scalar(act):
        act.wait_ge(logits_ready, 1)
        nc.scalar.activation(scores[:, :, :], logits[:, :, :], ACT.Sigmoid).then_inc(scores_ready, 1)

    return {"vector": vector, "scalar": scalar}


def finish_top1_sorted(until, ones, steps, slot, tile_expert):
    def finish(nc, ctx, tag, logits, bias, rw, logits_ready, bias_loaded):
        E = logits.shape[2]
        values, top, left, mask, before, above, reached, tiles, ends, place = small_tensors(
            nc, ctx, tag, values=[P, B, E + 7], top=[P, B, 8], left=[P, B, E + 7], mask=[P, B, E],
            before=[P, B + 1, E], above=[P, E, B], reached=[P, SORTED_TILES, E], tiles=[P, E], ends=[P, E],
            place=[P, SORTED_TILES])
        running = ctx.enter_context(nc.psum_tensor(f"{tag}_running", [P, B, E], F32))
        count = ctx.enter_context(nc.psum_tensor(f"{tag}_count", [P, B, E], F32))
        chain = signal(nc, f"{tag}_chain")
        values_ready = signal(nc, f"{tag}_values_ready")
        mask_ready = signal(nc, f"{tag}_mask_ready")
        counted = signal(nc, f"{tag}_counted")

        def vector(dve):
            step = stepper(dve, chain)
            step(nc.vector.memset(values[:, :, E:], BIG))
            step(nc.vector.memset(before[:, 0, :], 0.0))
            dve.wait_ge(values_ready, 1)
            choose_top(nc, step, 1, values, E, top, left, mask[:, :, :])
            nc.vector.tensor_copy(ends[:, :], mask[:, 0, :]).then_inc(mask_ready, 1)
            dve.wait_ge(mask_ready, 1)
            dve.wait_ge(counted, 1)
            for t in range(1, B + 1):
                step(nc.vector.tensor_tensor(before[:, t, :], before[:, t - 1, :], count[:, t - 1, :], ALU.add))
            step(nc.vector.tensor_scalar(above[:, :, :], steps[:, None, 0:B].to_broadcast([P, E, B]), float(P), None,
                                         ALU.mult))
            step(nc.vector.tensor_tensor(above[:, :, :], before[:, B, :, None].to_broadcast([P, E, B]),
                                         above[:, :, :], ALU.is_gt))
            step(nc.vector.reduce_sum(tiles[:, :], above[:, :, :], AX.X))
            step(nc.vector.tensor_copy(ends[:, :], tiles[:, :]))
            for e in range(1, E):
                step(nc.vector.tensor_tensor(ends[:, e:e + 1], ends[:, e - 1:e], tiles[:, e:e + 1], ALU.add))
            step(nc.vector.tensor_tensor(reached[:, :, :], steps[:, :, None].to_broadcast([P, SORTED_TILES, E]),
                                         ends[:, None, :].to_broadcast([P, SORTED_TILES, E]), ALU.is_ge))
            step(nc.vector.reduce_sum(place[:, :], reached[:, :, :], AX.X))
            step(nc.vector.tensor_scalar(place[:, :], place[:, :], float(E - 1), None, ALU.min))
            step(nc.vector.tensor_copy(tile_expert[:, :], place[:, :]))
            step(nc.vector.tensor_tensor(ends[:, :], ends[:, :], tiles[:, :], ALU.subtract))
            step(nc.vector.tensor_scalar(ends[:, :], ends[:, :], float(P), -1.0, ALU.mult, ALU.add))
            step(nc.vector.tensor_tensor(before[:, 0:B, :], before[:, 0:B, :], running[:, :, :], ALU.add))
            step(nc.vector.tensor_tensor(before[:, 0:B, :], before[:, 0:B, :],
                                         ends[:, None, :].to_broadcast([P, B, E]), ALU.add))
            step(nc.vector.tensor_tensor(before[:, 0:B, :], before[:, 0:B, :], mask[:, :, :], ALU.mult))
            step(nc.vector.reduce_sum(place[:, 0:B], before[:, 0:B, :], AX.X))
            step(nc.vector.tensor_copy(slot[:, :], place[:, 0:B]))

        def scalar(act):
            act.wait_ge(logits_ready, 1)
            nc.scalar.activation(values[:, :, 0:E], logits[:, :, :], ACT.Copy).then_inc(values_ready, 1)

        def tensor(pe):
            pe.wait_ge(mask_ready, 1)
            flat = mask[:, :, :].rearrange("p b e -> p (b e)")
            nc.tensor.matmul(running[:, :, :].rearrange("p b e -> p (b e)"), until[:, :], flat, start=True, stop=True)
            nc.tensor.matmul(count[:, :, :].rearrange("p b e -> p (b e)"), ones[:, :], flat,
                             start=True, stop=True).then_inc(counted, 1)

        return {"vector": vector, "scalar": scalar, "tensor": tensor}
    return finish


def finish_top1_capacity(until, ones, slot_base, spill, put, get, capacity):
    def finish(nc, ctx, tag, logits, bias, rw, logits_ready, bias_loaded):
        E = logits.shape[2]
        values, ex, top, left, mask, total, before, peak, place = small_tensors(
            nc, ctx, tag, values=[P, B, E + 7], ex=[P, B, E], top=[P, B, 8], left=[P, B, E + 7],
            mask=[P, B, E], total=[P, B, 2], before=[P, B, E], peak=[P, B, 1], place=[P, 3, B])
        running = ctx.enter_context(nc.psum_tensor(f"{tag}_running", [P, B, E], F32))
        count = ctx.enter_context(nc.psum_tensor(f"{tag}_count", [P, B, E], F32))
        chain = signal(nc, f"{tag}_chain")
        shifted = signal(nc, f"{tag}_shifted")
        exp_ready = signal(nc, f"{tag}_exp_ready")
        mask_ready = signal(nc, f"{tag}_mask_ready")
        counted = signal(nc, f"{tag}_counted")

        def vector(dve):
            step = stepper(dve, chain)
            step(nc.vector.memset(values[:, :, E:], BIG))
            step(nc.vector.memset(before[:, 0, :], 0.0))
            dve.wait_ge(logits_ready, 1)
            step(nc.vector.reduce_max(peak[:, :, 0], logits[:, :, :], AX.X))
            nc.vector.tensor_tensor(ex[:, :, :], logits[:, :, :], peak[:, :, :].to_broadcast([P, B, E]),
                                    ALU.subtract).then_inc(shifted, 1)
            dve.wait_ge(exp_ready, 1)
            step(nc.vector.reduce_sum(total[:, :, 0], values[:, :, 0:E], AX.X))
            step(nc.vector.reciprocal(total[:, :, 1], total[:, :, 0]))
            step(nc.vector.tensor_tensor(values[:, :, 0:E], values[:, :, 0:E],
                                         total[:, :, 1:2].to_broadcast([P, B, E]), ALU.mult))
            choose_top(nc, step, 1, values, E, top, left, mask[:, :, :])
            nc.vector.tensor_tensor(ex[:, :, :], values[:, :, 0:E], mask[:, :, :], ALU.mult).then_inc(mask_ready, 1)
            dve.wait_ge(counted, 1)
            for t in range(1, B):
                step(nc.vector.tensor_tensor(before[:, t, :], before[:, t - 1, :], count[:, t - 1, :], ALU.add))
            dve.wait_ge(mask_ready, 1)
            step(nc.vector.reduce_sum(total[:, :, 0], ex[:, :, :], AX.X))
            step(nc.vector.tensor_tensor(before[:, :, :], before[:, :, :], running[:, :, :], ALU.add))
            step(nc.vector.tensor_tensor(before[:, :, :], before[:, :, :], mask[:, :, :], ALU.mult))
            step(nc.vector.reduce_sum(place[:, 0, :], before[:, :, :], AX.X))
            step(nc.vector.tensor_tensor(ex[:, :, :], mask[:, :, :], slot_base[:, None, :].to_broadcast([P, B, E]),
                                         ALU.mult))
            step(nc.vector.reduce_sum(place[:, 1, :], ex[:, :, :], AX.X))
            step(nc.vector.tensor_tensor(place[:, 1, :], place[:, 1, :], place[:, 0, :], ALU.add))
            step(nc.vector.tensor_scalar(place[:, 0, :], place[:, 0, :], float(capacity), None, ALU.is_le))
            step(nc.vector.tensor_tensor(rw[:, :, 0], total[:, :, 0], place[:, 0, :], ALU.mult))
            step(nc.vector.tensor_tensor(place[:, 2, :], place[:, 1, :], spill[:, :], ALU.subtract))
            step(nc.vector.tensor_tensor(place[:, 2, :], place[:, 2, :], place[:, 0, :], ALU.mult))
            step(nc.vector.tensor_tensor(place[:, 2, :], place[:, 2, :], spill[:, :], ALU.add))
            step(nc.vector.tensor_copy(put[:, :], place[:, 2, :]))
            step(nc.vector.tensor_scalar(place[:, 1, :], place[:, 1, :], float(E * capacity - 1), None, ALU.min))
            step(nc.vector.tensor_copy(get[:, :], place[:, 1, :]))

        def scalar(act):
            act.wait_ge(shifted, 1)
            nc.scalar.activation(values[:, :, 0:E], ex[:, :, :], ACT.Exp).then_inc(exp_ready, 1)

        def tensor(pe):
            pe.wait_ge(mask_ready, 1)
            flat = mask[:, :, :].rearrange("p b e -> p (b e)")
            nc.tensor.matmul(running[:, :, :].rearrange("p b e -> p (b e)"), until[:, :], flat, start=True, stop=True)
            nc.tensor.matmul(count[:, :, :].rearrange("p b e -> p (b e)"), ones[:, :], flat,
                             start=True, stop=True).then_inc(counted, 1)

        return {"vector": vector, "scalar": scalar, "tensor": tensor}
    return finish


def ensemble_gate(nc, tag, rw, ctx_dram, itok_dram, ones, n_experts, repeat):
    E = n_experts
    with ExitStack() as ctx:
        weight = ctx.enter_context(nc.sbuf_tensor(f"{tag}_weight", [P, B, P], F32))
        index = ctx.enter_context(nc.sbuf_tensor(f"{tag}_index", [P, B, P], I32))
        index_f = ctx.enter_context(nc.sbuf_tensor(f"{tag}_index_f", [P, B, P], F32))
        picked = ctx.enter_context(nc.sbuf_tensor(f"{tag}_picked", [P, 2, B, P], F32))
        gate = ctx.enter_context(nc.psum_tensor(f"{tag}_gate", [P, E, B], F32))
        weight_loaded = signal(nc, f"{tag}_weight_loaded")
        index_loaded = signal(nc, f"{tag}_index_loaded")
        index_ready = signal(nc, f"{tag}_index_ready")
        picked_ready = signal(nc, f"{tag}_picked_ready")
        gate_ready = signal(nc, f"{tag}_gate_ready")
        with nc.Block() as block:
            @block.sync
            def _(sp):
                sp.dma_start(index[:, :, :], itok_dram.rearrange("b k s -> k b s")).then_inc(index_loaded, 16)
                sp.dma_start(weight[:, :, :], ctx_dram.rearrange("b k s -> k b s")).then_inc(weight_loaded, 16)

            @block.vector
            def _(dve):
                dve.wait_ge(index_loaded, 16)
                nc.vector.tensor_copy(index_f[:, :, :], index[:, :, :]).then_inc(index_ready, 1)
                dve.wait_ge(index_ready, 1)
                dve.wait_ge(weight_loaded, 16)
                for e in range(E):
                    if e >= 2:
                        dve.wait_ge(gate_ready, e - 1)
                    nc.vector.scalar_tensor_tensor(
                        picked[:, e % 2, :, :].rearrange("p b s -> p (b s)"),
                        index_f[:, :, :].rearrange("p b s -> p (b s)"), float(e),
                        weight[:, :, :].rearrange("p b s -> p (b s)"),
                        ALU.is_equal, ALU.mult).then_inc(picked_ready, 1)
                dve.wait_ge(gate_ready, E)
                for r in range(repeat):
                    nc.vector.tensor_copy(rw[:, :, r:E * repeat:repeat],
                                          gate[:, :, :].rearrange("p e b -> p b e"))

            @block.tensor
            def _(pe):
                for e in range(E):
                    pe.wait_ge(picked_ready, e + 1)
                    for b in range(B):
                        last = nc.tensor.matmul(gate[:, e, b:b + 1], picked[:, e % 2, b, :], ones[:, 0:1],
                                                start=True, stop=True)
                    last.then_inc(gate_ready, 1)


def experts(nc, tag, x, xnT, rw, w_dram, func, gated):
    E, _, C, WIDTH = w_dram.shape
    AB = (2 if gated else 1) * D
    STEPS = 2 * NG * C
    PAIRS = E // 2
    assert E % 2 == 0 and WIDTH == AB + D
    with ExitStack() as ctx:
        w = ctx.enter_context(nc.sbuf_tensor(f"{tag}_w", [P, 2, C, WIDTH], F32))
        acted = ctx.enter_context(nc.sbuf_tensor(f"{tag}_acted", [P, 2, GW], F32))
        hidden = ctx.enter_context(nc.sbuf_tensor(f"{tag}_hidden", [P, 2, GW], F32))
        gate = ctx.enter_context(nc.psum_tensor(f"{tag}_gate", [P, 2, GW], F32))
        up = ctx.enter_context(nc.psum_tensor(f"{tag}_up", [P, 2, GW], F32))
        out = ctx.enter_context(nc.psum_tensor(f"{tag}_out", [P, 2, GT, D], F32))
        w_loaded = [signal(nc, f"{tag}_w_loaded{s}") for s in range(2)]
        gate_ready = signal(nc, f"{tag}_gate_ready")
        up_ready = signal(nc, f"{tag}_up_ready")
        acted_ready = signal(nc, f"{tag}_acted_ready")
        hidden_ready = signal(nc, f"{tag}_hidden_ready")
        down_done = signal(nc, f"{tag}_down_done")
        combined = signal(nc, f"{tag}_combined")

        def step_of(s):
            return s // (NG * C), s // C % NG, s % C

        def pairs(engine, program):
            if PAIRS > 1:
                with engine.Fori(0, PAIRS - 1) as pair:
                    program(pair, False)
            program(PAIRS - 1, True)

        with nc.Block() as block:
            @block.sync
            def _(sp):
                for s in range(2):
                    sp.dma_start(w[:, s, :, :], w_dram[s, :, :, :]).then_inc(w_loaded[s], 16)
                with sp.Fori(1, PAIRS) as pair:
                    for s in range(2):
                        sp.wait_ge(down_done, STEPS * pair - (1 - s) * NG * C)
                        sp.dma_start(w[:, s, :, :],
                                     w_dram[bass.ds(2 * pair + s, 1), :, :, :].rearrange("a p c n -> p (a c) n")
                                     ).then_inc(w_loaded[s], 16)

            @block.tensor
            def _(pe):
                def gate_up(pair, s):
                    e, g, c = step_of(s % STEPS)
                    nth = STEPS * pair + s
                    if g == 0 and c == 0:
                        pe.wait_ge(w_loaded[e], 16 * (pair + s // STEPS) + 16)
                    if s > 0:
                        pe.wait_ge(hidden_ready, 2 + nth - 1)
                    for part, (bank, ready) in enumerate(((gate, gate_ready), (up, up_ready))[:AB // D]):
                        for k in range(KC):
                            at = part * D + k * P
                            last = nc.tensor.matmul(bank[:, s % 2, :], w[:, e, c, at:at + P],
                                                    xnT[:, k, g * GW:(g + 1) * GW], start=(k == 0), stop=(k == KC - 1))
                        last.then_inc(ready, 1)

                def down(pair, s):
                    e, g, c = step_of(s)
                    nth = STEPS * pair + s
                    turn = 2 * NG * pair + s // C
                    pe.wait_ge(hidden_ready, 2 + nth + 1)
                    if c == 0:
                        pe.wait_ge(combined, NG + turn - 1)
                    for j in range(GT):
                        last = nc.tensor.matmul(out[:, g % 2, j, :], hidden[:, s % 2, j * P:(j + 1) * P],
                                                w[:, e, c, AB:AB + D], start=(c == 0 and j % 2 == 0),
                                                stop=(c == C - 1), skip_group_check=True)
                    last.then_inc(down_done, 1)

                def program(pair, last):
                    for s in range(STEPS):
                        if not (last and s == STEPS - 1):
                            gate_up(pair, s + 1)
                        down(pair, s)

                gate_up(0, 0)
                pairs(pe, program)

            @block.scalar
            def _(act):
                def program(pair, last):
                    for s in range(STEPS):
                        nth = STEPS * pair + s
                        act.wait_ge(gate_ready, nth + 1)
                        if gated:
                            nc.scalar.activation(acted[:, s % 2, :], gate[:, s % 2, :], func).then_inc(acted_ready, 1)
                        else:
                            nc.scalar.activation(hidden[:, s % 2, :], gate[:, s % 2, :], func).then_inc(hidden_ready, 1)
                pairs(act, program)

            @block.vector
            def _(dve):
                def multiply(pair, s):
                    if not gated:
                        return
                    nth = STEPS * pair + s
                    dve.wait_ge(acted_ready, nth + 1)
                    dve.wait_ge(up_ready, nth + 1)
                    nc.vector.tensor_tensor(hidden[:, s % 2, :], acted[:, s % 2, :], up[:, s % 2, :],
                                            ALU.mult).then_inc(hidden_ready, 1)

                def combine(pair, s):
                    e, g, _ = step_of(s)
                    turn = 2 * NG * pair + s // C
                    dve.wait_ge(down_done, STEPS * pair + s + 1)
                    dve.wait_ge(combined, turn + 1)
                    for j in range(GT):
                        t = g * GT + j
                        expert = 2 * pair + e
                        weight = rw[:, t, expert:expert + 1] if isinstance(pair, int) else \
                            rw[:, t, bass.ds(expert, 1)]
                        last = nc.vector.scalar_tensor_tensor(x[:, t, :], out[:, g % 2, j, :], weight, x[:, t, :],
                                                              ALU.mult, ALU.add)
                    last.then_inc(combined, 1)

                def program(pair, last):
                    for s in range(STEPS):
                        if not (last and s == STEPS - 1):
                            multiply(pair, s + 1)
                        if s % C == C - 1:
                            combine(pair, s)

                dve.sem_inc(combined, NG)
                dve.sem_inc(hidden_ready, 2)
                multiply(0, 0)
                pairs(dve, program)


def capacity_experts(nc, tag, x, xn, gate_of, put, get, ident, w_dram, slots_dram, y_dram, cleared, S):
    E, _, C, WIDTH = w_dram.shape
    ROWS = E * S
    TILES = ROWS // P
    RING = 4
    AB = 2 * D
    ROUNDS = E // RING
    assert ROWS % (GT * P) == 0 and E % RING == 0
    with ExitStack() as ctx:
        w = ctx.enter_context(nc.sbuf_tensor(f"{tag}_w", [P, RING, C, WIDTH], F32))
        rows = ctx.enter_context(nc.sbuf_tensor(f"{tag}_rows", [P, TILES, D], F32))
        rowsT = ctx.enter_context(nc.sbuf_tensor(f"{tag}_rowsT", [P, KC, ROWS], F32))
        acted = ctx.enter_context(nc.sbuf_tensor(f"{tag}_acted", [P, 2, C * S], F32))
        hidden = ctx.enter_context(nc.sbuf_tensor(f"{tag}_hidden", [P, 2, C, S], F32))
        y = ctx.enter_context(nc.sbuf_tensor(f"{tag}_y", [S, RING, D], F32))
        back = ctx.enter_context(nc.sbuf_tensor(f"{tag}_back", [P, B, D], F32))
        gate = ctx.enter_context(nc.psum_tensor(f"{tag}_gate", [P, 2, 512], F32))
        up = ctx.enter_context(nc.psum_tensor(f"{tag}_up", [P, 2, 512], F32))
        out = ctx.enter_context(nc.psum_tensor(f"{tag}_out", [P, 2, 512], F32))
        turned = ctx.enter_context(nc.psum_tensor(f"{tag}_turned", [P, 2, GW], F32))
        scattered, rows_loaded = signal(nc, f"{tag}_scattered"), signal(nc, f"{tag}_rows_loaded")
        w_loaded = [signal(nc, f"{tag}_w_loaded{r}") for r in range(RING)]
        turned_ready, rowsT_written = signal(nc, f"{tag}_turned_ready"), signal(nc, f"{tag}_rowsT_written")
        gate_ready, up_ready = signal(nc, f"{tag}_gate_ready"), signal(nc, f"{tag}_up_ready")
        acted_ready, hidden_ready = signal(nc, f"{tag}_acted_ready"), signal(nc, f"{tag}_hidden_ready")
        down_done, y_ready = signal(nc, f"{tag}_down_done"), signal(nc, f"{tag}_y_ready")
        y_stored = [signal(nc, f"{tag}_y_stored{r}") for r in range(RING)]
        gathered, x_summed = signal(nc, f"{tag}_gathered"), signal(nc, f"{tag}_x_summed")

        def rounds(engine, program):
            with engine.Fori(0, ROUNDS - 1) as n:
                program(n, False)
            program(ROUNDS - 1, True)

        with nc.Block() as block:
            @block.gpsimd
            def _(pool):
                pool.wait_ge(cleared, 16)
                for t in range(B):
                    nc.gpsimd.indirect_dma_start(
                        out=slots_dram, out_offset=bass.IndirectOffsetOnAxis(ap=put[:, t:t + 1], axis=0),
                        in_=xn[:, t, :], in_offset=None).then_inc(scattered, 16)
                nc.gpsimd.tensor_tensor(x[:, :, :], x[:, :, :], xn[:, :, :], ALU.add).then_inc(x_summed, 1)
                for r in range(RING):
                    pool.wait_ge(y_stored[r], 16 * (ROUNDS + 1))
                for t in range(B):
                    nc.gpsimd.indirect_dma_start(
                        out=back[:, t, :], out_offset=None, in_=y_dram,
                        in_offset=bass.IndirectOffsetOnAxis(ap=get[:, t:t + 1], axis=0)).then_inc(gathered, 16)

            @block.sync
            def _(sp):
                for r in range(RING):
                    sp.dma_start(w[:, r, :, :], w_dram[r, :, :, :]).then_inc(w_loaded[r], 16)
                sp.wait_ge(scattered, 16 * B)
                sp.dma_start(rows[:, :, :], slots_dram[0:ROWS, :].rearrange("(t p) d -> p t d", p=P)
                             ).then_inc(rows_loaded, 16)
                with sp.Fori(1, ROUNDS) as n:
                    for r in range(RING):
                        sp.wait_ge(down_done, RING * (n - 1) + r + 1)
                        sp.dma_start(w[:, r, :, :],
                                     w_dram[bass.ds(RING * n + r, 1), :, :, :].rearrange("a p c n -> p (a c) n")
                                     ).then_inc(w_loaded[r], 16)

            @block.tensor
            def _(pe):
                pe.wait_ge(rows_loaded, 16)
                for n in range(TILES // GT * KC):
                    g, k = n // KC, n % KC
                    if n >= 2:
                        pe.wait_ge(rowsT_written, n - 1)
                    for j in range(GT):
                        last = nc.tensor.transpose(turned[:, n % 2, j * P:(j + 1) * P],
                                                   rows[:, g * GT + j, k * P:(k + 1) * P], ident[:, :])
                    last.then_inc(turned_ready, 1)
                pe.wait_ge(rowsT_written, TILES // GT * KC)

                def gate_up(n, r):
                    nth = RING * n + r
                    pe.wait_ge(w_loaded[r % RING], 16 * (n + r // RING) + 16)
                    pe.wait_ge(hidden_ready, 2 + nth - 1)
                    for part, (bank, ready) in enumerate(((gate, gate_ready), (up, up_ready))):
                        for c in range(C):
                            for k in range(KC):
                                at = part * D + k * P
                                last = nc.tensor.matmul(bank[:, r % 2, c * S:(c + 1) * S], w[:, r % RING, c, at:at + P],
                                                        rowsT[:, k, bass.ds(nth * S, S)],
                                                        start=(k == 0), stop=(k == KC - 1))
                        last.then_inc(ready, 1)

                def down(n, r):
                    nth = RING * n + r
                    pe.wait_ge(hidden_ready, 2 + nth + 1)
                    pe.wait_ge(y_ready, 2 + nth - 1)
                    for c in range(C):
                        last = nc.tensor.matmul(out[0:S, r % 2, 0:D], hidden[:, r % 2, c, :],
                                                w[:, r, c, AB:AB + D], start=(c == 0), stop=(c == C - 1))
                    last.then_inc(down_done, 1)

                def program(n, last):
                    for r in range(RING):
                        if not (last and r == RING - 1):
                            gate_up(n, r + 1)
                        down(n, r)
                gate_up(0, 0)
                rounds(pe, program)

            @block.scalar
            def _(act):
                for n in range(TILES // GT * KC):
                    g, k = n // KC, n % KC
                    act.wait_ge(turned_ready, n + 1)
                    nc.scalar.activation(rowsT[:, k, g * GW:(g + 1) * GW], turned[:, n % 2, :],
                                         ACT.Copy).then_inc(rowsT_written, 1)

                def activate(n, r):
                    act.wait_ge(gate_ready, RING * n + r + 1)
                    nc.scalar.activation(acted[:, r % 2, :], gate[:, r % 2, 0:C * S], ACT.Silu).then_inc(acted_ready, 1)

                def store(n, r):
                    act.wait_ge(y_ready, 2 + RING * n + r + 1)
                    act.dma_start(y_dram[bass.ds((RING * n + r) * S, S), :], y[:, r, :]).then_inc(y_stored[r], 16)

                def program(n, last):
                    for r in range(RING):
                        if not (last and r == RING - 1):
                            activate(n, r + 1)
                        store(n, r)
                activate(0, 0)
                rounds(act, program)

            @block.vector
            def _(dve):
                def multiply(n, r):
                    dve.wait_ge(acted_ready, RING * n + r + 1)
                    dve.wait_ge(up_ready, RING * n + r + 1)
                    nc.vector.tensor_tensor(hidden[:, r % 2, :, :].rearrange("p c n -> p (c n)"), acted[:, r % 2, :],
                                            up[:, r % 2, 0:C * S], ALU.mult).then_inc(hidden_ready, 1)

                def copy_out(n, r):
                    dve.wait_ge(down_done, RING * n + r + 1)
                    dve.wait_ge(y_stored[r], 16 * n + 16)
                    nc.vector.tensor_copy(y[:, r, :], out[0:S, r % 2, 0:D]).then_inc(y_ready, 1)

                def program(n, last):
                    for r in range(RING):
                        if not (last and r == RING - 1):
                            multiply(n, r + 1)
                        copy_out(n, r)
                dve.sem_inc(hidden_ready, 2)
                dve.sem_inc(y_ready, 2)
                for r in range(RING):
                    dve.sem_inc(y_stored[r], 16)
                multiply(0, 0)
                rounds(dve, program)
                dve.wait_ge(x_summed, 1)
                dve.wait_ge(gathered, 16 * B)
                for t in range(B):
                    nc.vector.scalar_tensor_tensor(x[:, t, :], back[:, t, :], gate_of[:, t, 0:1], x[:, t, :],
                                                   ALU.mult, ALU.add)


def sorted_experts(nc, tag, x, xn, slot, tile_expert, ident, w_dram, rows_dram, y_dram, cleared):
    PASSES, _, E, WIDTH = w_dram.shape
    H = WIDTH // (2 * KC + KC)
    HC = H // P
    NT = SORTED_TILES
    AB = KC * 2 * H
    assert WIDTH == AB + HC * D and NT % GT == 0 and 2 * H == 512
    with ExitStack() as ctx:
        w = ctx.enter_context(nc.sbuf_tensor(f"{tag}_w", [P, 2, E, WIDTH], F32))
        rows = ctx.enter_context(nc.sbuf_tensor(f"{tag}_rows", [P, NT, D], F32))
        rowsT = ctx.enter_context(nc.sbuf_tensor(f"{tag}_rowsT", [P, KC, NT * P], F32))
        back = rowsT[:, :, :].rearrange("p k n -> p (k n)")[:, 0:B * D].rearrange("p (b d) -> p b d", d=D)
        acted = ctx.enter_context(nc.sbuf_tensor(f"{tag}_acted", [P, 2, H], F32))
        hidden = ctx.enter_context(nc.sbuf_tensor(f"{tag}_hidden", [P, 2, H], F32))
        hiddenT = ctx.enter_context(nc.sbuf_tensor(f"{tag}_hiddenT", [P, 2, HC, P], F32))
        gate_up = ctx.enter_context(nc.psum_tensor(f"{tag}_gate_up", [P, 2, 512], F32))
        turned = ctx.enter_context(nc.psum_tensor(f"{tag}_turned", [P, 2, 512], F32))
        out = ctx.enter_context(nc.psum_tensor(f"{tag}_out", [P, 2, 512], F32))
        scattered, rows_loaded = signal(nc, f"{tag}_scattered"), signal(nc, f"{tag}_rows_loaded")
        w_loaded = [signal(nc, f"{tag}_w_loaded{r}") for r in range(2)]
        rows_turned, rowsT_written = signal(nc, f"{tag}_rows_turned"), signal(nc, f"{tag}_rowsT_written")
        rows_zeroed = signal(nc, f"{tag}_rows_zeroed")
        products_ready, acted_ready = signal(nc, f"{tag}_products_ready"), signal(nc, f"{tag}_acted_ready")
        hidden_ready, turned_ready = signal(nc, f"{tag}_hidden_ready"), signal(nc, f"{tag}_turned_ready")
        hiddenT_ready, down_done = signal(nc, f"{tag}_hiddenT_ready"), signal(nc, f"{tag}_down_done")
        added, y_stored, gathered = signal(nc, f"{tag}_added"), signal(nc, f"{tag}_y_stored"), signal(nc, f"{tag}_gathered")

        with nc.Block() as block:
            @block.gpsimd
            def _(pool):
                pool.wait_ge(cleared, 16)
                for t in range(B):
                    nc.gpsimd.indirect_dma_start(
                        out=rows_dram, out_offset=bass.IndirectOffsetOnAxis(ap=slot[:, t:t + 1], axis=0),
                        in_=xn[:, t, :], in_offset=None).then_inc(scattered, 16)
                pool.wait_ge(y_stored, 16)
                for t in range(B):
                    nc.gpsimd.indirect_dma_start(
                        out=back[:, t, :], out_offset=None, in_=y_dram,
                        in_offset=bass.IndirectOffsetOnAxis(ap=slot[:, t:t + 1], axis=0)).then_inc(gathered, 16)

            @block.sync
            def _(sp):
                sp.dma_start(w[:, 0, :, :], w_dram[0, :, :, :]).then_inc(w_loaded[0], 16)
                sp.wait_ge(scattered, 16 * B)
                sp.dma_start(rows[:, :, :], rows_dram.rearrange("(t p) d -> p t d", p=P)).then_inc(rows_loaded, 16)
                sp.dma_start(w[:, 1, :, :], w_dram[1, :, :, :]).then_inc(w_loaded[1], 16)
                for q in range(2, PASSES):
                    sp.wait_ge(down_done, NT * (q - 1))
                    sp.dma_start(w[:, q % 2, :, :], w_dram[q, :, :, :]).then_inc(w_loaded[q % 2], 16)
                sp.wait_ge(added, NT + NT * PASSES)
                sp.dma_start(y_dram.rearrange("(t p) d -> p t d", p=P), rows[:, :, :]).then_inc(y_stored, 16)
                sp.wait_ge(y_stored, 16)

            @block.tensor
            def _(pe):
                pe.wait_ge(rows_loaded, 16)
                for n in range(NT // GT * KC):
                    g, k = n // KC, n % KC
                    if n >= 2:
                        pe.wait_ge(rowsT_written, n - 1)
                    for j in range(GT):
                        last = nc.tensor.transpose(gate_up[:, n % 2, j * P:(j + 1) * P],
                                                   rows[:, g * GT + j, k * P:(k + 1) * P], ident[:, :])
                    last.then_inc(rows_turned, 1)
                pe.wait_ge(rowsT_written, NT // GT * KC)

                def one_pass(q, parity):
                    for s in range(NT + 2):
                        nth = NT * (2 * q + parity) + s
                        if s < NT:
                            expert = pe.value_load(tile_expert[0:1, s:s + 1], min_val=0, max_val=E - 1)
                            owner_of[s % 3] = expert
                            if s == 0:
                                pe.wait_ge(w_loaded[parity], 16 * q + 16)
                            pe.wait_ge(hidden_ready, 2 + nth - 1)
                            for k in range(KC):
                                last = nc.tensor.matmul(gate_up[:, s % 2, :], rowsT[:, k, s * P:(s + 1) * P],
                                                        w[:, parity, bass.ds(expert, 1), k * 2 * H:(k + 1) * 2 * H],
                                                        start=(k == 0), stop=(k == KC - 1))
                            last.then_inc(products_ready, 1)
                        if 1 <= s <= NT:
                            pe.wait_ge(hidden_ready, 2 + nth)
                            for c in range(HC):
                                last = nc.tensor.transpose(turned[:, (s - 1) % 2, c * P:(c + 1) * P],
                                                           hidden[:, (s - 1) % 2, c * P:(c + 1) * P], ident[:, :])
                            last.then_inc(turned_ready, 1)
                        if s >= 2:
                            pe.wait_ge(hiddenT_ready, nth - 1)
                            pe.wait_ge(added, NT + nth - 3)
                            for c in range(HC):
                                last = nc.tensor.matmul(out[:, s % 2, 0:D], hiddenT[:, s % 2, c, :],
                                                        w[:, parity, bass.ds(owner_of[(s - 2) % 3], 1),
                                                          AB + c * D:AB + (c + 1) * D],
                                                        start=(c == 0), stop=(c == HC - 1))
                            last.then_inc(down_done, 1)
                owner_of = [None] * 3
                with pe.Fori(0, PASSES // 2) as q:
                    for parity in range(2):
                        one_pass(q, parity)

            @block.scalar
            def _(act):
                for n in range(NT // GT * KC):
                    g, k = n // KC, n % KC
                    act.wait_ge(rows_turned, n + 1)
                    nc.scalar.activation(rowsT[:, k, g * GW:(g + 1) * GW], gate_up[:, n % 2, :],
                                         ACT.Copy).then_inc(rowsT_written, 1)
                with act.Fori(0, PASSES) as q:
                    for s in range(NT + 1):
                        if s < NT:
                            act.wait_ge(products_ready, NT * q + s + 1)
                            nc.scalar.activation(acted[:, s % 2, :], gate_up[:, s % 2, 0:H],
                                                 ACT.Gelu).then_inc(acted_ready, 1)
                        if s >= 1:
                            act.wait_ge(turned_ready, NT * q + s)
                            nc.scalar.activation(hiddenT[:, (s - 1) % 2, :, :].rearrange("p c n -> p (c n)"),
                                                 turned[:, (s - 1) % 2, 0:H], ACT.Copy).then_inc(hiddenT_ready, 1)

            @block.vector
            def _(dve):
                dve.wait_ge(rowsT_written, NT // GT * KC)
                nc.vector.memset(rows[:, :, :], 0.0).then_inc(rows_zeroed, 1)
                dve.wait_ge(rows_zeroed, 1)
                dve.sem_inc(hidden_ready, 2)
                dve.sem_inc(added, NT)
                with dve.Fori(0, PASSES) as q:
                    for s in range(NT + 2):
                        nth = NT * q + s
                        if s < NT:
                            dve.wait_ge(acted_ready, nth + 1)
                            nc.vector.tensor_tensor(hidden[:, s % 2, :], acted[:, s % 2, :], gate_up[:, s % 2, H:2 * H],
                                                    ALU.mult).then_inc(hidden_ready, 1)
                        if s >= 2:
                            dve.wait_ge(down_done, nth - 1)
                            dve.wait_ge(added, nth - 1)
                            nc.vector.tensor_tensor(rows[:, s - 2, :], rows[:, s - 2, :], out[:, s % 2, 0:D],
                                                    ALU.add).then_inc(added, 1)
                for t in range(B):
                    dve.wait_ge(gathered, 16 * B)
                    nc.vector.tensor_tensor(x[:, t, :], x[:, t, :], back[:, t, :], ALU.add)


def attention(nc, tag, x, xnT, ctxT_dram, ident, wq_dram, wk_dram, wv_dram, heads, padded, head_dim, scale,
              wo_dram=None, bq_dram=None, bk_dram=None, bv_dram=None, bo_dram=None):
    CQ = wq_dram.shape[1] // P
    V = wv_dram.shape[1]
    ROWS = min(padded, P)
    RT = P // ROWS
    HC = padded // ROWS
    GH = min(heads, RT * 4)
    GROUPS = heads // GH
    QUAD = min(4, heads)
    QUADS = heads // QUAD
    QC = min(CQ, 4)
    VW = min(V, 512)
    CO = V // P
    OC = min(CO, 4)
    PROJ = [("q", i) for i in range(CQ // QC)] + [("k", i) for i in range(CQ // QC)] + [("v", i) for i in range(V // VW)]
    TURN = [("p", i) for i in range(QUADS)]
    LAST = ([("o", i) for i in range(CO // OC)] + [("y", 0)]) if wo_dram is not None else []
    USES = len(PROJ) + len(TURN) + len(LAST)

    def use_of(pair, b, kind, i, final=False):
        if (kind, i) in PROJ:
            if isinstance(pair, int) and pair == 0 and b == 0:
                at, pair = PROJ.index((kind, i)), 0
            else:
                at = len(PROJ) + USES * (b - 1) + PROJ.index((kind, i))
        else:
            at = (0 if final else len(PROJ)) + len(PROJ) + USES * b + (TURN + LAST).index((kind, i))
        return at % 2, USES * pair + at // 2, 2 * USES * pair + at

    def place(h):
        r = h % RT
        return h // GH, r, (h % GH) // RT, r * ROWS, h // RT * HC

    with ExitStack() as ctx:
        def sb(name, shape):
            return ctx.enter_context(nc.sbuf_tensor(f"{tag}_{name}", shape, F32))

        def sem(name):
            return signal(nc, f"{tag}_{name}")
        wq, wk, wv = sb("wq", [P, KC, CQ * P]), sb("wk", [P, CQ * P]), sb("wv", [P, V])
        wo = sb("wo", [P, CO, D]) if wo_dram is not None else None
        bq = sb("bq", [P, CQ]) if bq_dram is not None else None
        bk = sb("bk", [P, CQ]) if bk_dram is not None else None
        bv = sb("bv", [P, V]) if bv_dram is not None else None
        bo = sb("bo", [P, D]) if bo_dram is not None else None
        keys = sb("keys", [P, 2, P])
        q, k, v = sb("q", [P, 2, CQ, P]), sb("k", [P, 2, CQ, P]), sb("v", [P, 2, V])
        probs = sb("probs", [P, heads, P])
        probsT = sb("probsT", [P, 2, QUAD, P])
        peak, bias = sb("peak", [P, GROUPS, RT, GH // RT]), sb("bias", [P, GROUPS, RT, GH // RT])
        total, inverse = sb("total", [P, heads]), sb("inverse", [P, heads])
        o, oT = sb("o", [P, V]), sb("oT", [P, CO, P])
        work = ctx.enter_context(nc.psum_tensor(f"{tag}_work", [P, 2, 512], F32))
        scores = ctx.enter_context(nc.psum_tensor(f"{tag}_scores", [P, 4, 512], F32))
        o_sum = ctx.enter_context(nc.psum_tensor(f"{tag}_o_sum", [P, 2, 512], F32))
        weights_loaded, keys_loaded = sem("weights_loaded"), [sem("keys_loaded0"), sem("keys_loaded1")]
        work_ready, work_free = sem("work_ready"), [sem("work_free0"), sem("work_free1")]
        qkv_ready, scores_ready, bias_ready, exp_done = sem("qkv_ready"), sem("scores_ready"), sem("bias_ready"), sem("exp_done")
        o_summed, o_ready, chain, x_ready = sem("o_summed"), sem("o_ready"), sem("chain"), sem("x_ready")
        n_weights = 3 + sum(m is not None for m in (wo, bq, bk, bv, bo))

        def batches(engine, program):
            with engine.Fori(0, B // 2 - 1) as pair:
                for b in range(2):
                    program(pair, b, False)
            for b in range(2):
                program(B // 2 - 1, b, b == 1)

        def next_of(pair, b):
            return (pair, 1) if b == 0 else (pair + 1, 0)

        with nc.Block() as block:
            @block.sync
            def _(sp):
                def load(dst, src):
                    sp.dma_start(dst, src).then_inc(weights_loaded, 16)
                load(wq[:, :, :], wq_dram.rearrange("(k p) n -> p k n", p=P))
                load(wk[:, :], wk_dram)
                load(wv[:, :], wv_dram)
                for b in range(2):
                    sp.dma_start(keys[:, b, :], ctxT_dram[b, :, :]).then_inc(keys_loaded[b], 16)
                if wo is not None:
                    load(wo[:, :, :], wo_dram.rearrange("(c p) n -> p c n", p=P))
                if bq is not None:
                    load(bq[:, :], bq_dram)
                    load(bk[:, :], bk_dram)
                    load(bv[:, :], bv_dram[None, :].to_broadcast([P, V]))
                if bo is not None:
                    load(bo[:, :], bo_dram[None, :].to_broadcast([P, D]))
                with sp.Fori(1, B // 2) as pair:
                    for b in range(2):
                        sp.wait_ge(qkv_ready, 2 * pair - 1 + b)
                        sp.dma_start(keys[:, b, :], ctxT_dram[bass.ds(2 * pair + b, 1), :, :].rearrange("a d m -> d (a m)")
                                     ).then_inc(keys_loaded[b], 16)

            @block.tensor
            def _(pe):
                def take(pair, b, kind, i, final=False):
                    slot, before, _ = use_of(pair, b, kind, i, final)
                    if not isinstance(before, int) or before > 0:
                        pe.wait_ge(work_free[slot], before)
                    return slot

                def read_out(pair, b, kind, i, final=False):
                    slot, before, _ = use_of(pair, b, kind, i, final)
                    pe.wait_ge(work_free[slot], before + 1)

                def project(pair, b):
                    for kind, i in PROJ:
                        slot = take(pair, b, kind, i)
                        if (kind, i) == ("k", 0):
                            pe.wait_ge(keys_loaded[b], 16 * pair + 16)
                        if kind == "q":
                            for j in range(QC):
                                at = (i * QC + j) * P
                                for c in range(KC):
                                    last = nc.tensor.matmul(work[:, slot, j * P:(j + 1) * P], wq[:, c, at:at + P],
                                                            xnT[:, c, bass.ts(2 * pair + b, P)],
                                                            start=(c == 0), stop=(c == KC - 1))
                        elif kind == "k":
                            for j in range(QC):
                                at = (i * QC + j) * P
                                last = nc.tensor.matmul(work[:, slot, j * P:(j + 1) * P], wk[:, at:at + P],
                                                        keys[:, b, :], start=True, stop=True)
                        else:
                            last = nc.tensor.matmul(work[:, slot, 0:VW], keys[:, b, :], wv[:, i * VW:(i + 1) * VW],
                                                    start=True, stop=True)
                        last.then_inc(work_ready, 1)

                def score(pair, b, g):
                    if g == 0:
                        pe.wait_ge(qkv_ready, 2 * pair + b + 1)
                    n = GROUPS * (2 * pair + b) + g
                    for h in range(g * GH, (g + 1) * GH):
                        _, r, col, row, chunk = place(h)
                        bank = (g * RT + r) % 4
                        for c in range(HC):
                            last = nc.tensor.matmul(scores[:, bank, col * P:(col + 1) * P],
                                                    q[row:row + ROWS, b, chunk + c, :], k[row:row + ROWS, b, chunk + c, :],
                                                    start=(c == 0), stop=(c == HC - 1))
                    last.then_inc(scores_ready, 1)

                def turn(pair, b, i, final):
                    slot = take(pair, b, "p", i, final)
                    pe.wait_ge(exp_done, heads * (2 * pair + b) + QUAD * (i + 1))
                    for j in range(QUAD):
                        last = nc.tensor.transpose(work[:, slot, j * P:(j + 1) * P], probs[:, i * QUAD + j, :],
                                                   ident[:, :])
                    last.then_inc(work_ready, 1)

                def weigh(pair, b, i, final):
                    read_out(pair, b, "p", i, final)
                    if i == 0:
                        pe.wait_ge(o_ready, 2 * pair + b + 1)
                    for j in range(QUAD):
                        h = i * QUAD + j
                        at = h * (V // heads)
                        last = nc.tensor.matmul(o_sum[:, at // 512, at % 512:at % 512 + V // heads], probsT[:, i % 2, j, :],
                                                v[:, b, at:at + V // heads], start=True, stop=True)
                    if i == QUADS - 1:
                        last.then_inc(o_summed, 1)

                def project_out(pair, b, final):
                    pe.wait_ge(o_ready, 2 * pair + b + 2)
                    for kind, i in LAST[:-1]:
                        slot = take(pair, b, kind, i, final)
                        for j in range(OC):
                            c = i * OC + j
                            last = nc.tensor.transpose(work[:, slot, j * P:(j + 1) * P], o[:, c * P:(c + 1) * P],
                                                       ident[:, :])
                        last.then_inc(work_ready, 1)
                    slot = take(pair, b, "y", 0, final)
                    for kind, i in LAST[:-1]:
                        read_out(pair, b, kind, i, final)
                    for c in range(CO):
                        last = nc.tensor.matmul(work[:, slot, 0:D], oT[:, c, :], wo[:, c, :],
                                                start=(c == 0), stop=(c == CO - 1))
                    last.then_inc(work_ready, 1)

                def program(pair, b, final):
                    for g in range(GROUPS):
                        score(pair, b, g)
                    if not final:
                        project(*next_of(pair, b))
                    for i in range(QUADS):
                        turn(pair, b, i, final)
                        if i > 0:
                            weigh(pair, b, i - 1, final)
                    weigh(pair, b, QUADS - 1, final)
                    if wo is not None:
                        project_out(pair, b, final)

                pe.wait_ge(weights_loaded, 16 * n_weights)
                project(0, 0)
                batches(pe, program)

            @block.scalar
            def _(act):
                def copy_out(pair, b, kind, i, dst, width, final=False):
                    slot, _, before = use_of(pair, b, kind, i, final)
                    act.wait_ge(work_ready, before + 1)
                    nc.scalar.activation(dst, work[:, slot, 0:width], ACT.Copy).then_inc(work_free[slot], 1)

                def exps(pair, b, i):
                    for h in range(i * QUAD, (i + 1) * QUAD):
                        g, r, col, _, _ = place(h)
                        if h % GH == 0:
                            act.wait_ge(bias_ready, GROUPS * (2 * pair + b) + g + 1)
                        nc.scalar.activation(probs[:, h, :], scores[:, (g * RT + r) % 4, col * P:(col + 1) * P], ACT.Exp,
                                             bias=bias[:, g, r, col:col + 1], scale=scale,
                                             accum_out=total[:, h:h + 1]).then_inc(exp_done, 1)

                def program(pair, b, final):
                    for i in range(QUADS + 1):
                        if i < QUADS:
                            exps(pair, b, i)
                        if i > 0:
                            copy_out(pair, b, "p", i - 1, probsT[:, (i - 1) % 2, :, :].rearrange("p a n -> p (a n)"),
                                     QUAD * P, final)
                    for kind, i in LAST[:-1]:
                        copy_out(pair, b, kind, i, oT[:, i * OC:(i + 1) * OC, :].rearrange("p a n -> p (a n)"),
                                 OC * P, final)

                batches(act, program)

            @block.vector
            def _(dve):
                def largest(pair, b, g):
                    dve.wait_ge(scores_ready, GROUPS * (2 * pair + b) + g + 1)
                    bank = g * RT % 4
                    nc.vector.reduce_max(
                        peak[:, g, :, :],
                        scores[:, bank:bank + RT, 0:GH // RT * P].rearrange("p r (c n) -> p r c n", n=P),
                        AX.X).then_inc(chain, 1)
                    dve.wait_ge(chain, (GROUPS + 1) * (2 * pair + b) + g + 1)
                    nc.vector.tensor_scalar(bias[:, g, :, :], peak[:, g, :, :], -scale, None,
                                            ALU.mult).then_inc(bias_ready, 1)

                def projected(pair, b):
                    for kind, i in PROJ:
                        slot, _, before = use_of(pair, b, kind, i)
                        dve.wait_ge(work_ready, before + 1)
                        if kind == "v":
                            dst, src = v[:, b, i * VW:(i + 1) * VW], work[:, slot, 0:VW]
                            add = bv[:, i * VW:(i + 1) * VW] if bv is not None else None
                        else:
                            dst = (q if kind == "q" else k)[:, b, i * QC:(i + 1) * QC, :]
                            src = work[:, slot, 0:QC * P].rearrange("p (a n) -> p a n", n=P)
                            rows = bq if kind == "q" else bk
                            add = rows[:, i * QC:(i + 1) * QC, None].to_broadcast([P, QC, P]) if bq is not None else None
                        if add is not None:
                            last = nc.vector.tensor_tensor(dst, src, add, ALU.add)
                        else:
                            last = nc.vector.tensor_copy(dst, src)
                        last.then_inc(work_free[slot], 1)
                    nc.vector.tensor_copy(peak[:, 0, 0, 0:1], peak[:, 0, 0, 0:1]).then_inc(qkv_ready, 1)

                def program(pair, b, final):
                    for g in range(GROUPS):
                        largest(pair, b, g)
                    if not final:
                        projected(*next_of(pair, b))
                    dve.wait_ge(exp_done, heads * (2 * pair + b + 1))
                    nc.vector.reciprocal(inverse[:, :], total[:, :]).then_inc(chain, 1)
                    dve.wait_ge(chain, (GROUPS + 1) * (2 * pair + b + 1))
                    dve.wait_ge(o_summed, 2 * pair + b + 1)
                    tile = x[:, bass.ds(2 * pair + b, 1), :].rearrange("p a d -> p (a d)") \
                        if not isinstance(pair, int) else x[:, 2 * pair + b, :]
                    if wo is None:
                        nc.vector.scalar_tensor_tensor(tile, o_sum[:, 0, 0:V], inverse[:, 0:1], tile,
                                                       ALU.mult, ALU.add).then_inc(o_ready, 1)
                        return
                    banks = max(1, V // 512)
                    sums = o_sum[:, 0:banks, 0:V // banks].rearrange("p a (h n) -> p (a h) n", n=V // heads) \
                        if banks == 1 else o_sum[:, :, :].rearrange("p a (h n) -> p (a h) n", n=V // heads)
                    nc.vector.tensor_tensor(o[:, :].rearrange("p (h n) -> p h n", n=V // heads), sums,
                                            inverse[:, :, None].to_broadcast([P, heads, V // heads]),
                                            ALU.mult).then_inc(o_ready, 1)
                    slot, _, before = use_of(pair, b, "y", 0, final)
                    dve.wait_ge(work_ready, before + 1)
                    nc.vector.tensor_tensor(tile, tile, work[:, slot, 0:D], ALU.add).then_inc(work_free[slot], 1)

                dve.sem_inc(o_ready, 1)
                dve.wait_ge(weights_loaded, 16 * n_weights)
                if bo is not None:
                    nc.vector.tensor_tensor(x[:, :, :], x[:, :, :], bo[:, None, :].to_broadcast([P, B, D]),
                                            ALU.add).then_inc(x_ready, 1)
                    dve.wait_ge(x_ready, 1)
                nc.vector.memset(peak[:, :, :, :], 0.0)
                projected(0, 0)
                batches(dve, program)


def build(nc, t, out, stages=range(8)):
    with ExitStack() as ctx:
        x = ctx.enter_context(nc.sbuf_tensor("x", [P, B, D], F32))
        xn = ctx.enter_context(nc.sbuf_tensor("xn", [P, B, D], F32))
        xnT = ctx.enter_context(nc.sbuf_tensor("xnT", [P, KC, T], F32))
        ident = ctx.enter_context(nc.sbuf_tensor("ident", [P, P], F32))
        ones = ctx.enter_context(nc.sbuf_tensor("ones", [P, P], F32))
        until = ctx.enter_context(nc.sbuf_tensor("until", [P, P], F32))
        LIVE.clear()
        zeros = ctx.enter_context(nc.sbuf_tensor("zeros", [P, D], F32))
        slot_base = ctx.enter_context(nc.sbuf_tensor("slot_base", [P, 32], F32))
        spill = ctx.enter_context(nc.sbuf_tensor("spill", [P, B], F32))
        put = ctx.enter_context(nc.sbuf_tensor("put", [P, B], I32))
        get = ctx.enter_context(nc.sbuf_tensor("get", [P, B], I32))
        slots_dram = nc.dram_tensor("slots", (32 * CAPACITY + T, D), F32).ap()
        y_dram = nc.dram_tensor("expert_rows", (32 * CAPACITY, D), F32).ap()
        steps = ctx.enter_context(nc.sbuf_tensor("steps", [P, SORTED_TILES], F32))
        rows_dram = nc.dram_tensor("sorted_rows", (SORTED_TILES * P, D), F32).ap()
        sorted_y_dram = nc.dram_tensor("sorted_y", (SORTED_TILES * P, D), F32).ap()
        rows_cleared = nc.alloc_semaphore("rows_cleared")
        slots_cleared = nc.alloc_semaphore("slots_cleared")
        zeros_ready = nc.alloc_semaphore("zeros_ready")
        loaded = nc.alloc_semaphore("loaded")
        stored = nc.alloc_semaphore("stored")

        def load(sp):
            sp.dma_start(x[:, :, :], t["x"].rearrange("b p d -> p b d")).then_inc(loaded, 16)
            sp.dma_start(ident[:, :], t["identity"]).then_inc(loaded, 16)
            sp.dma_start(until[:, :], t["until"]).then_inc(loaded, 16)
            sp.dma_start(slot_base[:, :], t["slot_base"]).then_inc(loaded, 16)
            sp.dma_start(spill[:, :], t["spill"]).then_inc(loaded, 16)
            sp.dma_start(steps[:, :], t["steps"]).then_inc(loaded, 16)
            sp.wait_ge(zeros_ready, 1)
            for rows, cleared in ((rows_dram, rows_cleared), (slots_dram[0:32 * CAPACITY, :], slots_cleared)):
                sp.dma_start(rows.rearrange("(t p) d -> p t d", p=P),
                             zeros[:, None, :].to_broadcast([P, rows.shape[0] // P, D])).then_inc(cleared, 16)
            sp.wait_ge(loaded, 6 * 16)

        with nc.Block() as block:
            @block.sync
            def _(sp):
                load(sp)

            @block.gpsimd
            def _(pool):
                nc.gpsimd.memset(ones[:, :], 1.0)
                nc.gpsimd.memset(zeros[:, :], 0.0).then_inc(zeros_ready, 1)

        def routed(tag, columns, route, *arguments):
            with nc.sbuf_tensor(f"{tag}_rw", [P, B, columns], F32) as rw:
                route(rw)
                experts(nc, tag, x, xnT, rw, *arguments)

        if 0 in stages:
            layer_norm(nc, "n0", x, xn, xnT, ident)
            attention(nc, "a0", x, xnT, t["ctxT"], ident, t["L0_xattn_Wq"], t["L0_xattn_Wk"], t["L0_xattn_Wv"],
                      16, 64, 64, 64 ** -0.5, wo_dram=t["L0_xattn_Wo"], bo_dram=t["L0_xattn_bo"])
        recycle_signals(nc)
        if 1 in stages:
            layer_norm(nc, "n1", x, xn, xnT, ident)
            routed("f0", 10, lambda rw: routing(nc, "r0", xnT, rw, t["L0_wr"], 8, finish_top2_softmax,
                                                t["L0_ffn_expert_bias"]), t["L0_experts"], ACT.Silu, True)
        recycle_signals(nc)
        if 2 in stages:
            layer_norm(nc, "n2", x, xn, xnT, ident)
            attention(nc, "a1", x, xnT, t["ctxT"], ident, t["L1_xattn_Wq"], t["L1_xattn_Wk"], t["L1_xattn_Wv"],
                      1, 256, 256, 1.0, bq_dram=t["L1_xattn_bq"], bk_dram=t["L1_xattn_bk"], bv_dram=t["L1_xattn_bv"])
        recycle_signals(nc)
        if 3 in stages:
            layer_norm(nc, "n3", x, xn, xnT, ident)
            routed("f1", 34, lambda rw: routing(nc, "r1", xnT, rw, t["L1_wr"], 32, finish_grouped_top8,
                                                t["L1_ffn_gate_bias"]), t["L1_experts"], ACT.Silu, True)
        recycle_signals(nc)
        if 4 in stages:
            layer_norm(nc, "n4", x, xn, xnT, ident)
            routed("e2", 16, lambda rw: ensemble_gate(nc, "g2", rw, t["ctx"], t["itok"], ones, 8, 2),
                   t["L2_ensemble"], ACT.Relu, False)
        recycle_signals(nc)
        if 5 in stages:
            layer_norm(nc, "n5", x, xn, xnT, ident)
            with (nc.sbuf_tensor("slot", [P, B], I32) as slot,
                  nc.sbuf_tensor("tile_expert", [P, SORTED_TILES], I32) as tile_expert):
                routing(nc, "r2", xnT, None, t["L2_wr"], 8, finish_top1_sorted(until, ones, steps, slot, tile_expert))
                with nc.sbuf_tensor("shared_weight", [P, B, 4], F32) as shared_weight:
                    with nc.Block() as block:
                        @block.gpsimd
                        def _(pool):
                            nc.gpsimd.memset(shared_weight[:, :, :], 1.0)
                    experts(nc, "s2", x, xnT, shared_weight, t["L2_shared"], ACT.Gelu, True)
                sorted_experts(nc, "f2", x, xn, slot, tile_expert, ident, t["L2_experts"], rows_dram, sorted_y_dram,
                               rows_cleared)
        recycle_signals(nc)
        if 6 in stages:
            layer_norm(nc, "n6", x, xn, xnT, ident)
            attention(nc, "a3", x, xnT, t["ctxT"], ident, t["L3_xattn_Wq"], t["L3_xattn_Wk"], t["L3_xattn_Wv"],
                      16, 32, 16, 0.25, wo_dram=t["L3_xattn_Wo"], bq_dram=t["L3_xattn_bq"], bk_dram=t["L3_xattn_bk"],
                      bv_dram=t["L3_xattn_bv"], bo_dram=t["L3_xattn_bo"])
        recycle_signals(nc)
        if 7 in stages:
            layer_norm(nc, "n7", x, xn, xnT, ident)
            with nc.sbuf_tensor("gate_of", [P, B, 1], F32) as gate_of:
                routing(nc, "r3", xnT, gate_of, t["L3_wr"], 32,
                        finish_top1_capacity(until, ones, slot_base, spill, put, get, CAPACITY))
                capacity_experts(nc, "f3", x, xn, gate_of, put, get, ident, t["L3_experts"], slots_dram,
                                 y_dram, slots_cleared, CAPACITY)
        with nc.Block() as block:
            @block.sync
            def _(sp):
                sp.dma_start(out.rearrange("b p d -> p b d"), x[:, :, :]).then_inc(stored, 16)
                sp.wait_ge(stored, 16)


def pack(a, b, c, chunks):
    def rows(m):
        e, _, f = m.shape
        return m.reshape(e, KC, P, f // P, P).transpose(0, 3, 2, 1, 4).reshape(e * (f // P), P, D)
    parts = [rows(a)] + ([rows(b)] if b is not None else []) + [c.reshape(-1, P, D)]
    packed = np.concatenate(parts, axis=2)
    return np.ascontiguousarray(packed.reshape(-1, chunks, P, packed.shape[2]).transpose(0, 2, 1, 3))


def pack_passes(a, b, c, h):
    e, _, f = a.shape
    ab = np.stack([m.reshape(e, KC, P, f // h, h) for m in (a, b)], axis=4)
    ab = ab.transpose(3, 2, 0, 1, 4, 5).reshape(f // h, P, e, KC * 2 * h)
    down = c.reshape(e, f // h, h // P, P, D).transpose(1, 3, 0, 2, 4).reshape(f // h, P, e, h // P * D)
    return np.concatenate([ab, down], axis=3)


def kernel(**inputs):
    import concourse.bacc as bacc
    from concourse.bass_utils import run_bass_kernel_spmd

    a = {name: np.asarray(value) for name, value in inputs.items()}
    f = lambda name: a[name].astype(a[name].dtype)
    sw = lambda m: m.transpose(0, 2, 1)
    arrays = {
        "x": a["x"], "ctx": a["ctx_512"], "itok": a["itok_BxS2xS_0_7"],
        "ctxT": np.ascontiguousarray(sw(a["ctx_512"])),
        "identity": np.eye(P, dtype=np.float32),
        "slot_base": np.tile(np.arange(32, dtype=np.float32) * CAPACITY - 1, (P, 1)),
        "spill": (32 * CAPACITY + np.arange(T, dtype=np.float32)).reshape(B, P).T,
        "until": np.triu(np.ones((P, P), np.float32)),
        "L0_experts": np.concatenate([pack(a["L0_ffn_Wg"], a["L0_ffn_Wu"], a["L0_ffn_Wd"], 1),
                                      pack(a["L0_ffn_Sg"][None], a["L0_ffn_Su"][None], a["L0_ffn_Sd"][None], 1)]),
        "L0_wr": a["L0_ffn_Wr"], "L0_ffn_expert_bias": a["L0_ffn_expert_bias"],
        "L1_experts": np.concatenate([pack(sw(a["L1_ffn_w_gate"]), sw(a["L1_ffn_w_up"]), sw(a["L1_ffn_w_down"]), 1),
                                      pack(a["L1_ffn_sh_gate"].T[None], a["L1_ffn_sh_up"].T[None],
                                           a["L1_ffn_sh_down"].T[None], 1)]),
        "L1_wr": np.ascontiguousarray(a["L1_ffn_gate_w"].T), "L1_ffn_gate_bias": a["L1_ffn_gate_bias"],
        "L2_ensemble": pack(sw(a["L2_xattn_proj_in"]), None, sw(a["L2_xattn_proj_out"]), 2),
        "L2_experts": pack_passes(a["L2_ffn_W1"], a["L2_ffn_W2"], a["L2_ffn_W3"], 256),
        "L2_shared": pack(a["L2_ffn_w1s"][None], a["L2_ffn_w2s"][None], a["L2_ffn_w3s"][None], 2),
        "steps": np.tile(np.arange(SORTED_TILES, dtype=np.float32), (P, 1)),
        "L2_wr": a["L2_ffn_Wg"],
        "L3_experts": pack(a["L3_ffn_w_gate"], a["L3_ffn_w_up"], a["L3_ffn_w_down"], 2),
        "L3_wr": a["L3_ffn_w_router"],
    }
    for name in a:
        if "_xattn_" in name and "proj" not in name:
            m = a[name]
            if name in ("L3_xattn_Wq", "L3_xattn_Wk"):
                m = np.concatenate([m.reshape(-1, 16, 16), np.zeros((m.shape[0], 16, 16), m.dtype)], 2).reshape(-1, 512)
            if name in ("L3_xattn_bq", "L3_xattn_bk"):
                m = np.concatenate([m.reshape(16, 16), np.zeros((16, 16), m.dtype)], 1).reshape(512)
            if name in ("L1_xattn_bq", "L1_xattn_bk", "L3_xattn_bq", "L3_xattn_bk"):
                m = m.reshape(-1, P).T
            arrays[name] = m
    arrays = {name: np.ascontiguousarray(value) for name, value in arrays.items()}
    nc = bacc.Bacc("TRN2", target_bir_lowering=False, num_devices=1)
    tensors = {name: nc.dram_tensor(name + "_dram", value.shape, mybir.dt.from_np(value.dtype),
                                    kind="ExternalInput").ap() for name, value in arrays.items()}
    out = nc.dram_tensor("out_dram", (B, P, D), F32, kind="ExternalOutput").ap()
    build(nc, tensors, out)
    result = run_bass_kernel_spmd(nc, [{name + "_dram": value for name, value in arrays.items()}], core_ids=[0])
    return result.results[0]["out_dram"]
```

```python
from contextlib import ExitStack, contextmanager

import numpy as np
import concourse.bass as bass
from concourse import mybir

F32 = mybir.dt.float32
F32R = mybir.dt.float32r
I32 = mybir.dt.int32
ACT = mybir.ActivationFunctionType
ALU = mybir.AluOpType
AX = mybir.AxisListType

P = 128
B = 16
D = 256
KC = D // P
T = B * P
GT = 4
GW = GT * P
NG = B // GT
EPS = 1e-5
BIG = 3.0e38
CAPACITY = -(-5 * T // (4 * 32))
SORTED_TILES = 24


LIVE = []


def signal(nc, name):
    LIVE.append(nc.alloc_semaphore(name))
    return LIVE[-1]


def recycle_signals(nc):
    nc.clear_and_free_semaphores(LIVE)
    LIVE.clear()
    nc.all_engine_barrier()


def round_to(engine, high, value, ones):
    return engine.tensor_tensor(high, value, ones, ALU.mult)


def low_part(engine, low, value, high):
    return engine.tensor_tensor(low, value, high.bitcast(F32), ALU.subtract)


@contextmanager
def parts_of(nc, name, shape):
    with nc.sbuf_tensor(f"{name}_high", shape, F32R) as high, nc.sbuf_tensor(f"{name}_low", shape, F32R) as low:
        yield high, low


def product(nc, out, lhsT, rhs, start, stop, **options):
    (lhs_high, lhs_low), (rhs_high, rhs_low) = lhsT, rhs
    nc.tensor.matmul(out, lhs_high, rhs_high, start=start, stop=False, **options)
    nc.tensor.matmul(out, lhs_high, rhs_low, start=False, stop=False, **options)
    return nc.tensor.matmul(out, lhs_low, rhs_high, start=False, stop=stop, **options)


XT_PARTS = NG * KC


def layer_norm(nc, ctx, tag, x, xn, xT, turned, ident):
    x_high, x_low = xT
    stats = ctx.enter_context(nc.sbuf_tensor(f"{tag}_stats", [P, B, 6], F32))
    mean_var = ctx.enter_context(nc.sbuf_tensor(f"{tag}_mean_var", [P, B, 2], F32))
    spread = ctx.enter_context(nc.sbuf_tensor(f"{tag}_spread", [P, 3, B], F32))
    stats_done, var_ready, eps_added, std_ready, rstd_ready, xn_ready, turned_ready, high_ready, low_ready = (
        signal(nc, f"{tag}_{n}") for n in ("stats_done", "var_ready", "eps_added", "std_ready", "rstd_ready",
                                           "xn_ready", "turned_ready", "high_ready", "low_ready"))
    variance, std, rstd = (spread[:, i, :] for i in range(3))

    def vector(dve):
        def statistics(g):
            tiles = slice(g * GT, (g + 1) * GT)
            for t in range(g * GT, (g + 1) * GT):
                nc.vector.bn_stats(stats[:, t, :], x[:, t, :]).then_inc(stats_done, 1)
            for t in range(g * GT, (g + 1) * GT):
                dve.wait_ge(stats_done, t + 1)
                nc.vector.bn_aggr(mean_var[:, t, :], stats[:, t, :]).then_inc(var_ready, 1)
            dve.wait_ge(var_ready, (g + 1) * GT)
            nc.vector.tensor_scalar(variance[:, tiles], mean_var[:, tiles, 1], EPS, None,
                                    ALU.add).then_inc(eps_added, 1)

        def inverse_spread(g):
            tiles = slice(g * GT, (g + 1) * GT)
            dve.wait_ge(std_ready, g + 1)
            nc.vector.reciprocal(rstd[:, tiles], std[:, tiles]).then_inc(rstd_ready, 1)
            dve.wait_ge(rstd_ready, g + 1)
            for t in range(g * GT, (g + 1) * GT):
                nc.vector.tensor_scalar(xn[:, t, :], x[:, t, :], mean_var[:, t, 0:1], rstd[:, t:t + 1],
                                        ALU.subtract, ALU.mult).then_inc(xn_ready, 1)

        def low(g):
            for n in range(g * KC, (g + 1) * KC):
                dve.wait_ge(high_ready, n + 1)
                low_part(nc.vector, x_low[:, n % KC, g * GW:(g + 1) * GW], turned[:, n % 4, :],
                         x_high[:, n % KC, g * GW:(g + 1) * GW]).then_inc(low_ready, 1)

        statistics(0)
        for g in range(NG):
            if g + 1 < NG:
                statistics(g + 1)
            inverse_spread(g)
            if g > 0:
                low(g - 1)
        low(NG - 1)

    behind_group = []

    def tensor(pe):
        for g in range(NG):
            for k in range(KC):
                n = g * KC + k
                if n >= 4:
                    pe.wait_ge(low_ready, n - 3)
                for j in range(GT):
                    t = g * GT + j
                    pe.wait_ge(xn_ready, t + 1)
                    last = nc.tensor.transpose(turned[:, n % 4, j * P:(j + 1) * P],
                                               xn[:, t, k * P:(k + 1) * P], ident[:, :])
                last.then_inc(turned_ready, 1)
            for program in behind_group if g > 0 else ():
                program(pe, g - 1)
        for program in behind_group:
            program(pe, NG - 1)

    def scalar(act):
        def high(g):
            for n in range(g * KC, (g + 1) * KC):
                act.wait_ge(turned_ready, n + 1)
                nc.scalar.activation(x_high[:, n % KC, g * GW:(g + 1) * GW], turned[:, n % 4, :],
                                     ACT.Copy).then_inc(high_ready, 1)

        for g in range(NG):
            tiles = slice(g * GT, (g + 1) * GT)
            act.wait_ge(eps_added, g + 1)
            nc.scalar.activation(std[:, tiles], variance[:, tiles], ACT.Sqrt).then_inc(std_ready, 1)
            if g > 0:
                high(g - 1)
        high(NG - 1)

    return {"vector": vector, "tensor": tensor, "scalar": scalar, "behind_group": behind_group}, xn_ready, low_ready


def routing(nc, ctx, tag, norm, xT, xT_ready, rw, banks, wr, finish, bias_dram=None):
    E = wr[0].shape[2]
    bias = ctx.enter_context(nc.sbuf_tensor(f"{tag}_bias", [P, E], F32))
    logits, running, count = (bank[:, 0:B * E].rearrange("p (b e) -> p b e", e=E) for bank in banks)
    bias_loaded = signal(nc, f"{tag}_bias_loaded")
    logits_ready = signal(nc, f"{tag}_logits_ready")
    programs = finish(nc, ctx, tag, logits, running, count, bias, rw, logits_ready, bias_loaded)

    def sync(sp):
        if bias_dram is not None:
            sp.dma_start(bias[:, :], bias_dram[None, :].to_broadcast([P, E])).then_inc(bias_loaded, 16)

    def logits_of(pe, g):
        pe.wait_ge(xT_ready, (g + 1) * KC)
        for t in range(g * GT, (g + 1) * GT):
            for k in range(KC):
                last = product(nc, logits[:, t, :], [m[:, k, t * P:(t + 1) * P] for m in xT],
                               [m[:, k, :] for m in wr], k == 0, k == KC - 1)
        if g == NG - 1:
            last.then_inc(logits_ready, 1)

    norm["behind_group"].append(logits_of)

    return {**programs, "sync": sync}


def run(programs, part, engine):
    for program in programs:
        if part in program:
            program[part](engine)


def choose_top(nc, step, count, values, width, top, left, mask):
    full = width + 8 - count
    for t in range(B):
        last = nc.vector.max(top[:, t, :], values[:, t, 0:full])
    step(last, B)
    for t in range(B):
        last = nc.vector.match_replace(left[:, t, 0:full], top[:, t, :], values[:, t, 0:full], -BIG)
    step(last, B)
    step(nc.vector.tensor_tensor(mask, left[:, :, 0:width], values[:, :, 0:width], ALU.is_lt))


def small_tensors(nc, ctx, tag, **shapes):
    return [ctx.enter_context(nc.sbuf_tensor(f"{tag}_{name}", shape, F32)) for name, shape in shapes.items()]


def stepper(dve, sem):
    done = [0]

    def step(ins, _=None):
        done[0] += 1
        ins.then_inc(sem, 1)
        dve.wait_ge(sem, done[0])
    return step


def finish_top2_softmax(nc, ctx, tag, logits, running, count, bias, rw, logits_ready, bias_loaded):
    E = logits.shape[2]
    values, top, left, mask, ex, total = small_tensors(
        nc, ctx, tag, values=[P, B, E + 6], top=[P, B, 8], left=[P, B, E + 6], mask=[P, B, E],
        ex=[P, B, E], total=[P, B, 2])
    chain = signal(nc, f"{tag}_chain")
    shifted = signal(nc, f"{tag}_shifted")
    exp_ready = signal(nc, f"{tag}_exp_ready")

    def vector(dve):
        step = stepper(dve, chain)
        step(nc.vector.memset(values[:, :, E:E + 6], BIG))
        step(nc.vector.memset(rw[:, :, E:], 1.0))
        dve.wait_ge(bias_loaded, 16)
        dve.wait_ge(logits_ready, 1)
        step(nc.vector.tensor_tensor(values[:, :, 0:E], logits[:, :, :],
                                     bias[:, None, :].to_broadcast([P, B, E]), ALU.add))
        choose_top(nc, step, 2, values, E, top, left, mask[:, :, :])
        nc.vector.tensor_tensor(ex[:, :, :], values[:, :, 0:E], top[:, :, 6:7].to_broadcast([P, B, E]),
                                ALU.subtract).then_inc(shifted, 1)
        dve.wait_ge(exp_ready, 1)
        step(nc.vector.tensor_tensor(mask[:, :, :], mask[:, :, :], values[:, :, 0:E], ALU.mult))
        step(nc.vector.reduce_sum(total[:, :, 0], mask[:, :, :], AX.X))
        step(nc.vector.reciprocal(total[:, :, 1], total[:, :, 0]))
        step(nc.vector.tensor_tensor(rw[:, :, 0:E], mask[:, :, :], total[:, :, 1:2].to_broadcast([P, B, E]),
                                     ALU.mult))

    def scalar(act):
        act.wait_ge(shifted, 1)
        nc.scalar.activation(values[:, :, 0:E], ex[:, :, :], ACT.Exp).then_inc(exp_ready, 1)

    return {"vector": vector, "scalar": scalar, "logits_read": (chain, 3)}


def finish_grouped_top8(nc, ctx, tag, logits, running, count, bias, rw, logits_ready, bias_loaded):
    E, GROUPS, KEPT, SCALE = logits.shape[2], 8, 4, 2.5
    M = E // GROUPS
    scores, biased, best, pair, chosen, top, left, mask, total = small_tensors(
        nc, ctx, tag, scores=[P, B, E], biased=[P, B, E], best=[P, B, GROUPS + 8 - KEPT],
        pair=[P, B, GROUPS], chosen=[P, B, GROUPS], top=[P, B, 8], left=[P, B, E], mask=[P, B, E], total=[P, B, 2])
    chain = signal(nc, f"{tag}_chain")
    scores_ready = signal(nc, f"{tag}_scores_ready")

    def vector(dve):
        step = stepper(dve, chain)
        step(nc.vector.memset(best[:, :, GROUPS:], BIG))
        step(nc.vector.memset(rw[:, :, E:], 1.0))
        dve.wait_ge(bias_loaded, 16)
        dve.wait_ge(scores_ready, 1)
        step(nc.vector.tensor_tensor(biased[:, :, :], scores[:, :, :],
                                     bias[:, None, :].to_broadcast([P, B, E]), ALU.add))
        member = biased[:, :, :].rearrange("p b (g m) -> p b g m", m=M)
        pairs = [(i, j) for i in range(M) for j in range(i + 1, M)]
        for n, (i, j) in enumerate(pairs):
            out = best[:, :, 0:GROUPS] if n == 0 else pair[:, :, :]
            step(nc.vector.tensor_tensor(out, member[:, :, :, i], member[:, :, :, j], ALU.add))
            if n:
                step(nc.vector.tensor_tensor(best[:, :, 0:GROUPS], best[:, :, 0:GROUPS], pair[:, :, :], ALU.max))
        choose_top(nc, step, KEPT, best, GROUPS, top, left, chosen[:, :, :])
        for m in range(M):
            last = nc.vector.tensor_tensor(member[:, :, :, m], member[:, :, :, m], chosen[:, :, :], ALU.mult)
        step(last)
        choose_top(nc, step, 8, biased, E, top, left, mask[:, :, :])
        step(nc.vector.tensor_tensor(mask[:, :, :], mask[:, :, :], scores[:, :, :], ALU.mult))
        step(nc.vector.reduce_sum(total[:, :, 0], mask[:, :, :], AX.X))
        step(nc.vector.tensor_scalar(total[:, :, 0], total[:, :, 0], 1e-20, None, ALU.add))
        step(nc.vector.reciprocal(total[:, :, 1], total[:, :, 0]))
        step(nc.vector.tensor_tensor(mask[:, :, :], mask[:, :, :], total[:, :, 1:2].to_broadcast([P, B, E]), ALU.mult))
        step(nc.vector.tensor_scalar(rw[:, :, 0:E], mask[:, :, :], SCALE, None, ALU.mult))

    def scalar(act):
        act.wait_ge(logits_ready, 1)
        nc.scalar.activation(scores[:, :, :], logits[:, :, :], ACT.Sigmoid).then_inc(scores_ready, 1)

    return {"vector": vector, "scalar": scalar, "logits_read": (scores_ready, 1)}


def finish_top1_sorted(until, ones, steps, slot, tile_expert, slots_known):
    def finish(nc, ctx, tag, logits, running, count, bias, rw, logits_ready, bias_loaded):
        E = logits.shape[2]
        values, top, left, mask, before, above, reached, tiles, ends, place = small_tensors(
            nc, ctx, tag, values=[P, B, E + 7], top=[P, B, 8], left=[P, B, E + 7], mask=[P, B, E],
            before=[P, B + 1, E], above=[P, E, B], reached=[P, SORTED_TILES, E], tiles=[P, E], ends=[P, E],
            place=[P, SORTED_TILES])
        chain = signal(nc, f"{tag}_chain")
        values_ready = signal(nc, f"{tag}_values_ready")
        mask_ready = signal(nc, f"{tag}_mask_ready")
        counted = signal(nc, f"{tag}_counted")

        def vector(dve):
            step = stepper(dve, chain)
            step(nc.vector.memset(values[:, :, E:], BIG))
            step(nc.vector.memset(before[:, 0, :], 0.0))
            step(nc.vector.memset(rw[:, :, 0:4], 1.0))
            dve.wait_ge(values_ready, 1)
            choose_top(nc, step, 1, values, E, top, left, mask[:, :, :])
            nc.vector.tensor_copy(ends[:, :], mask[:, 0, :]).then_inc(mask_ready, 1)
            dve.wait_ge(mask_ready, 1)
            dve.wait_ge(counted, 1)
            for t in range(1, B + 1):
                step(nc.vector.tensor_tensor(before[:, t, :], before[:, t - 1, :], count[:, t - 1, :], ALU.add))
            step(nc.vector.tensor_scalar(above[:, :, :], steps[:, None, 0:B].to_broadcast([P, E, B]), float(P), None,
                                         ALU.mult))
            step(nc.vector.tensor_tensor(above[:, :, :], before[:, B, :, None].to_broadcast([P, E, B]),
                                         above[:, :, :], ALU.is_gt))
            step(nc.vector.reduce_sum(tiles[:, :], above[:, :, :], AX.X))
            step(nc.vector.tensor_copy(ends[:, :], tiles[:, :]))
            for e in range(1, E):
                step(nc.vector.tensor_tensor(ends[:, e:e + 1], ends[:, e - 1:e], tiles[:, e:e + 1], ALU.add))
            step(nc.vector.tensor_tensor(reached[:, :, :], steps[:, :, None].to_broadcast([P, SORTED_TILES, E]),
                                         ends[:, None, :].to_broadcast([P, SORTED_TILES, E]), ALU.is_ge))
            step(nc.vector.reduce_sum(place[:, :], reached[:, :, :], AX.X))
            step(nc.vector.tensor_scalar(place[:, :], place[:, :], float(E - 1), None, ALU.min))
            step(nc.vector.tensor_copy(tile_expert[:, :], place[:, :]))
            step(nc.vector.tensor_tensor(ends[:, :], ends[:, :], tiles[:, :], ALU.subtract))
            step(nc.vector.tensor_scalar(ends[:, :], ends[:, :], float(P), -1.0, ALU.mult, ALU.add))
            step(nc.vector.tensor_tensor(before[:, 0:B, :], before[:, 0:B, :], running[:, :, :], ALU.add))
            step(nc.vector.tensor_tensor(before[:, 0:B, :], before[:, 0:B, :],
                                         ends[:, None, :].to_broadcast([P, B, E]), ALU.add))
            step(nc.vector.tensor_tensor(before[:, 0:B, :], before[:, 0:B, :], mask[:, :, :], ALU.mult))
            step(nc.vector.reduce_sum(place[:, 0:B], before[:, 0:B, :], AX.X))
            step(nc.vector.tensor_copy(slot[:, :], place[:, 0:B]))
            dve.sem_inc(slots_known, 1)

        def scalar(act):
            act.wait_ge(logits_ready, 1)
            nc.scalar.activation(values[:, :, 0:E], logits[:, :, :], ACT.Copy).then_inc(values_ready, 1)

        def tensor_late(pe):
            pe.wait_ge(mask_ready, 1)
            flat = mask[:, :, :].rearrange("p b e -> p (b e)")
            nc.tensor.matmul(running.rearrange("p b e -> p (b e)"), until[:, :], flat, start=True, stop=True)
            nc.tensor.matmul(count.rearrange("p b e -> p (b e)"), ones[:, :], flat,
                             start=True, stop=True).then_inc(counted, 1)

        return {"vector": vector, "scalar": scalar, "logits_read": (values_ready, 1), "tensor_late": tensor_late}
    return finish


def finish_top1_capacity(until, ones, slot_base, spill, put, get, slots_known, capacity):
    def finish(nc, ctx, tag, logits, running, count, bias, rw, logits_ready, bias_loaded):
        E = logits.shape[2]
        values, ex, top, left, mask, total, before, peak, place = small_tensors(
            nc, ctx, tag, values=[P, B, E + 7], ex=[P, B, E], top=[P, B, 8], left=[P, B, E + 7],
            mask=[P, B, E], total=[P, B, 2], before=[P, B, E], peak=[P, B, 1], place=[P, 3, B])
        chain = signal(nc, f"{tag}_chain")
        shifted = signal(nc, f"{tag}_shifted")
        exp_ready = signal(nc, f"{tag}_exp_ready")
        mask_ready = signal(nc, f"{tag}_mask_ready")
        counted = signal(nc, f"{tag}_counted")

        def vector(dve):
            step = stepper(dve, chain)
            step(nc.vector.memset(values[:, :, E:], BIG))
            step(nc.vector.memset(before[:, 0, :], 0.0))
            dve.wait_ge(logits_ready, 1)
            step(nc.vector.reduce_max(peak[:, :, 0], logits[:, :, :], AX.X))
            nc.vector.tensor_tensor(ex[:, :, :], logits[:, :, :], peak[:, :, :].to_broadcast([P, B, E]),
                                    ALU.subtract).then_inc(shifted, 1)
            dve.wait_ge(exp_ready, 1)
            step(nc.vector.reduce_sum(total[:, :, 0], values[:, :, 0:E], AX.X))
            step(nc.vector.reciprocal(total[:, :, 1], total[:, :, 0]))
            step(nc.vector.tensor_tensor(values[:, :, 0:E], values[:, :, 0:E],
                                         total[:, :, 1:2].to_broadcast([P, B, E]), ALU.mult))
            choose_top(nc, step, 1, values, E, top, left, mask[:, :, :])
            nc.vector.tensor_tensor(ex[:, :, :], values[:, :, 0:E], mask[:, :, :], ALU.mult).then_inc(mask_ready, 1)
            dve.wait_ge(counted, 1)
            for t in range(1, B):
                step(nc.vector.tensor_tensor(before[:, t, :], before[:, t - 1, :], count[:, t - 1, :], ALU.add))
            dve.wait_ge(mask_ready, 1)
            step(nc.vector.reduce_sum(total[:, :, 0], ex[:, :, :], AX.X))
            step(nc.vector.tensor_tensor(before[:, :, :], before[:, :, :], running[:, :, :], ALU.add))
            step(nc.vector.tensor_tensor(before[:, :, :], before[:, :, :], mask[:, :, :], ALU.mult))
            step(nc.vector.reduce_sum(place[:, 0, :], before[:, :, :], AX.X))
            step(nc.vector.tensor_tensor(ex[:, :, :], mask[:, :, :], slot_base[:, None, :].to_broadcast([P, B, E]),
                                         ALU.mult))
            step(nc.vector.reduce_sum(place[:, 1, :], ex[:, :, :], AX.X))
            step(nc.vector.tensor_tensor(place[:, 1, :], place[:, 1, :], place[:, 0, :], ALU.add))
            step(nc.vector.tensor_scalar(place[:, 0, :], place[:, 0, :], float(capacity), None, ALU.is_le))
            step(nc.vector.tensor_tensor(rw[:, :, 0], total[:, :, 0], place[:, 0, :], ALU.mult))
            step(nc.vector.tensor_tensor(place[:, 2, :], place[:, 1, :], spill[:, :], ALU.subtract))
            step(nc.vector.tensor_tensor(place[:, 2, :], place[:, 2, :], place[:, 0, :], ALU.mult))
            step(nc.vector.tensor_tensor(place[:, 2, :], place[:, 2, :], spill[:, :], ALU.add))
            step(nc.vector.tensor_copy(put[:, :], place[:, 2, :]))
            step(nc.vector.tensor_scalar(place[:, 1, :], place[:, 1, :], float(E * capacity - 1), None, ALU.min))
            step(nc.vector.tensor_copy(get[:, :], place[:, 1, :]))
            dve.sem_inc(slots_known, 1)

        def scalar(act):
            act.wait_ge(shifted, 1)
            nc.scalar.activation(values[:, :, 0:E], ex[:, :, :], ACT.Exp).then_inc(exp_ready, 1)

        def tensor_late(pe):
            pe.wait_ge(mask_ready, 1)
            flat = mask[:, :, :].rearrange("p b e -> p (b e)")
            nc.tensor.matmul(running.rearrange("p b e -> p (b e)"), until[:, :], flat, start=True, stop=True)
            nc.tensor.matmul(count.rearrange("p b e -> p (b e)"), ones[:, :], flat,
                             start=True, stop=True).then_inc(counted, 1)

        return {"vector": vector, "scalar": scalar, "tensor_late": tensor_late}
    return finish


def ensemble_gate(nc, ctx, tag, rw, ctxT_dram, itokT_dram, steps):
    weight = ctx.enter_context(nc.sbuf_tensor(f"{tag}_weight", [P, B * P], F32))
    index = ctx.enter_context(nc.sbuf_tensor(f"{tag}_index", [P, B * P], I32))
    index_f = ctx.enter_context(nc.sbuf_tensor(f"{tag}_index_f", [P, B * P], F32))
    picked = ctx.enter_context(nc.sbuf_tensor(f"{tag}_picked", [P, B * P], F32))
    weight_loaded = signal(nc, f"{tag}_weight_loaded")
    index_loaded = signal(nc, f"{tag}_index_loaded")
    index_ready = signal(nc, f"{tag}_index_ready")
    gate_done = signal(nc, f"{tag}_gate_done")

    def batch_rows(m):
        return m[:, :].rearrange("s (b k) -> s b k", k=P)

    def sync(sp):
        sp.dma_start(batch_rows(index), itokT_dram.rearrange("b s k -> s b k")).then_inc(index_loaded, 16)
        sp.dma_start(batch_rows(weight), ctxT_dram.rearrange("b s k -> s b k")).then_inc(weight_loaded, 16)

    def gate_step(dve, e, i):
        if not isinstance(e, int) or 3 * e + i > 0:
            dve.wait_ge(gate_done, 3 * e + i)
        if i == 0:
            scalar = steps[:, e:e + 1] if isinstance(e, int) else steps[:, bass.ds(e, 1)]
            ins = nc.vector.scalar_tensor_tensor(picked[:, :], index_f[:, :], scalar, weight[:, :],
                                                 ALU.is_equal, ALU.mult)
        else:
            first, second = (rw[:, :, 2 * e + n] if isinstance(e, int) else
                             rw[:, :, bass.ds(2 * e + n, 1)].rearrange("p b a -> p (b a)") for n in range(2))
            ins = nc.vector.reduce_sum(first, batch_rows(picked), AX.X) if i == 1 else \
                nc.vector.tensor_copy(second, first)
        ins.then_inc(gate_done, 1)

    def vector(dve):
        dve.wait_ge(index_loaded, 16)
        nc.vector.tensor_copy(index_f[:, :], index[:, :]).then_inc(index_ready, 1)
        dve.wait_ge(index_ready, 1)
        dve.wait_ge(weight_loaded, 16)
        for i in range(3):
            gate_step(dve, 0, i)

    return {"sync_second": sync, "vector": vector}, gate_step, gate_done


def experts(nc, tag, x, xT, xT_ready, rw, ones, gate_up_banks, out, before, w_dram, func, gated,
            gate_step=None, gate_done=None):
    E, _, C, WIDTH = w_dram.shape
    AB = (2 if gated else 1) * D
    HALF = NG * C
    STEPS = 2 * HALF
    PAIRS = E // 2
    assert E % 2 == 0 and WIDTH == AB + D
    with ExitStack() as ctx:
        w = ctx.enter_context(nc.sbuf_tensor(f"{tag}_w", [P, 2, C, WIDTH], F32))
        w_parts = [ctx.enter_context(nc.sbuf_tensor(f"{tag}_w_{part}", [P, 2, C, WIDTH], F32R)) for part in ("high", "low")]
        acted = ctx.enter_context(nc.sbuf_tensor(f"{tag}_acted", [P, 2, GW], F32)) if gated else None
        hidden = ctx.enter_context(nc.sbuf_tensor(f"{tag}_hidden", [P, 2, GW], F32))
        h_parts = [ctx.enter_context(nc.sbuf_tensor(f"{tag}_h_{part}", [P, 2, GW], F32R)) for part in ("high", "low")]
        gate, up = gate_up_banks[:, 0:2, :], gate_up_banks[:, 2:4, :]
        w_loaded = [signal(nc, f"{tag}_w_loaded{s}") for s in range(2)]
        w_rounded, w_split = signal(nc, f"{tag}_w_rounded"), signal(nc, f"{tag}_w_split")
        gate_ready, up_ready, acted_ready, hidden_ready, high_ready, low_ready, down_done, combined = (
            signal(nc, f"{tag}_{n}") for n in ("gate_ready", "up_ready", "acted_ready", "hidden_ready", "high_ready",
                                               "low_ready", "down_done", "combined"))

        def step_of(s):
            return s // HALF, s // C % NG, s % C

        def pairs(engine, program):
            with engine.Fori(0, PAIRS - 1) as pair:
                program(pair, False)
            program(PAIRS - 1, True)

        with nc.Block() as block:
            @block.sync
            def _(sp):
                run(before, "sync", sp)
                for s in range(2):
                    sp.dma_start(w[:, s, :, :], w_dram[s, :, :, :]).then_inc(w_loaded[s], 16)
                run(before, "sync_second", sp)
                with sp.Fori(1, PAIRS) as pair:
                    for s in range(2):
                        sp.wait_ge(w_split, 2 * pair - 1 + s)
                        sp.dma_start(w[:, s, :, :],
                                     w_dram[bass.ds(2 * pair + s, 1), :, :, :].rearrange("a p c n -> p (a c) n")
                                     ).then_inc(w_loaded[s], 16)
                run(before, "sync_late", sp)

            @block.gpsimd
            def _(pool):
                run(before, "gpsimd", pool)

                def split(pair, s, free):
                    pool.wait_ge(w_loaded[s], 16 * pair + 16)
                    if free is not None:
                        pool.wait_ge(down_done, free)
                    round_to(nc.gpsimd, w_parts[0][:, s, :, :], w[:, s, :, :],
                             ones[:, 0:1, None].to_broadcast([P, C, WIDTH])).then_inc(w_rounded, 1)
                    pool.wait_ge(w_rounded, 2 * pair + s + 1)
                    low_part(nc.gpsimd, w_parts[1][:, s, :, :], w[:, s, :, :],
                             w_parts[0][:, s, :, :]).then_inc(w_split, 1)
                for s in range(2):
                    split(0, s, None)
                run(before, "gpsimd_late", pool)
                with pool.Fori(1, PAIRS) as pair:
                    for s in range(2):
                        split(pair, s, STEPS * pair - (1 - s) * HALF)

            @block.tensor
            def _(pe):
                def gate_up(pair, s):
                    e, g, c = step_of(s % STEPS)
                    if g == 0 and c == 0:
                        pe.wait_ge(w_split, 2 * (pair + s // STEPS) + e + 1)
                    if s >= 2:
                        pe.wait_ge(hidden_ready, STEPS * pair + s - 1)
                    for part, (bank, ready) in enumerate(((gate, gate_ready), (up, up_ready))[:AB // D]):
                        for k in range(KC):
                            at = part * D + k * P
                            last = product(nc, bank[:, s % 2, :], [m[:, e, c, at:at + P] for m in w_parts],
                                           [m[:, k, g * GW:(g + 1) * GW] for m in xT], k == 0, k == KC - 1)
                        last.then_inc(ready, 1)

                def down(pair, s):
                    e, g, c = step_of(s)
                    pe.wait_ge(low_ready, STEPS * pair + s + 1)
                    if c == 0:
                        pe.wait_ge(combined, NG + 2 * NG * pair + s // C - 1)
                    for j in range(GT):
                        last = product(nc, out[:, g % 2, j, :], [m[:, s % 2, j * P:(j + 1) * P] for m in h_parts],
                                       [m[:, e, c, AB:AB + D] for m in w_parts], c == 0 and j % 2 == 0, c == C - 1,
                                       skip_group_check=True)
                    last.then_inc(down_done, 1)

                def program(pair, last):
                    for s in range(STEPS):
                        if not (last and s >= STEPS - 2):
                            gate_up(pair, s + 2)
                        down(pair, s)

                run(before, "tensor", pe)
                pe.wait_ge(xT_ready, XT_PARTS)
                gate_up(0, 0)
                for made in before:
                    if "logits_read" in made:
                        pe.wait_ge(*made["logits_read"])
                gate_up(0, 1)
                run(before, "tensor_late", pe)
                pairs(pe, program)

            @block.scalar
            def _(act):
                def activate(pair, s):
                    act.wait_ge(gate_ready, STEPS * pair + s + 1)
                    if gated:
                        nc.scalar.activation(acted[:, s % 2, :], gate[:, s % 2, :], func).then_inc(acted_ready, 1)
                    else:
                        if s >= 2:
                            act.wait_ge(low_ready, STEPS * pair + s - 1)
                        nc.scalar.activation(hidden[:, s % 2, :], gate[:, s % 2, :], func).then_inc(hidden_ready, 1)

                def high(pair, s):
                    act.wait_ge(hidden_ready, STEPS * pair + s + 1)
                    nc.scalar.activation(h_parts[0][:, s % 2, :], hidden[:, s % 2, :], ACT.Copy).then_inc(high_ready, 1)

                def program(pair, last):
                    for s in range(STEPS):
                        if not (last and s >= STEPS - 2):
                            activate(pair, s + 2)
                        if not (last and s == STEPS - 1):
                            if last and s == STEPS - 2:
                                act.wait_ge(down_done, STEPS * pair + s)
                            high(pair, s + 1)

                run(before, "scalar", act)
                activate(0, 0)
                activate(0, 1)
                high(0, 0)
                pairs(act, program)

            @block.vector
            def _(dve):
                def multiply(pair, s):
                    if gated:
                        dve.wait_ge(acted_ready, STEPS * pair + s + 1)
                        dve.wait_ge(up_ready, STEPS * pair + s + 1)
                        if s >= 2:
                            dve.wait_ge(low_ready, STEPS * pair + s - 1)
                        nc.vector.tensor_tensor(hidden[:, s % 2, :], acted[:, s % 2, :], up[:, s % 2, :],
                                                ALU.mult).then_inc(hidden_ready, 1)

                def low(pair, s):
                    dve.wait_ge(high_ready, STEPS * pair + s + 1)
                    low_part(nc.vector, h_parts[1][:, s % 2, :], hidden[:, s % 2, :],
                             h_parts[0][:, s % 2, :]).then_inc(low_ready, 1)

                def combine(pair, s):
                    e, g, _ = step_of(s)
                    if gate_step is not None and s == C - 1:
                        dve.wait_ge(gate_done, 3 * pair + 3)
                    dve.wait_ge(down_done, STEPS * pair + s + 1)
                    dve.wait_ge(combined, 2 * NG * pair + s // C + 1)
                    for j in range(GT):
                        t = g * GT + j
                        expert = 2 * pair + e
                        weight = rw[:, t, expert:expert + 1] if isinstance(pair, int) else \
                            rw[:, t, bass.ds(expert, 1)]
                        last = nc.vector.scalar_tensor_tensor(x[:, t, :], out[:, g % 2, j, :], weight, x[:, t, :],
                                                              ALU.mult, ALU.add)
                    last.then_inc(combined, 1)

                def program(pair, last):
                    for s in range(STEPS):
                        if not (last and s >= STEPS - 2):
                            multiply(pair, s + 2)
                        if not (last and s == STEPS - 1):
                            low(pair, s + 1)
                        if s % C == C - 1:
                            combine(pair, s)
                        if gate_step is not None and not last and s % 4 == 2 and s < 12:
                            gate_step(dve, pair + 1, s // 4)

                dve.sem_inc(combined, NG)
                run(before, "vector", dve)
                multiply(0, 0)
                multiply(0, 1)
                low(0, 0)
                pairs(dve, program)


def capacity_experts(nc, tag, x, xn, gate_of, put, get, slots_known, banks, before, ident, w_dram, slots_dram, y_dram,
                     cleared, S):
    E, _, C, WIDTH = w_dram.shape
    ROWS = E * S
    TILES = ROWS // P
    RING = 4
    AB = 2 * D
    ROUNDS = E // RING
    assert ROWS % (GT * P) == 0 and E % RING == 0
    with ExitStack() as ctx:
        w = ctx.enter_context(nc.sbuf_tensor(f"{tag}_w", [P, RING, C, WIDTH], F32))
        rows = ctx.enter_context(nc.sbuf_tensor(f"{tag}_rows", [P, TILES, D], F32))
        rowsT = ctx.enter_context(nc.sbuf_tensor(f"{tag}_rowsT", [P, KC, ROWS], F32))
        acted = ctx.enter_context(nc.sbuf_tensor(f"{tag}_acted", [P, 2, C * S], F32))
        hidden = ctx.enter_context(nc.sbuf_tensor(f"{tag}_hidden", [P, 2, C, S], F32))
        y = ctx.enter_context(nc.sbuf_tensor(f"{tag}_y", [S, RING, D], F32))
        back = ctx.enter_context(nc.sbuf_tensor(f"{tag}_back", [P, B, D], F32))
        gate, up, out, turned = (banks[:, 2 * i:2 * i + 2, :] for i in range(4))
        scattered, rows_loaded = signal(nc, f"{tag}_scattered"), signal(nc, f"{tag}_rows_loaded")
        w_loaded = [signal(nc, f"{tag}_w_loaded{r}") for r in range(RING)]
        turned_ready, rowsT_written = signal(nc, f"{tag}_turned_ready"), signal(nc, f"{tag}_rowsT_written")
        gate_ready, up_ready = signal(nc, f"{tag}_gate_ready"), signal(nc, f"{tag}_up_ready")
        acted_ready, hidden_ready = signal(nc, f"{tag}_acted_ready"), signal(nc, f"{tag}_hidden_ready")
        down_done, y_ready = signal(nc, f"{tag}_down_done"), signal(nc, f"{tag}_y_ready")
        y_stored = [signal(nc, f"{tag}_y_stored{r}") for r in range(RING)]
        gathered, x_summed = signal(nc, f"{tag}_gathered"), signal(nc, f"{tag}_x_summed")

        def rounds(engine, program):
            with engine.Fori(0, ROUNDS - 1) as n:
                program(n, False)
            program(ROUNDS - 1, True)

        with nc.Block() as block:
            @block.gpsimd
            def _(pool):
                run(before, "gpsimd", pool)
                pool.wait_ge(slots_known, 1)
                pool.wait_ge(cleared, 16)
                for t in range(B):
                    nc.gpsimd.indirect_dma_start(
                        out=slots_dram, out_offset=bass.IndirectOffsetOnAxis(ap=put[:, t:t + 1], axis=0),
                        in_=xn[:, t, :], in_offset=None).then_inc(scattered, 16)
                nc.gpsimd.tensor_tensor(x[:, :, :], x[:, :, :], xn[:, :, :], ALU.add).then_inc(x_summed, 1)
                for r in range(RING):
                    pool.wait_ge(y_stored[r], 16 * (ROUNDS + 1))
                for t in range(B):
                    nc.gpsimd.indirect_dma_start(
                        out=back[:, t, :], out_offset=None, in_=y_dram,
                        in_offset=bass.IndirectOffsetOnAxis(ap=get[:, t:t + 1], axis=0)).then_inc(gathered, 16)

            @block.sync
            def _(sp):
                run(before, "sync", sp)
                for r in range(RING):
                    sp.dma_start(w[:, r, :, :], w_dram[r, :, :, :]).then_inc(w_loaded[r], 16)
                sp.wait_ge(scattered, 16 * B)
                sp.dma_start(rows[:, :, :], slots_dram[0:ROWS, :].rearrange("(t p) d -> p t d", p=P)
                             ).then_inc(rows_loaded, 16)
                with sp.Fori(1, ROUNDS) as n:
                    for r in range(RING):
                        sp.wait_ge(down_done, RING * (n - 1) + r + 1)
                        sp.dma_start(w[:, r, :, :],
                                     w_dram[bass.ds(RING * n + r, 1), :, :, :].rearrange("a p c n -> p (a c) n")
                                     ).then_inc(w_loaded[r], 16)

            @block.tensor
            def _(pe):
                run(before, "tensor", pe)
                run(before, "tensor_late", pe)
                pe.wait_ge(rows_loaded, 16)
                for n in range(TILES // GT * KC):
                    g, k = n // KC, n % KC
                    if n >= 2:
                        pe.wait_ge(rowsT_written, n - 1)
                    for j in range(GT):
                        last = nc.tensor.transpose(turned[:, n % 2, j * P:(j + 1) * P],
                                                   rows[:, g * GT + j, k * P:(k + 1) * P], ident[:, :])
                    last.then_inc(turned_ready, 1)
                pe.wait_ge(rowsT_written, TILES // GT * KC)

                def gate_up(n, r):
                    nth = RING * n + r
                    pe.wait_ge(w_loaded[r % RING], 16 * (n + r // RING) + 16)
                    pe.wait_ge(hidden_ready, 2 + nth - 1)
                    for part, (bank, ready) in enumerate(((gate, gate_ready), (up, up_ready))):
                        for c in range(C):
                            for k in range(KC):
                                at = part * D + k * P
                                last = nc.tensor.matmul(bank[:, r % 2, c * S:(c + 1) * S], w[:, r % RING, c, at:at + P],
                                                        rowsT[:, k, bass.ds(nth * S, S)],
                                                        start=(k == 0), stop=(k == KC - 1))
                        last.then_inc(ready, 1)

                def down(n, r):
                    nth = RING * n + r
                    pe.wait_ge(hidden_ready, 2 + nth + 1)
                    pe.wait_ge(y_ready, 2 + nth - 1)
                    for c in range(C):
                        last = nc.tensor.matmul(out[0:S, r % 2, 0:D], hidden[:, r % 2, c, :],
                                                w[:, r, c, AB:AB + D], start=(c == 0), stop=(c == C - 1))
                    last.then_inc(down_done, 1)

                def program(n, last):
                    for r in range(RING):
                        if not (last and r == RING - 1):
                            gate_up(n, r + 1)
                        down(n, r)
                gate_up(0, 0)
                rounds(pe, program)

            @block.scalar
            def _(act):
                run(before, "scalar", act)
                for n in range(TILES // GT * KC):
                    g, k = n // KC, n % KC
                    act.wait_ge(turned_ready, n + 1)
                    nc.scalar.activation(rowsT[:, k, g * GW:(g + 1) * GW], turned[:, n % 2, :],
                                         ACT.Copy).then_inc(rowsT_written, 1)

                def activate(n, r):
                    act.wait_ge(gate_ready, RING * n + r + 1)
                    nc.scalar.activation(acted[:, r % 2, :], gate[:, r % 2, 0:C * S], ACT.Silu).then_inc(acted_ready, 1)

                def store(n, r):
                    act.wait_ge(y_ready, 2 + RING * n + r + 1)
                    act.dma_start(y_dram[bass.ds((RING * n + r) * S, S), :], y[:, r, :]).then_inc(y_stored[r], 16)

                def program(n, last):
                    for r in range(RING):
                        if not (last and r == RING - 1):
                            activate(n, r + 1)
                        store(n, r)
                activate(0, 0)
                rounds(act, program)

            @block.vector
            def _(dve):
                def multiply(n, r):
                    dve.wait_ge(acted_ready, RING * n + r + 1)
                    dve.wait_ge(up_ready, RING * n + r + 1)
                    nc.vector.tensor_tensor(hidden[:, r % 2, :, :].rearrange("p c n -> p (c n)"), acted[:, r % 2, :],
                                            up[:, r % 2, 0:C * S], ALU.mult).then_inc(hidden_ready, 1)

                def copy_out(n, r):
                    dve.wait_ge(down_done, RING * n + r + 1)
                    dve.wait_ge(y_stored[r], 16 * n + 16)
                    nc.vector.tensor_copy(y[:, r, :], out[0:S, r % 2, 0:D]).then_inc(y_ready, 1)

                def program(n, last):
                    for r in range(RING):
                        if not (last and r == RING - 1):
                            multiply(n, r + 1)
                        copy_out(n, r)
                run(before, "vector", dve)
                dve.sem_inc(hidden_ready, 2)
                dve.sem_inc(y_ready, 2)
                for r in range(RING):
                    dve.sem_inc(y_stored[r], 16)
                multiply(0, 0)
                rounds(dve, program)
                dve.wait_ge(x_summed, 1)
                dve.wait_ge(gathered, 16 * B)
                for t in range(B):
                    nc.vector.scalar_tensor_tensor(x[:, t, :], back[:, t, :], gate_of[:, t, 0:1], x[:, t, :],
                                                   ALU.mult, ALU.add)


def scatter_rows(nc, tag, xn, slot, slots_known, rows_dram, cleared, rows, w_first, w_dram):
    scattered, rows_loaded, w_loaded = (signal(nc, f"{tag}_{n}") for n in ("scattered", "rows_loaded", "w_loaded"))

    def gpsimd_late(pool):
        pool.wait_ge(slots_known, 1)
        pool.wait_ge(cleared, 16)
        for t in range(B):
            nc.gpsimd.indirect_dma_start(
                out=rows_dram, out_offset=bass.IndirectOffsetOnAxis(ap=slot[:, t:t + 1], axis=0),
                in_=xn[:, t, :], in_offset=None).then_inc(scattered, 16)

    def sync_late(sp):
        sp.dma_start(w_first[:, :, :], w_dram[0, :, :, :]).then_inc(w_loaded, 16)
        sp.wait_ge(scattered, 16 * B)
        sp.dma_start(rows[:, :, :], rows_dram.rearrange("(t p) d -> p t d", p=P)).then_inc(rows_loaded, 16)

    return {"gpsimd_late": gpsimd_late, "sync_late": sync_late}, rows_loaded, w_loaded


def sorted_experts(nc, tag, x, rows, rows_loaded, w_first, w_first_loaded, slot, tile_expert, ident, w_dram, y_dram):
    PASSES, _, E, WIDTH = w_dram.shape
    H = WIDTH // (2 * KC + KC)
    HC = H // P
    NT = SORTED_TILES
    AB = KC * 2 * H
    assert WIDTH == AB + HC * D and NT % GT == 0 and 2 * H == 512
    with ExitStack() as ctx:
        w = [w_first, ctx.enter_context(nc.sbuf_tensor(f"{tag}_w", [P, E, WIDTH], F32))]
        rowsT = ctx.enter_context(nc.sbuf_tensor(f"{tag}_rowsT", [P, KC, NT * P], F32))
        back = rowsT[:, :, :].rearrange("p k n -> p (k n)")[:, 0:B * D].rearrange("p (b d) -> p b d", d=D)
        acted = ctx.enter_context(nc.sbuf_tensor(f"{tag}_acted", [P, 2, H], F32))
        hidden = ctx.enter_context(nc.sbuf_tensor(f"{tag}_hidden", [P, 2, H], F32))
        hiddenT = ctx.enter_context(nc.sbuf_tensor(f"{tag}_hiddenT", [P, 2, HC, P], F32))
        gate_up = ctx.enter_context(nc.psum_tensor(f"{tag}_gate_up", [P, 2, 512], F32))
        turned = ctx.enter_context(nc.psum_tensor(f"{tag}_turned", [P, 2, 512], F32))
        out = ctx.enter_context(nc.psum_tensor(f"{tag}_out", [P, 2, 512], F32))
        w_loaded = [w_first_loaded, signal(nc, f"{tag}_w_loaded1")]
        rows_turned, rowsT_written = signal(nc, f"{tag}_rows_turned"), signal(nc, f"{tag}_rowsT_written")
        rows_zeroed = signal(nc, f"{tag}_rows_zeroed")
        products_ready, acted_ready = signal(nc, f"{tag}_products_ready"), signal(nc, f"{tag}_acted_ready")
        hidden_ready, turned_ready = signal(nc, f"{tag}_hidden_ready"), signal(nc, f"{tag}_turned_ready")
        hiddenT_ready, down_done = signal(nc, f"{tag}_hiddenT_ready"), signal(nc, f"{tag}_down_done")
        added, y_stored, gathered = signal(nc, f"{tag}_added"), signal(nc, f"{tag}_y_stored"), signal(nc, f"{tag}_gathered")

        with nc.Block() as block:
            @block.gpsimd
            def _(pool):
                pool.wait_ge(y_stored, 16 * NT // GT)
                for t in range(B):
                    nc.gpsimd.indirect_dma_start(
                        out=back[:, t, :], out_offset=None, in_=y_dram,
                        in_offset=bass.IndirectOffsetOnAxis(ap=slot[:, t:t + 1], axis=0)).then_inc(gathered, 16)

            @block.sync
            def _(sp):
                sp.dma_start(w[1][:, :, :], w_dram[1, :, :, :]).then_inc(w_loaded[1], 16)
                for q in range(2, PASSES):
                    sp.wait_ge(down_done, NT * (q - 1))
                    sp.dma_start(w[q % 2][:, :, :], w_dram[q, :, :, :]).then_inc(w_loaded[q % 2], 16)
                y_tiles = y_dram.rearrange("(t p) d -> p t d", p=P)
                for t in range(0, NT, GT):
                    sp.wait_ge(added, NT * PASSES + t + GT)
                    sp.dma_start(y_tiles[:, t:t + GT, :], rows[:, t:t + GT, :]).then_inc(y_stored, 16)
                sp.wait_ge(y_stored, 16 * NT // GT)

            @block.tensor
            def _(pe):
                pe.wait_ge(rows_loaded, 16)
                for n in range(NT // GT * KC):
                    g, k = n // KC, n % KC
                    if n >= 2:
                        pe.wait_ge(rowsT_written, n - 1)
                    for j in range(GT):
                        last = nc.tensor.transpose(gate_up[:, n % 2, j * P:(j + 1) * P],
                                                   rows[:, g * GT + j, k * P:(k + 1) * P], ident[:, :])
                    last.then_inc(rows_turned, 1)
                pe.wait_ge(rowsT_written, NT // GT * KC)

                def one_pass(q, parity):
                    for s in range(NT + 2):
                        nth = NT * (2 * q + parity) + s
                        if s < NT:
                            expert = pe.value_load(tile_expert[0:1, s:s + 1], min_val=0, max_val=E - 1)
                            owner_of[s % 3] = expert
                            if s == 0:
                                pe.wait_ge(w_loaded[parity], 16 * q + 16)
                            pe.wait_ge(hidden_ready, 2 + nth - 1)
                            for k in range(KC):
                                last = nc.tensor.matmul(gate_up[:, s % 2, :], rowsT[:, k, s * P:(s + 1) * P],
                                                        w[parity][:, bass.ds(expert, 1), k * 2 * H:(k + 1) * 2 * H],
                                                        start=(k == 0), stop=(k == KC - 1))
                            last.then_inc(products_ready, 1)
                        if 1 <= s <= NT:
                            pe.wait_ge(hidden_ready, 2 + nth)
                            for c in range(HC):
                                last = nc.tensor.transpose(turned[:, (s - 1) % 2, c * P:(c + 1) * P],
                                                           hidden[:, (s - 1) % 2, c * P:(c + 1) * P], ident[:, :])
                            last.then_inc(turned_ready, 1)
                        if s >= 2:
                            pe.wait_ge(hiddenT_ready, nth - 1)
                            pe.wait_ge(added, NT + nth - 3)
                            for c in range(HC):
                                last = nc.tensor.matmul(out[:, s % 2, 0:D], hiddenT[:, s % 2, c, :],
                                                        w[parity][:, bass.ds(owner_of[(s - 2) % 3], 1),
                                                                  AB + c * D:AB + (c + 1) * D],
                                                        start=(c == 0), stop=(c == HC - 1))
                            last.then_inc(down_done, 1)
                owner_of = [None] * 3
                with pe.Fori(0, PASSES // 2) as q:
                    for parity in range(2):
                        one_pass(q, parity)

            @block.scalar
            def _(act):
                for n in range(NT // GT * KC):
                    g, k = n // KC, n % KC
                    act.wait_ge(rows_turned, n + 1)
                    nc.scalar.activation(rowsT[:, k, g * GW:(g + 1) * GW], gate_up[:, n % 2, :],
                                         ACT.Copy).then_inc(rowsT_written, 1)
                with act.Fori(0, PASSES) as q:
                    for s in range(NT + 1):
                        if s < NT:
                            act.wait_ge(products_ready, NT * q + s + 1)
                            nc.scalar.activation(acted[:, s % 2, :], gate_up[:, s % 2, 0:H],
                                                 ACT.Gelu).then_inc(acted_ready, 1)
                        if s >= 1:
                            act.wait_ge(turned_ready, NT * q + s)
                            nc.scalar.activation(hiddenT[:, (s - 1) % 2, :, :].rearrange("p c n -> p (c n)"),
                                                 turned[:, (s - 1) % 2, 0:H], ACT.Copy).then_inc(hiddenT_ready, 1)

            @block.vector
            def _(dve):
                dve.wait_ge(rowsT_written, NT // GT * KC)
                nc.vector.memset(rows[:, :, :], 0.0).then_inc(rows_zeroed, 1)
                dve.wait_ge(rows_zeroed, 1)
                dve.sem_inc(hidden_ready, 2)
                dve.sem_inc(added, NT)
                with dve.Fori(0, PASSES) as q:
                    for s in range(NT + 2):
                        nth = NT * q + s
                        if s < NT:
                            dve.wait_ge(acted_ready, nth + 1)
                            nc.vector.tensor_tensor(hidden[:, s % 2, :], acted[:, s % 2, :], gate_up[:, s % 2, H:2 * H],
                                                    ALU.mult).then_inc(hidden_ready, 1)
                        if s >= 2:
                            dve.wait_ge(down_done, nth - 1)
                            dve.wait_ge(added, nth - 1)
                            nc.vector.tensor_tensor(rows[:, s - 2, :], rows[:, s - 2, :], out[:, s % 2, 0:D],
                                                    ALU.add).then_inc(added, 1)
                for t in range(B):
                    dve.wait_ge(gathered, 16 * B)
                    nc.vector.tensor_tensor(x[:, t, :], x[:, t, :], back[:, t, :], ALU.add)


def attention(nc, tag, x, xn, xT, ctxT_dram, ident, ones, wq_dram, wk_dram, wv_dram, heads, padded, head_dim, scale,
              wo_dram=None, bq_dram=None, bk_dram=None, bv_dram=None, bo_dram=None, later_loads=None):
    CQ = wq_dram.shape[1] // P
    V = wv_dram.shape[1]
    ROWS = min(padded, P)
    RT = P // ROWS
    HC = padded // ROWS
    GB = min(RT, 2)
    GH = min(heads, GB * 4)
    GROUPS = heads // GH
    QUAD = min(4, heads)
    QUADS = heads // QUAD
    QC = 2
    VW = min(V, 512)
    CO = V // P
    OC = min(CO, 4)
    AHEAD = max(1, 3 * QUADS // 4)
    QK = [(kind, i) for kind in "qk" for i in range(CQ // QC)]
    VS = [("v", i) for i in range(V // VW)]
    SUMS = [("o", i) for i in range(CO // OC)] if wo_dram is not None else []
    LAST = SUMS + ([("y", 0)] if wo_dram is not None else [])
    TURNS = [("p", i) for i in range(QUADS)]
    MIXED = TURNS[:2]
    for i in range(2, max(QUADS, 2)):
        MIXED += SUMS[i - 2:i - 1] + TURNS[i:i + 1]
    MIXED += LAST[len(SUMS):]
    PARTS = [QK + VS, MIXED, VS, MIXED]
    FIRST, USES = len(QK) + 2 * len(VS) + QUADS, sum(len(part) for part in PARTS)
    assert CQ % QC == 0 and USES % 2 == 0 and all(use in MIXED for use in LAST)

    def use_of(pair, b, kind, i):
        is_first, is_last = (isinstance(pair, int) and pair == n for n in (0, B // 2 - 1))
        if kind in "qkv":
            at = (QK + VS).index((kind, i)) + len(VS) * b - FIRST if is_first else \
                -USES + sum(len(part) for part in PARTS[:2 * b]) + PARTS[2 * b].index((kind, i))
        elif kind == "p" and b == 0:
            at = i - QUADS if is_first else -len(MIXED) + MIXED.index((kind, i))
        elif kind == "p" or b == 0:
            at = (0 if is_last else len(PARTS[0])) + MIXED.index((kind, i))
        else:
            at = len(MIXED) + LAST.index((kind, i)) if is_last else USES - len(MIXED) + MIXED.index((kind, i))
        at += FIRST
        return at % 2, USES // 2 * pair + at // 2, USES * pair + at

    def place(n):
        g, r, col = n // GH, n % GB, n % GH // GB
        if RT > GB:
            return g, r, col, (g * GB + r) * ROWS, col, col * RT + g * GB + r
        return g, r, col, r * ROWS, n // RT * HC, n

    def bank_of(b, g, r):
        return ((b * GROUPS + g) * GB + r) % 4

    with ExitStack() as ctx:
        def sb(name, shape):
            return ctx.enter_context(nc.sbuf_tensor(f"{tag}_{name}", shape, F32))

        def sem(name):
            return signal(nc, f"{tag}_{name}")
        def parts(name, shape):
            return [ctx.enter_context(nc.sbuf_tensor(f"{tag}_{name}_{part}", shape, F32R)) for part in ("high", "low")]

        shapes = [(CQ * P, KC, wq_dram), (CQ * P, 1, wk_dram), (V, 1, wv_dram)]
        if wo_dram is not None:
            shapes.append((D, CO, wo_dram))
        raw = sb("raw", [P, 3, max(n * k for n, k, _ in shapes)])
        wq, wk, wv = parts("wq", [P, KC, CQ * P]), parts("wk", [P, 1, CQ * P]), parts("wv", [P, 1, V])
        wo = parts("wo", [P, CO, D]) if wo_dram is not None else None
        split_weights = [wq, wk, wv] + ([wo] if wo is not None else [])
        bq = sb("bq", [P, CQ]) if bq_dram is not None else None
        bk = sb("bk", [P, CQ]) if bk_dram is not None else None
        bv = sb("bv", [P, V]) if bv_dram is not None else None
        bo = sb("bo", [P, D]) if bo_dram is not None else None
        keys = sb("keys", [P, 2, P])
        key_parts = parts("keys", [P, 2 * P])
        q, k, v = sb("q", [P, CQ, 2 * P]), sb("k", [P, CQ, 2 * P]), sb("v", [P, 2, V])
        probs = sb("probs", [P, heads, P])
        probsT = sb("probsT", [P, 2, QUAD, P])
        peak, bias = sb("peak", [P, 2, GROUPS, GB, GH // GB]), sb("bias", [P, 2, GROUPS, GB, GH // GB])
        total, inverse = sb("total", [P, 2, heads]), sb("inverse", [P, heads])
        behind = sb("behind", [P, 2])
        o, oT = sb("o", [P, V]), parts("oT", [P, CO, P])
        work = ctx.enter_context(nc.psum_tensor(f"{tag}_work", [P, 2, 512], F32))
        scores = ctx.enter_context(nc.psum_tensor(f"{tag}_scores", [P, 4, 512], F32))
        o_sum = ctx.enter_context(nc.psum_tensor(f"{tag}_o_sum", [P, 2, 512], F32))
        biases_loaded, keys_loaded = sem("biases_loaded"), sem("keys_loaded")
        work_ready, work_free = sem("work_ready"), [sem("work_free0"), sem("work_free1")]
        qk_ready, v_ready = sem("qk_ready"), sem("v_ready")
        scores_ready, bias_ready, exp_done = sem("scores_ready"), sem("bias_ready"), sem("exp_done")
        o_summed, o_ready, chain, x_ready = sem("o_summed"), sem("o_ready"), sem("chain"), sem("x_ready")
        inverted = sem("inverted")
        raw_loaded = [sem(f"raw_loaded{n}") for n in range(3)]
        qk_rounded, qk_split, vo_rounded, vo_split = sem("qk_rounded"), sem("qk_split"), sem("vo_rounded"), sem("vo_split")
        norm, xn_ready, xT_ready = layer_norm(nc, ctx, f"{tag}_norm", x, xn, xT, scores, ident)
        keys_rounded, keys_split, oT_high = sem("keys_rounded"), sem("keys_split"), sem("oT_high")
        n_biases = sum(m is not None for m in (bq, bk, bv, bo))

        def batches(engine, program):
            with engine.Fori(0, B // 2 - 1) as pair:
                for b in range(2):
                    program(pair, b, 2)
            for b in range(2):
                program(B // 2 - 1, b, 1 - b)

        def next_of(pair, b):
            return (pair, 1) if b == 0 else (pair + 1, 0)

        with nc.Block() as block:
            @block.sync
            def _(sp):
                def load(dst, src):
                    sp.dma_start(dst, src).then_inc(biases_loaded, 16)
                def load_weights(n):
                    width, chunks, w_dram = shapes[n]
                    sp.dma_start(raw[:, n % 3, 0:width * chunks].rearrange("p (c n) -> p c n", n=width),
                                 w_dram.rearrange("(c p) n -> p c n", p=P)).then_inc(raw_loaded[n % 3], 16)

                load_weights(0)
                load_weights(1)
                sp.dma_start(keys[:, :, :], ctxT_dram[0:2, :, :].rearrange("b d m -> d b m")).then_inc(keys_loaded, 16)
                load_weights(2)
                if bq is not None:
                    load(bq[:, :], bq_dram)
                    load(bk[:, :], bk_dram)
                    load(bv[:, :], bv_dram[None, :].to_broadcast([P, V]))
                if bo is not None:
                    load(bo[:, :], bo_dram[None, :].to_broadcast([P, D]))
                if len(shapes) > 3:
                    sp.wait_ge(qk_split, 1)
                    load_weights(3)
                if later_loads is not None:
                    later_loads(sp)
                with sp.Fori(1, B // 2) as pair:
                    sp.wait_ge(keys_split, pair)
                    sp.dma_start(keys[:, :, :], ctxT_dram[bass.ds(2 * pair, 2), :, :].rearrange("b d m -> d b m")
                                 ).then_inc(keys_loaded, 16)

            @block.tensor
            def _(pe):
                def take(pair, b, kind, i):
                    slot, before, _ = use_of(pair, b, kind, i)
                    if not isinstance(before, int) or before > 0:
                        pe.wait_ge(work_free[slot], before)
                    return slot

                def read_out(pair, b, kind, i):
                    slot, before, _ = use_of(pair, b, kind, i)
                    pe.wait_ge(work_free[slot], before + 1)

                def project(pair, b, kind, i):
                    slot = take(pair, b, kind, i)
                    if (kind, i) == ("k", 0):
                        pe.wait_ge(keys_split, pair + 1)
                    if kind in "qk":
                        for j in range(QC):
                            at = (i * QC + j) * P
                            for c in range(KC if kind == "q" else 1):
                                last = product(
                                    nc, work[:, slot, j * 2 * P:(j + 1) * 2 * P],
                                    [m[:, c, at:at + P] for m in (wq if kind == "q" else wk)],
                                    [m[:, c, bass.ts(pair, 2 * P)] for m in xT] if kind == "q" else
                                    [m[:, :] for m in key_parts],
                                    c == 0, c == KC - 1 or kind == "k")
                    else:
                        last = product(nc, work[:, slot, 0:VW], [m[:, b * P:(b + 1) * P] for m in key_parts],
                                       [m[:, 0, i * VW:(i + 1) * VW] for m in wv], True, True)
                    last.then_inc(work_ready, 1)

                def score(pair, b, g):
                    if g == 0:
                        pe.wait_ge(qk_ready, pair + 1)
                    if not isinstance(pair, int) or pair + b > 0:
                        pe.wait_ge(exp_done, heads * (2 * pair + b - 1) + GH * (g + 1))
                    for n in range(g * GH, (g + 1) * GH):
                        _, r, col, row, chunk, _ = place(n)
                        bank = bank_of(b, g, r)
                        for c in range(HC):
                            last = nc.tensor.matmul(scores[:, bank, col * P:(col + 1) * P],
                                                    q[row:row + ROWS, chunk + c, b * P:(b + 1) * P],
                                                    k[row:row + ROWS, chunk + c, b * P:(b + 1) * P],
                                                    start=(c == 0), stop=(c == HC - 1))
                    last.then_inc(scores_ready, 1)

                def turn(pair, b, i):
                    slot = take(pair, b, "p", i)
                    pe.wait_ge(exp_done, heads * (2 * pair + b) + QUAD * (i + 1))
                    for j in range(QUAD):
                        last = nc.tensor.transpose(work[:, slot, j * P:(j + 1) * P], probs[:, i * QUAD + j, :],
                                                   ident[:, :])
                    last.then_inc(work_ready, 1)

                def weigh(pair, b, i):
                    read_out(pair, b, "p", i)
                    if i == 0:
                        pe.wait_ge(o_ready, 2 * pair + b + 1)
                        pe.wait_ge(v_ready, 2 * pair + b + 1)
                    for j in range(QUAD):
                        at = place(i * QUAD + j)[-1] * (V // heads)
                        last = nc.tensor.matmul(o_sum[:, at // 512, at % 512:at % 512 + V // heads], probsT[:, i % 2, j, :],
                                                v[:, b, at:at + V // heads], start=True, stop=True)
                    if i == QUADS - 1:
                        last.then_inc(o_summed, 1)

                def turn_sums(pair, b, i):
                    slot = take(pair, b, "o", i)
                    if i == 0:
                        pe.wait_ge(o_ready, 2 * pair + b + 2)
                    for j in range(OC):
                        c = i * OC + j
                        last = nc.tensor.transpose(work[:, slot, j * P:(j + 1) * P], o[:, c * P:(c + 1) * P],
                                                   ident[:, :])
                    last.then_inc(work_ready, 1)

                def project_out(pair, b):
                    slot = take(pair, b, "y", 0)
                    for kind, i in SUMS:
                        if use_of(pair, b, kind, i)[0] != slot:
                            read_out(pair, b, kind, i)
                    for c in range(CO):
                        last = product(nc, work[:, slot, 0:D], [m[:, c, :] for m in oT], [m[:, c, :] for m in wo],
                                       c == 0, c == CO - 1)
                    last.then_inc(work_ready, 1)

                def turns(pair, b, scored, former=None):
                    for kind, i in MIXED if former is not None else TURNS:
                        if kind == "p":
                            turn(pair, b, i)
                            if i == 0 and scored:
                                score(*next_of(pair, b), 0)
                            if i > 0:
                                weigh(pair, b, i - 1)
                            if i == QUADS - 1:
                                for g in range(1, GROUPS) if scored else ():
                                    score(*next_of(pair, b), g)
                                weigh(pair, b, i)
                        else:
                            sums(*former, kind, i)

                def sums(pair, b, kind, i):
                    if kind == "o":
                        turn_sums(pair, b, i)
                    else:
                        project_out(pair, b)

                def program(pair, b, following):
                    if following >= 2:
                        for kind, i in PARTS[2 * b]:
                            project(pair + 1, b, kind, i)
                    if following >= 1:
                        turns(*next_of(pair, b), following >= 2, (pair, b))
                    else:
                        for kind, i in LAST:
                            sums(pair, b, kind, i)

                norm["tensor"](pe)
                pe.wait_ge(qk_split, 2)
                pe.wait_ge(xT_ready, XT_PARTS)
                for kind, i in QK:
                    project(0, 0, kind, i)
                pe.wait_ge(vo_split, len(shapes) - 2)
                for kind, i in VS:
                    project(0, 0, kind, i)
                for kind, i in VS:
                    project(0, 1, kind, i)
                for g in range(GROUPS):
                    score(0, 0, g)
                turns(0, 0, True)
                batches(pe, program)

            @block.gpsimd
            def _(pool):
                def split(pair):
                    pool.wait_ge(keys_loaded, 16 * pair + 16)
                    if not isinstance(pair, int):
                        pool.wait_ge(v_ready, 2 * pair)
                    whole = keys[:, :, :].rearrange("p b m -> p (b m)")
                    round_to(nc.gpsimd, key_parts[0][:, :], whole, ones[:, 0:1].to_broadcast([P, 2 * P])
                             ).then_inc(keys_rounded, 1)
                    pool.wait_ge(keys_rounded, pair + 1)
                    low_part(nc.gpsimd, key_parts[1][:, :], whole, key_parts[0][:, :]).then_inc(keys_split, 1)
                for n, (width, chunks, _) in enumerate(shapes[:2]):
                    high, low = (m[:, :, :].rearrange("p c n -> p (c n)") for m in split_weights[n])
                    pool.wait_ge(raw_loaded[n], 16)
                    round_to(nc.gpsimd, high, raw[:, n, 0:width * chunks],
                             ones[:, 0:1].to_broadcast([P, width * chunks])).then_inc(qk_rounded, 1)
                    pool.wait_ge(qk_rounded, n + 1)
                    low_part(nc.gpsimd, low, raw[:, n, 0:width * chunks], high).then_inc(qk_split, 1)
                split(0)
                if bo is not None:
                    pool.wait_ge(biases_loaded, 16 * n_biases)
                    pool.wait_ge(xn_ready, B)
                    nc.gpsimd.tensor_tensor(x[:, :, :], x[:, :, :], bo[:, None, :].to_broadcast([P, B, D]),
                                            ALU.add).then_inc(x_ready, 1)
                with pool.Fori(1, B // 2) as pair:
                    split(pair)

            @block.scalar
            def _(act):
                def copy_out(pair, b, kind, i, dst, width):
                    slot, _, before = use_of(pair, b, kind, i)
                    act.wait_ge(work_ready, before + 1)
                    nc.scalar.activation(dst, work[:, slot, 0:width], ACT.Copy).then_inc(
                        work_free[slot] if kind == "p" else oT_high, 1)

                def exps(pair, b, i):
                    for n in range(i * QUAD, (i + 1) * QUAD):
                        g, r, col, _, _, h = place(n)
                        if n % GH == 0:
                            act.wait_ge(bias_ready, GROUPS * (2 * pair + b) + g + 1)
                        nc.scalar.activation(probs[:, n, :], scores[:, bank_of(b, g, r), col * P:(col + 1) * P],
                                             ACT.Exp, bias=bias[:, b, g, r, col:col + 1], scale=scale,
                                             accum_out=total[:, b, h:h + 1]).then_inc(exp_done, 1)

                def sums(pair, b, kind, i):
                    if kind == "o":
                        copy_out(pair, b, "o", i, oT[0][:, i * OC:(i + 1) * OC, :].rearrange("p a n -> p (a n)"),
                                 OC * P)

                def turns(pair, b, scored, former=None):
                    for kind, i in MIXED if former is not None else TURNS:
                        if kind == "p":
                            copy_out(pair, b, "p", i, probsT[:, i % 2, :, :].rearrange("p a n -> p (a n)"), QUAD * P)
                            if i < QUADS - AHEAD:
                                exps(pair, b, AHEAD + i)
                        else:
                            sums(*former, kind, i)
                    for i in range(AHEAD) if scored else ():
                        exps(*next_of(pair, b), i)

                def program(pair, b, following):
                    if following >= 1:
                        turns(*next_of(pair, b), following >= 2, (pair, b))
                    else:
                        for kind, i in LAST:
                            sums(pair, b, kind, i)

                norm["scalar"](act)
                for n, (width, chunks, _) in list(enumerate(shapes))[2:]:
                    act.wait_ge(raw_loaded[n % 3], 16 * (n // 3) + 16)
                    nc.scalar.activation(split_weights[n][0][:, :, :].rearrange("p c n -> p (c n)"),
                                         raw[:, n % 3, 0:width * chunks], ACT.Copy).then_inc(vo_rounded, 1)
                for i in range(AHEAD):
                    exps(0, 0, i)
                turns(0, 0, True)
                batches(act, program)

            @block.vector
            def _(dve):
                def largest(pair, b, g):
                    dve.wait_ge(scores_ready, GROUPS * (2 * pair + b) + g + 1)
                    bank = bank_of(b, g, 0)
                    nc.vector.reduce_max(
                        peak[:, b, g, :, :],
                        scores[:, bank:bank + GB, 0:GH // GB * P].rearrange("p r (c n) -> p r c n", n=P),
                        AX.X).then_inc(chain, 1)
                    dve.wait_ge(chain, GROUPS * (2 * pair + b) + g + 1)
                    nc.vector.tensor_scalar(bias[:, b, g, :, :], peak[:, b, g, :, :], -scale, None,
                                            ALU.mult).then_inc(bias_ready, 1)

                def projected(pair, b, kind, i):
                    slot, _, before = use_of(pair, b, kind, i)
                    dve.wait_ge(work_ready, before + 1)
                    if kind == "v":
                        dst, src = v[:, b, i * VW:(i + 1) * VW], work[:, slot, 0:VW]
                        add = bv[:, i * VW:(i + 1) * VW] if bv is not None else None
                    else:
                        dst = (q if kind == "q" else k)[:, i * QC:(i + 1) * QC, :]
                        src = work[:, slot, :].rearrange("p (a n) -> p a n", n=2 * P)
                        rows = bq if kind == "q" else bk
                        add = rows[:, i * QC:(i + 1) * QC, None].to_broadcast([P, QC, 2 * P]) if bq is not None else None
                    if add is not None:
                        last = nc.vector.tensor_tensor(dst, src, add, ALU.add)
                    else:
                        last = nc.vector.tensor_copy(dst, src)
                    last.then_inc(work_free[slot], 1)
                    if (kind, i) in (QK[-1], VS[-1]):
                        column, ready, before = (1, v_ready, 2 * pair + b) if kind == "v" else (0, qk_ready, pair)
                        if not isinstance(pair, int) or before > 0:
                            dve.wait_ge(ready, before)
                        nc.vector.tensor_copy(behind[:, column:column + 1], ones[:, 0:1]).then_inc(ready, 1)

                def tile_of(pair, b):
                    return x[:, 2 * pair + b, :] if isinstance(pair, int) else \
                        x[:, bass.ds(2 * pair + b, 1), :].rearrange("p a d -> p (a d)")

                def normalise(pair, b):
                    dve.wait_ge(o_ready, 2 * pair + b + 1)
                    dve.wait_ge(exp_done, heads * (2 * pair + b + 1))
                    nc.vector.reciprocal(inverse[:, :], total[:, b, :]).then_inc(inverted, 1)
                    dve.wait_ge(inverted, 2 * pair + b + 1)
                    dve.wait_ge(o_summed, 2 * pair + b + 1)
                    if wo is None:
                        nc.vector.scalar_tensor_tensor(tile_of(pair, b), o_sum[:, 0, 0:V], inverse[:, 0:1],
                                                       tile_of(pair, b), ALU.mult, ALU.add).then_inc(o_ready, 1)
                        return
                    banks = max(1, V // 512)
                    sums = o_sum[:, 0:banks, 0:V // banks].rearrange("p a (h n) -> p (a h) n", n=V // heads) \
                        if banks == 1 else o_sum[:, :, :].rearrange("p a (h n) -> p (a h) n", n=V // heads)
                    nc.vector.tensor_tensor(o[:, :].rearrange("p (h n) -> p h n", n=V // heads), sums,
                                            inverse[:, :, None].to_broadcast([P, heads, V // heads]),
                                            ALU.mult).then_inc(o_ready, 1)

                def sums(pair, b, kind, i):
                    slot, _, before = use_of(pair, b, kind, i)
                    if kind == "o":
                        dve.wait_ge(oT_high, len(SUMS) * (2 * pair + b) + i + 1)
                        low_part(nc.vector, oT[1][:, i * OC:(i + 1) * OC, :].rearrange("p a n -> p (a n)"),
                                 work[:, slot, 0:OC * P],
                                 oT[0][:, i * OC:(i + 1) * OC, :].rearrange("p a n -> p (a n)")
                                 ).then_inc(work_free[slot], 1)
                    else:
                        dve.wait_ge(work_ready, before + 1)
                        dve.wait_ge(x_ready, 1)
                        nc.vector.tensor_tensor(tile_of(pair, b), tile_of(pair, b), work[:, slot, 0:D],
                                                ALU.add).then_inc(work_free[slot], 1)

                def turns(pair, b, scored, former=None):
                    if scored:
                        largest(*next_of(pair, b), 0)
                    for kind, i in MIXED if former is not None else TURNS:
                        if kind == "o":
                            sums(*former, kind, i)
                        elif (kind, i) == TURNS[-1]:
                            for g in range(1, GROUPS) if scored else ():
                                largest(*next_of(pair, b), g)
                    normalise(pair, b)
                    if former is not None and wo is not None:
                        sums(*former, "y", 0)

                def program(pair, b, following):
                    if following >= 2:
                        for kind, i in PARTS[2 * b]:
                            projected(pair + 1, b, kind, i)
                    if following >= 1:
                        turns(*next_of(pair, b), following >= 2, (pair, b))
                    else:
                        for kind, i in LAST:
                            sums(pair, b, kind, i)

                dve.sem_inc(o_ready, 1)
                norm["vector"](dve)
                if n_biases:
                    dve.wait_ge(biases_loaded, 16 * n_biases)
                for kind, i in QK:
                    projected(0, 0, kind, i)
                for n, (width, chunks, _) in list(enumerate(shapes))[2:]:
                    dve.wait_ge(vo_rounded, n - 1)
                    low_part(nc.vector, split_weights[n][1][:, :, :].rearrange("p c n -> p (c n)"),
                             raw[:, n % 3, 0:width * chunks],
                             split_weights[n][0][:, :, :].rearrange("p c n -> p (c n)")).then_inc(vo_split, 1)
                for kind, i in VS:
                    projected(0, 0, kind, i)
                for kind, i in VS:
                    projected(0, 1, kind, i)
                for g in range(GROUPS):
                    largest(0, 0, g)
                turns(0, 0, True)
                batches(dve, program)


def build(nc, t, out, stages=range(8)):
    with ExitStack() as ctx:
        x = ctx.enter_context(nc.sbuf_tensor("x", [P, B, D], F32))
        xn = ctx.enter_context(nc.sbuf_tensor("xn", [P, B, D], F32))
        ident = ctx.enter_context(nc.sbuf_tensor("ident", [P, P], F32))
        ones = ctx.enter_context(nc.sbuf_tensor("ones", [P, P], F32))
        until = ctx.enter_context(nc.sbuf_tensor("until", [P, P], F32))
        LIVE.clear()
        zeros = ctx.enter_context(nc.sbuf_tensor("zeros", [P, D], F32))
        slot_base = ctx.enter_context(nc.sbuf_tensor("slot_base", [P, 32], F32))
        spill = ctx.enter_context(nc.sbuf_tensor("spill", [P, B], F32))
        slots_dram = nc.dram_tensor("slots", (32 * CAPACITY + T, D), F32).ap()
        y_dram = nc.dram_tensor("expert_rows", (32 * CAPACITY, D), F32).ap()
        steps = ctx.enter_context(nc.sbuf_tensor("steps", [P, SORTED_TILES], F32))
        rows_dram = nc.dram_tensor("sorted_rows", (SORTED_TILES * P, D), F32).ap()
        sorted_y_dram = nc.dram_tensor("sorted_y", (SORTED_TILES * P, D), F32).ap()
        router = [ctx.enter_context(nc.sbuf_tensor(f"wr{n}", [P, KC, t[f"L{n}_wr"].shape[1]], F32)) for n in range(4)]
        wr_parts = [ctx.enter_context(parts_of(nc, f"wr{n}", list(m.shape))) for n, m in enumerate(router)]
        router_loaded, router_rounded = nc.alloc_semaphore("router_loaded"), nc.alloc_semaphore("router_rounded")
        rows_cleared = nc.alloc_semaphore("rows_cleared")
        slots_cleared = nc.alloc_semaphore("slots_cleared")
        zeros_ready = nc.alloc_semaphore("zeros_ready")
        loaded = nc.alloc_semaphore("loaded")
        stored = nc.alloc_semaphore("stored")

        def load(sp):
            sp.dma_start(x[:, :, :], t["x"].rearrange("b p d -> p b d")).then_inc(loaded, 16)
            sp.dma_start(ident[:, :], t["identity"]).then_inc(loaded, 16)
            sp.dma_start(until[:, :], t["until"]).then_inc(loaded, 16)
            sp.dma_start(slot_base[:, :], t["slot_base"]).then_inc(loaded, 16)
            sp.dma_start(spill[:, :], t["spill"]).then_inc(loaded, 16)
            sp.dma_start(steps[:, :], t["steps"]).then_inc(loaded, 16)
            for n, m in enumerate(router):
                sp.dma_start(m[:, :, :], t[f"L{n}_wr"].rearrange("(k p) e -> p k e", p=P)).then_inc(router_loaded, 16)
            sp.wait_ge(loaded, 6 * 16)

        def clear_rows(sp):
            sp.wait_ge(zeros_ready, 1)
            for rows, cleared in ((rows_dram, rows_cleared), (slots_dram[0:32 * CAPACITY, :], slots_cleared)):
                sp.dma_start(rows.rearrange("(t p) d -> p t d", p=P),
                             zeros[:, None, :].to_broadcast([P, rows.shape[0] // P, D])).then_inc(cleared, 16)

        with nc.Block() as block:
            @block.sync
            def _(sp):
                load(sp)

            @block.gpsimd
            def _(pool):
                nc.gpsimd.memset(ones[:, :], 1.0)
                nc.gpsimd.memset(zeros[:, :], 0.0).then_inc(zeros_ready, 1)
                pool.wait_ge(zeros_ready, 1)
                pool.wait_ge(router_loaded, 16 * len(router))
                for n, (m, (high, low)) in enumerate(zip(router, wr_parts)):
                    round_to(nc.gpsimd, high[:, :, :], m[:, :, :],
                             ones[:, 0:1, None].to_broadcast(list(m.shape))).then_inc(router_rounded, 1)
                    pool.wait_ge(router_rounded, n + 1)
                    low_part(nc.gpsimd, low[:, :, :], m[:, :, :], high[:, :, :])

        for layer in range(4):
            if 2 * layer in stages and layer != 2:
                with parts_of(nc, f"xa{layer}", [P, KC, T]) as xT:
                    if layer == 0:
                        attention(nc, "a0", x, xn, xT, t["ctxT"], ident, ones, t["L0_xattn_Wq"], t["L0_xattn_Wk"],
                                  t["L0_xattn_Wv"], 16, 64, 64, 64 ** -0.5,
                                  wo_dram=t["L0_xattn_Wo"], bo_dram=t["L0_xattn_bo"],
                                  later_loads=clear_rows)
                    elif layer == 1:
                        attention(nc, "a1", x, xn, xT, t["ctxT"], ident, ones, t["L1_xattn_Wq"], t["L1_xattn_Wk"],
                                  t["L1_xattn_Wv"], 1, 256, 256, 1.0, bq_dram=t["L1_xattn_bq"],
                                  bk_dram=t["L1_xattn_bk"], bv_dram=t["L1_xattn_bv"])
                    else:
                        attention(nc, "a3", x, xn, xT, t["ctxT"], ident, ones, t["L3_xattn_Wq"], t["L3_xattn_Wk"],
                                  t["L3_xattn_Wv"], 16, 32, 16, 0.25, wo_dram=t["L3_xattn_Wo"],
                                  bq_dram=t["L3_xattn_bq"], bk_dram=t["L3_xattn_bk"],
                                  bv_dram=t["L3_xattn_bv"], bo_dram=t["L3_xattn_bo"])
                recycle_signals(nc)
            elif 2 * layer in stages:
                with ExitStack() as stage:
                    rw = stage.enter_context(nc.sbuf_tensor("ensemble_rw", [P, B, 16], F32))
                    xT = stage.enter_context(parts_of(nc, "xa2", [P, KC, T]))
                    banks = stage.enter_context(nc.psum_tensor("ensemble_banks", [P, 2, GT, D], F32))
                    gate_up_banks = stage.enter_context(nc.psum_tensor("ensemble_gate_up_banks", [P, 4, GW], F32))
                    four = banks[:, :, :, :].rearrange("p a (b t) d -> p (a b) (t d)", b=2)
                    norm, _, xT_ready = layer_norm(nc, stage, "na2", x, xn, xT, four, ident)
                    gates, gate_step, gate_done = ensemble_gate(nc, stage, "g2", rw, t["ctxT"], t["itokT"], steps)
                    experts(nc, "e2", x, xT, xT_ready, rw, ones, gate_up_banks, banks, [norm, gates], t["L2_ensemble"],
                            ACT.Relu, False, gate_step, gate_done)
                recycle_signals(nc)
            if 2 * layer + 1 not in stages:
                continue
            with ExitStack() as stage:
                rw = stage.enter_context(nc.sbuf_tensor(f"rw{layer}", [P, B, 34], F32))
                if layer < 2:
                    with ExitStack() as inner:
                        xT = inner.enter_context(parts_of(nc, f"xf{layer}", [P, KC, T]))
                        banks = inner.enter_context(nc.psum_tensor(f"banks{layer}", [P, 2, GT, D], F32))
                        gate_up_banks = inner.enter_context(nc.psum_tensor("gate_up_banks" + str(layer), [P, 4, GW], F32))
                        four = banks[:, :, :, :].rearrange("p a (b t) d -> p (a b) (t d)", b=2)
                        norm, _, xT_ready = layer_norm(nc, inner, f"nf{layer}", x, xn, xT, four, ident)
                        route = routing(nc, inner, f"r{layer}", norm, xT, xT_ready, rw[:, :, 0:10] if layer == 0 else rw,
                                        [gate_up_banks[:, 3, :], four[:, 0, :], four[:, 1, :]], wr_parts[layer],
                                        finish_grouped_top8 if layer else finish_top2_softmax,
                                        t["L1_ffn_gate_bias" if layer else "L0_ffn_expert_bias"])
                        experts(nc, f"f{layer}", x, xT, xT_ready, rw, ones, gate_up_banks, banks, [norm, route],
                                t[f"L{layer}_experts"], ACT.Silu, True)
                elif layer == 2:
                    put = stage.enter_context(nc.sbuf_tensor("sorted_slot", [P, B], I32))
                    tile_expert = stage.enter_context(nc.sbuf_tensor("tile_expert", [P, SORTED_TILES], I32))
                    rows = stage.enter_context(nc.sbuf_tensor("rows", [P, SORTED_TILES, D], F32))
                    w_first = stage.enter_context(nc.sbuf_tensor("w_first", list(t["L2_experts"].shape[1:]), F32))
                    slots_known = signal(nc, "sorted_slots_known")
                    with ExitStack() as inner:
                        xT = inner.enter_context(parts_of(nc, "xf2", [P, KC, T]))
                        banks = inner.enter_context(nc.psum_tensor("banks2", [P, 2, GT, D], F32))
                        gate_up_banks = inner.enter_context(nc.psum_tensor("gate_up_banks" + str(layer), [P, 4, GW], F32))
                        four = banks[:, :, :, :].rearrange("p a (b t) d -> p (a b) (t d)", b=2)
                        norm, _, xT_ready = layer_norm(nc, inner, "nf2", x, xn, xT, four, ident)
                        route = routing(nc, inner, "r2", norm, xT, xT_ready, rw,
                                        [gate_up_banks[:, 3, :], four[:, 0, :], four[:, 1, :]],
                                        wr_parts[2], finish_top1_sorted(until, ones, steps, put, tile_expert, slots_known))
                        scatter, rows_loaded, w_first_loaded = scatter_rows(
                            nc, "f2", xn, put, slots_known, rows_dram, rows_cleared, rows, w_first, t["L2_experts"])
                        experts(nc, "s2", x, xT, xT_ready, rw, ones, gate_up_banks, banks, [norm, route, scatter],
                                t["L2_shared"], ACT.Gelu, True)
                    sorted_experts(nc, "f2", x, rows, rows_loaded, w_first, w_first_loaded, put, tile_expert, ident,
                                   t["L2_experts"], sorted_y_dram)
                else:
                    put = stage.enter_context(nc.sbuf_tensor("put", [P, B], I32))
                    get = stage.enter_context(nc.sbuf_tensor("get", [P, B], I32))
                    slots_known = signal(nc, "capacity_slots_known")
                    xT = stage.enter_context(parts_of(nc, "xf3", [P, KC, T]))
                    banks = stage.enter_context(nc.psum_tensor("banks3", [P, 8, GW], F32))
                    norm, _, xT_ready = layer_norm(nc, stage, "nf3", x, xn, xT, banks[:, 0:4, :], ident)
                    route = routing(nc, stage, "r3", norm, xT, xT_ready, rw, [banks[:, i, :] for i in (4, 5, 6)],
                                    wr_parts[3], finish_top1_capacity(until, ones, slot_base, spill, put, get,
                                                                     slots_known, CAPACITY))
                    capacity_experts(nc, "f3", x, xn, rw, put, get, slots_known, banks, [norm, route], ident,
                                     t["L3_experts"], slots_dram, y_dram, slots_cleared, CAPACITY)
            recycle_signals(nc)
        with nc.Block() as block:
            @block.sync
            def _(sp):
                sp.dma_start(out.rearrange("b p d -> p b d"), x[:, :, :]).then_inc(stored, 16)
                sp.wait_ge(stored, 16)


def pack(a, b, c, chunks):
    def rows(m):
        e, _, f = m.shape
        return m.reshape(e, KC, P, f // P, P).transpose(0, 3, 2, 1, 4).reshape(e * (f // P), P, D)
    parts = [rows(a)] + ([rows(b)] if b is not None else []) + [c.reshape(-1, P, D)]
    packed = np.concatenate(parts, axis=2)
    return np.ascontiguousarray(packed.reshape(-1, chunks, P, packed.shape[2]).transpose(0, 2, 1, 3))


def pack_passes(a, b, c, h):
    e, _, f = a.shape
    ab = np.stack([m.reshape(e, KC, P, f // h, h) for m in (a, b)], axis=4)
    ab = ab.transpose(3, 2, 0, 1, 4, 5).reshape(f // h, P, e, KC * 2 * h)
    down = c.reshape(e, f // h, h // P, P, D).transpose(1, 3, 0, 2, 4).reshape(f // h, P, e, h // P * D)
    return np.concatenate([ab, down], axis=3)


def kernel(**inputs):
    import concourse.bacc as bacc
    from concourse.bass_utils import run_bass_kernel_spmd

    a = {name: np.asarray(value) for name, value in inputs.items()}
    sw = lambda m: m.transpose(0, 2, 1)
    arrays = {
        "x": a["x"], "itokT": sw(a["itok_BxS2xS_0_7"]),
        "ctxT": np.ascontiguousarray(sw(a["ctx_512"])),
        "identity": np.eye(P, dtype=np.float32),
        "slot_base": np.tile(np.arange(32, dtype=np.float32) * CAPACITY - 1, (P, 1)),
        "spill": (32 * CAPACITY + np.arange(T, dtype=np.float32)).reshape(B, P).T,
        "until": np.triu(np.ones((P, P), np.float32)),
        "L0_experts": np.concatenate([pack(a["L0_ffn_Wg"], a["L0_ffn_Wu"], a["L0_ffn_Wd"], 1),
                                      pack(a["L0_ffn_Sg"][None], a["L0_ffn_Su"][None], a["L0_ffn_Sd"][None], 1)]),
        "L0_wr": a["L0_ffn_Wr"], "L0_ffn_expert_bias": a["L0_ffn_expert_bias"],
        "L1_experts": np.concatenate([pack(sw(a["L1_ffn_w_gate"]), sw(a["L1_ffn_w_up"]), sw(a["L1_ffn_w_down"]), 1),
                                      pack(a["L1_ffn_sh_gate"].T[None], a["L1_ffn_sh_up"].T[None],
                                           a["L1_ffn_sh_down"].T[None], 1)]),
        "L1_wr": np.ascontiguousarray(a["L1_ffn_gate_w"].T), "L1_ffn_gate_bias": a["L1_ffn_gate_bias"],
        "L2_ensemble": pack(sw(a["L2_xattn_proj_in"]), None, sw(a["L2_xattn_proj_out"]), 2),
        "L2_experts": pack_passes(a["L2_ffn_W1"], a["L2_ffn_W2"], a["L2_ffn_W3"], 256),
        "L2_shared": pack(a["L2_ffn_w1s"][None], a["L2_ffn_w2s"][None], a["L2_ffn_w3s"][None], 2),
        "steps": np.tile(np.arange(SORTED_TILES, dtype=np.float32), (P, 1)),
        "L2_wr": a["L2_ffn_Wg"],
        "L3_experts": pack(a["L3_ffn_w_gate"], a["L3_ffn_w_up"], a["L3_ffn_w_down"], 2),
        "L3_wr": a["L3_ffn_w_router"],
    }
    for name in a:
        if "_xattn_" in name and "proj" not in name:
            m = a[name]
            if name in ("L3_xattn_Wq", "L3_xattn_Wk"):
                m = np.concatenate([m.reshape(-1, 16, 16), np.zeros((m.shape[0], 16, 16), m.dtype)], 2).reshape(-1, 512)
            if name in ("L3_xattn_bq", "L3_xattn_bk"):
                m = np.concatenate([m.reshape(16, 16), np.zeros((16, 16), m.dtype)], 1).reshape(512)
            if name in ("L1_xattn_bq", "L1_xattn_bk", "L3_xattn_bq", "L3_xattn_bk"):
                m = m.reshape(-1, P).T
            arrays[name] = m
    arrays = {name: np.ascontiguousarray(value) for name, value in arrays.items()}
    nc = bacc.Bacc("TRN2", target_bir_lowering=False, num_devices=1)
    tensors = {name: nc.dram_tensor(name + "_dram", value.shape, mybir.dt.from_np(value.dtype),
                                    kind="ExternalInput").ap() for name, value in arrays.items()}
    out = nc.dram_tensor("out_dram", (B, P, D), F32, kind="ExternalOutput").ap()
    build(nc, tensors, out)
    result = run_bass_kernel_spmd(nc, [{name + "_dram": value for name, value in arrays.items()}], core_ids=[0])
    return result.results[0]["out_dram"]
```
